# Optimizing a Trainium2 kernel written in Bass

```python
import numpy as np
import jax
import jax.numpy as jnp

def _softmax(x, axis=-1):
    return jax.nn.softmax(x, axis=axis)

def _gelu(x):
    return jax.nn.gelu(x, approximate=True)

def _silu(x):
    return jax.nn.silu(x)

def _sigmoid(x):
    return jax.nn.sigmoid(x)

def _layernorm(x, axis=-1, eps=1e-05):
    m = jnp.mean(x, axis=axis, keepdims=True)
    v = jnp.var(x, axis=axis, keepdims=True)
    return (x - m) / jnp.sqrt(v + eps)

def _scatter_add(tgt, idx, src, axis=0):
    return tgt.at[idx].add(src)

def _segment_sum(src, seg, n):
    return jax.ops.segment_sum(src, seg, n)
kernel_name = 'mk_gnn_preln_d4_gnn_r32_3f9e62'

def setup_inputs(seed: int=0):
    np.random.seed(seed)
    _w = jnp.asarray

    def _rec_inputs():
        import jax
        import jax.numpy as jnp
        _gk = jax.random.key(seed)
        x = -0.000202 + 1 * jax.random.normal(jax.random.fold_in(_gk, 1), (3125, 64), jnp.float32)
        _s = jax.random.randint(jax.random.fold_in(_gk, 2), (25000,), 0, 3125, jnp.int32)
        _d = jax.random.randint(jax.random.fold_in(_gk, 3), (25000,), 0, 3125, jnp.int32)
        _loop = jnp.arange(3125, dtype=jnp.int32)
        src = jnp.concatenate([_s, _d, _loop])
        dst = jnp.concatenate([_d, _s, _loop])
        _o = jnp.argsort(dst, stable=True)
        src = src[_o]
        dst = dst[_o]
        edge_attr_32 = -5.16925e-05 + 1.00005 * jax.random.normal(jax.random.fold_in(_gk, 13), (53125, 32), jnp.float32)
        edge_attr_64 = -8.16379e-05 + 0.999858 * jax.random.normal(jax.random.fold_in(_gk, 14), (53125, 64), jnp.float32)
        edge_weight = jax.random.uniform(jax.random.fold_in(_gk, 16), (53125,), jnp.float32, 0.0, 0.999999)
        edge_weight_n2 = jax.random.uniform(jax.random.fold_in(_gk, 17), (53125,), jnp.float32, 0.0, 0.999999)
        return (x, src, dst, edge_attr_32, edge_attr_64, edge_weight, edge_weight_n2)
    x, src, dst, edge_attr_32, edge_attr_64, edge_weight, edge_weight_n2 = _rec_inputs()

    def _L0_gnn_setup():
        import jax, jax.numpy as jnp
        import numpy as np
        N_NODES = 3125
        N_EDGES = 100000
        EDGE_OUT = 32
        HID = 128
        NODE_OUT = 64
        N_GRAPHS = 16
        key = jax.random.key(seed)
        ks = jax.random.split(key, 9)
        x = jax.random.normal(ks[0], (N_NODES, 64), dtype=jnp.float32)
        edge_index = jax.random.randint(ks[1], (2, N_EDGES), 0, N_NODES, dtype=jnp.int64)
        edge_attr = jax.random.normal(ks[2], (N_EDGES, EDGE_OUT), dtype=jnp.float32)
        u = jax.random.normal(ks[3], (N_GRAPHS, 1), dtype=jnp.float32)
        batch = jnp.sort(jax.random.randint(ks[4], (N_NODES,), 0, N_GRAPHS, dtype=jnp.int64))
        d_in = 3 * EDGE_OUT + 1
        W1 = jax.random.normal(ks[5], (d_in, HID), dtype=jnp.float32) / np.sqrt(d_in)
        b1 = jnp.zeros((HID,), dtype=jnp.float32)
        W2 = jax.random.normal(ks[6], (HID, NODE_OUT), dtype=jnp.float32) / np.sqrt(HID)
        b2 = jnp.zeros((NODE_OUT,), dtype=jnp.float32)
        return {'x': x, 'edge_index': edge_index, 'edge_attr': edge_attr, 'u': u, 'batch': batch, 'W1': W1, 'b1': b1, 'W2': W2, 'b2': b2}
    _L0_gnn_all = _L0_gnn_setup()
    _L0_gnn_in = {k: v for k, v in _L0_gnn_all.items() if k in ('u', 'W1', 'b1', 'W2', 'b2')}
    del _L0_gnn_all

    def _L1_gnn_setup():
        import jax, jax.numpy as jnp
        import numpy as np
        N, DIM, H, E = (50000, 64, 8, 25000)
        NEG_SLOPE = 0.2
        key = jax.random.key(seed)
        ks = jax.random.split(key, 6)
        x = jax.random.normal(ks[0], (N, DIM), dtype=jnp.float32)
        edge_index = jax.random.randint(ks[1], (2, E), 0, N, dtype=jnp.int32)
        W = jax.random.normal(ks[2], (DIM, H * DIM), dtype=jnp.float32) * (1.0 / np.sqrt(DIM))
        att_src = jax.random.normal(ks[3], (H, DIM), dtype=jnp.float32) * (1.0 / np.sqrt(DIM))
        att_dst = jax.random.normal(ks[4], (H, DIM), dtype=jnp.float32) * (1.0 / np.sqrt(DIM))
        bias = jnp.zeros((DIM,), dtype=jnp.float32)
        return {'x': x, 'edge_index': edge_index, 'W': W, 'att_src': att_src, 'att_dst': att_dst, 'bias': bias}
    _L1_gnn_all = _L1_gnn_setup()
    _L1_gnn_in = {k: v for k, v in _L1_gnn_all.items() if k in ('W', 'att_src', 'att_dst', 'bias')}
    del _L1_gnn_all

    def _L2_gnn_setup():
        import jax, jax.numpy as jnp
        import numpy as np
        N_NODES = 3125
        N_EDGES = 50000
        D = 64

        def _segment_mean(data, segment_ids, num_segments):
            num = jax.ops.segment_sum(data, segment_ids, num_segments=num_segments)
            den = jax.ops.segment_sum(jnp.ones_like(data), segment_ids, num_segments=num_segments)
            return num / (1e-06 + den)
        key = jax.random.key(seed)
        ks = jax.random.split(key, 10)
        s = 1.0 / np.sqrt(D)
        return {'node_emb': jax.random.normal(ks[0], (N_NODES, D), jnp.float32), 'edge_emb': jax.random.normal(ks[1], (N_EDGES, D), jnp.float32), 'W1_msg': jax.random.normal(ks[2], (3 * D, D), jnp.float32) * s, 'b1_msg': jnp.zeros((D,), jnp.float32), 'W2_msg': jax.random.normal(ks[3], (D, D), jnp.float32) * s, 'b2_msg': jnp.zeros((D,), jnp.float32), 'W1_upd': jax.random.normal(ks[4], (2 * D, D), jnp.float32) * s, 'b1_upd': jnp.zeros((D,), jnp.float32), 'W2_upd': jax.random.normal(ks[5], (D, D), jnp.float32) * s, 'b2_upd': jnp.zeros((D,), jnp.float32), 'senders': jax.random.randint(ks[6], (N_EDGES,), 0, N_NODES), 'receivers': jax.random.randint(ks[7], (N_EDGES,), 0, N_NODES)}
    _L2_gnn_all = _L2_gnn_setup()
    _L2_gnn_in = {k: v for k, v in _L2_gnn_all.items() if k in ('W1_msg', 'b1_msg', 'W2_msg', 'b2_msg', 'W1_upd', 'b1_upd', 'W2_upd', 'b2_upd')}
    del _L2_gnn_all

    def _L3_gnn_setup():
        import jax, jax.numpy as jnp
        import numpy as np
        N, E, D_IN, D_OUT = (2048, 32768, 64, 64)
        EPS = 1e-08
        key = jax.random.key(seed)
        ks = jax.random.split(key, 8)
        h = jax.random.normal(ks[0], (N, D_IN), dtype=jnp.float32)
        edge_index = jax.random.randint(ks[1], (2, E), 0, N, dtype=jnp.int64 if jax.config.jax_enable_x64 else jnp.int32)
        adj_v = jax.random.uniform(ks[2], (E,), dtype=jnp.float32)
        deg_v = jax.random.uniform(ks[3], (E,), dtype=jnp.float32)
        W = jax.random.normal(ks[4], (D_IN, D_OUT), dtype=jnp.float32) / np.sqrt(D_IN)
        b = jax.random.normal(ks[5], (D_OUT,), dtype=jnp.float32) * 0.01
        deg_coeff = jnp.array([0.5, 0.0], dtype=jnp.float32)
        coeff_param = jnp.zeros((3,), dtype=jnp.float32)
        scale_param = 2.0 * jnp.ones((1,), dtype=jnp.float32)
        return {'h': h, 'edge_index': edge_index, 'adj_v': adj_v, 'deg_v': deg_v, 'W': W, 'b': b, 'deg_coeff': deg_coeff, 'coeff_param': coeff_param, 'scale_param': scale_param}
    _L3_gnn_all = _L3_gnn_setup()
    _L3_gnn_in = {k: v for k, v in _L3_gnn_all.items() if k in ('W', 'b', 'deg_coeff', 'coeff_param', 'scale_param')}
    del _L3_gnn_all
    return {'x': x, 'src': src, 'dst': dst, 'edge_attr_32': edge_attr_32, 'edge_attr_64': edge_attr_64, 'edge_weight': edge_weight, 'edge_weight_n2': edge_weight_n2, 'L0_gnn_u': _L0_gnn_in['u'], 'L0_gnn_W1': _L0_gnn_in['W1'], 'L0_gnn_b1': _L0_gnn_in['b1'], 'L0_gnn_W2': _L0_gnn_in['W2'], 'L0_gnn_b2': _L0_gnn_in['b2'], 'L1_gnn_W': _L1_gnn_in['W'], 'L1_gnn_att_src': _L1_gnn_in['att_src'], 'L1_gnn_att_dst': _L1_gnn_in['att_dst'], 'L1_gnn_bias': _L1_gnn_in['bias'], 'L2_gnn_W1_msg': _L2_gnn_in['W1_msg'], 'L2_gnn_b1_msg': _L2_gnn_in['b1_msg'], 'L2_gnn_W2_msg': _L2_gnn_in['W2_msg'], 'L2_gnn_b2_msg': _L2_gnn_in['b2_msg'], 'L2_gnn_W1_upd': _L2_gnn_in['W1_upd'], 'L2_gnn_b1_upd': _L2_gnn_in['b1_upd'], 'L2_gnn_W2_upd': _L2_gnn_in['W2_upd'], 'L2_gnn_b2_upd': _L2_gnn_in['b2_upd'], 'L3_gnn_W': _L3_gnn_in['W'], 'L3_gnn_b': _L3_gnn_in['b'], 'L3_gnn_deg_coeff': _L3_gnn_in['deg_coeff'], 'L3_gnn_coeff_param': _L3_gnn_in['coeff_param'], 'L3_gnn_scale_param': _L3_gnn_in['scale_param']}

def reference(x, src, dst, edge_attr_32, edge_attr_64, edge_weight, edge_weight_n2, L0_gnn_u, L0_gnn_W1, L0_gnn_b1, L0_gnn_W2, L0_gnn_b2, L1_gnn_W, L1_gnn_att_src, L1_gnn_att_dst, L1_gnn_bias, L2_gnn_W1_msg, L2_gnn_b1_msg, L2_gnn_W2_msg, L2_gnn_b2_msg, L2_gnn_W1_upd, L2_gnn_b1_upd, L2_gnn_W2_upd, L2_gnn_b2_upd, L3_gnn_W, L3_gnn_b, L3_gnn_deg_coeff, L3_gnn_coeff_param, L3_gnn_scale_param):
    import jax
    import jax.numpy as jnp

    def _L0_gnn_ref(x, edge_index, edge_attr, u, batch, W1, b1, W2, b2):
        import jax, jax.numpy as jnp
        import numpy as np
        N_NODES = 3125
        N_EDGES = 100000
        EDGE_OUT = 32
        HID = 128
        NODE_OUT = 64
        N_GRAPHS = 16
        N = x.shape[0]
        row = edge_index[0]
        seg_sum = jax.ops.segment_sum(edge_attr, row, num_segments=N)
        seg_max = jax.ops.segment_max(edge_attr, row, num_segments=N)
        cnt = jax.ops.segment_sum(jnp.ones((edge_attr.shape[0], 1), edge_attr.dtype), row, num_segments=N)
        seg_mean = seg_sum / jnp.maximum(cnt, 1.0)
        seg_max = jnp.where(cnt > 0, seg_max, 0.0)
        h = jnp.concatenate([seg_sum, seg_max, seg_mean, u[batch]], axis=1)
        h = jax.nn.relu(h @ W1 + b1)
        return h @ W2 + b2

    def _L1_gnn_ref(x, edge_index, W, att_src, att_dst, bias):
        import jax, jax.numpy as jnp
        import numpy as np
        N, DIM, H, E = (50000, 64, 8, 25000)
        NEG_SLOPE = 0.2
        n = x.shape[0]
        loops = jnp.arange(n, dtype=edge_index.dtype)
        src = jnp.concatenate([edge_index[0], loops])
        dst = jnp.concatenate([edge_index[1], loops])
        h = (x @ W).reshape(n, H, DIM)
        a_src = jnp.einsum('nhc,hc->nh', h, att_src)
        a_dst = jnp.einsum('nhc,hc->nh', h, att_dst)
        logits = jax.nn.leaky_relu(a_src[src] + a_dst[dst], negative_slope=NEG_SLOPE)
        seg_max = jax.ops.segment_max(logits, dst, num_segments=n)
        seg_max = jnp.where(jnp.isfinite(seg_max), seg_max, 0.0)
        e = jnp.exp(logits - seg_max[dst])
        denom = jax.ops.segment_sum(e, dst, num_segments=n)
        alpha = e / denom[dst]
        msg = h[src] * alpha[:, :, None]
        out = jax.ops.segment_sum(msg, dst, num_segments=n)
        return out.mean(axis=1) + bias

    def _L2_gnn_ref(node_emb, edge_emb, W1_msg, b1_msg, W2_msg, b2_msg, W1_upd, b1_upd, W2_upd, b2_upd, senders, receivers):
        import jax, jax.numpy as jnp
        import numpy as np
        N_NODES = 3125
        N_EDGES = 50000
        D = 64

        def _segment_mean(data, segment_ids, num_segments):
            num = jax.ops.segment_sum(data, segment_ids, num_segments=num_segments)
            den = jax.ops.segment_sum(jnp.ones_like(data), segment_ids, num_segments=num_segments)
            return num / (1e-06 + den)
        sender_emb = node_emb[senders]
        receiver_emb = node_emb[receivers]
        msg_in = jnp.concatenate([edge_emb, sender_emb, receiver_emb], axis=-1)
        h = jax.nn.silu(msg_in @ W1_msg + b1_msg)
        edge_messages = h @ W2_msg + b2_msg
        node_messages = _segment_mean(edge_messages, receivers, node_emb.shape[0])
        upd_in = jnp.concatenate([node_emb, node_messages], axis=-1)
        hu = jax.nn.silu(upd_in @ W1_upd + b1_upd)
        new_node_emb = hu @ W2_upd + b2_upd
        return new_node_emb

    def _L3_gnn_ref(h, edge_index, adj_v, deg_v, W, b, deg_coeff, coeff_param, scale_param):
        import jax, jax.numpy as jnp
        import numpy as np
        N, E, D_IN, D_OUT = (2048, 32768, 64, 64)
        EPS = 1e-08
        n_nodes = h.shape[0]
        Wh = h @ W + b
        row, col = (edge_index[0], edge_index[1])
        sc = jax.nn.softplus(deg_coeff[0] * deg_v + deg_coeff[1])
        Wr = Wh[row]
        Wc = Wh[col]
        dot = jnp.sum(Wr * Wc, axis=-1)
        nr = jnp.sqrt(jnp.sum(Wr * Wr, axis=-1))
        nc = jnp.sqrt(jnp.sum(Wc * Wc, axis=-1))
        sim = dot / jnp.maximum(nr * nc, EPS)
        sim_pos = jax.nn.relu(sim)
        sim_neg = -jax.nn.relu(-sim)
        no_diag = (row != col).astype(Wh.dtype)
        base = adj_v * sc * no_diag
        prop_pos = jax.ops.segment_sum((base * sim_pos)[:, None] * Wc, row, num_segments=n_nodes)
        prop_neg = jax.ops.segment_sum((base * sim_neg)[:, None] * Wc, row, num_segments=n_nodes)
        coeff = jax.nn.softmax(coeff_param)
        scale = jax.nn.softplus(scale_param)
        return scale * (coeff[0] * prop_pos + coeff[1] * prop_neg + coeff[2] * Wh)
    edge_index = jnp.stack([src, dst])
    batch0 = jnp.zeros((3125,), jnp.int32)
    h = jnp.maximum(_layernorm(x, axis=-1), 0.0)
    x = x + _L0_gnn_ref(h, edge_index, edge_attr_32, L0_gnn_u, batch0, L0_gnn_W1, L0_gnn_b1, L0_gnn_W2, L0_gnn_b2)
    h = jnp.maximum(_layernorm(x, axis=-1), 0.0)
    x = x + _L1_gnn_ref(h, edge_index, L1_gnn_W, L1_gnn_att_src, L1_gnn_att_dst, L1_gnn_bias)
    h = jnp.maximum(_layernorm(x, axis=-1), 0.0)
    x = x + _L2_gnn_ref(h, edge_attr_64, L2_gnn_W1_msg, L2_gnn_b1_msg, L2_gnn_W2_msg, L2_gnn_b2_msg, L2_gnn_W1_upd, L2_gnn_b1_upd, L2_gnn_W2_upd, L2_gnn_b2_upd, src, dst)
    h = jnp.maximum(_layernorm(x, axis=-1), 0.0)
    x = x + _L3_gnn_ref(h, edge_index, edge_weight, edge_weight_n2, L3_gnn_W, L3_gnn_b, L3_gnn_deg_coeff, L3_gnn_coeff_param, L3_gnn_scale_param)
    return x

_drawn_inputs = setup_inputs


def setup_inputs(seed=0):
    import zlib

    import numpy as np

    out = dict(_drawn_inputs(seed))
    spreads = {'L0_gnn_b1': (0.0, 0.1),
     'L0_gnn_b2': (0.0, 0.1),
     'L1_gnn_bias': (0.0, 0.1),
     'L2_gnn_b1_msg': (0.0, 0.573),
     'L2_gnn_b2_msg': (0.0, 0.322),
     'L2_gnn_b1_upd': (0.0, 0.1),
     'L2_gnn_b2_upd': (0.0, 0.1),
     'L3_gnn_coeff_param': (0.0, 0.1)}
    factors = {'edge_weight_n2': 2.797,
     'L1_gnn_att_src': 6.726,
     'L1_gnn_att_dst': 44.54,
     'L3_gnn_b': 3.973,
     'L0_gnn_u': 2.817}
    for name, (base, spread) in spreads.items():
        noise = np.random.default_rng([zlib.crc32(name.encode()), seed]).standard_normal(out[name].shape)
        drawn = base * np.exp(spread * noise) if base else spread * noise
        out[name] = jnp.asarray(drawn.astype(out[name].dtype))
    for name, factor in factors.items():
        out[name] = (out[name] * factor).astype(out[name].dtype)
    return out
```

```python
import concourse.bass as bass
from concourse import mybir
from contextlib import ExitStack

F32 = mybir.dt.float32
BF16 = mybir.dt.bfloat16
I32 = mybir.dt.int32
ALU = mybir.AluOpType
ACT = mybir.ActivationFunctionType
AX = mybir.AxisListType

P = 128
N = 3125
E = 53125
NT = 25
NP = NT * P
M = N + E
J = 440
L = P * J
SORT_W = 512
SORT_L = P * SORT_W
CP = L // SORT_W
TB = 44
NBLK = J // TB
RING = 2
BIG = 3.4028235e38
KEY_ONE = 1 << 28
D = 64
H = 8
WIN = 16
NWIN = 196
ACC_W = 200
IB = 14
BODIES = 46
ITEMS = IB * BODIES
R0 = 36
RE = 66
R1 = 82
R2 = 128
R3 = 66


def bc(ap, shape):
    return ap.to_broadcast(shape)


class Kern:
    pass


class Order:

    def __init__(self, name, sb, dram):
        self.name = name
        self.keep = sb("keep" + name, [P, J])
        self.node0 = sb("node0" + name, [P, 1])
        self.fk = sb("fk" + name, [P, 1])
        self.nm = sb("nm" + name, [P, 1])
        self.cnt = sb("cnt" + name, [P, NT])
        self.end = sb("end" + name, [P, NT], I32)
        self.key = dram("key" + name, (SORT_L,), I32)
        self.idx = dram("idx" + name, (P, J), I32)
        self.endd = dram("endd" + name, (NP,))
        self.startd = dram("startd" + name, (NP,))
        self.cntd = dram("cntd" + name, (NP,))


def build(nc, a, out):
    top = ExitStack()
    with top:
        K = Kern()
        K.nc, K.a, K.out = nc, a, out
        K.semaphores = []

        def sb(n, s, d=F32):
            return top.enter_context(nc.sbuf_tensor(n, s, d))

        def dram(n, s, d=F32):
            return nc.dram_tensor(n, s, d, kind="Internal").ap()

        K.ident = sb("ident", [P, P])
        K.x = sb("x", [P, NT, D])
        K.hn = sb("hn", [P, NT, D])
        K.by_src = Order("s", sb, dram)
        K.by_dst = Order("d", sb, dram)
        K.meta = sb("meta", [P, J, 2], I32)
        K.st = sb("st", [P, D])
        K.nodes = sb("nodes", [P, J])
        K.keepc = sb("keepc", [CP, SORT_W])
        K.nxc = sb("nxc", [CP, 1])
        K.nmc = sb("nmc", [CP, 2])
        K.node0c = sb("node0c", [CP, 1], I32)
        K.nodec = sb("nodec", [CP, SORT_W])
        K.F = sb("F", [CP, H, SORT_W])
        K.base = sb("base", [P, J])
        K.co = sb("co", [P, 5])
        K.wh = sb("wh", [P, NT, R3])
        K.item_w = sb("item_w", [1, ITEMS], I32)
        K.item_slot = sb("item_slot", [1, ITEMS], I32)
        K.item_first = sb("item_first", [1, BODIES], I32)
        K.iota16 = sb("iota16", [P, WIN])
        K.idxdst = dram("idxdst", (P, J), I32)
        K.sums0 = dram("sums0", (L, D))
        K.sums2 = dram("sums2", (L, D))
        K.sums3 = dram("sums3", (L, D))
        K.edgeu = dram("edgeu", (P, J, D))
        K.srcd = dram("srcd", (L,), I32)
        K.idxtp = dram("idxtp", (P, J), I32)
        K.tab1 = dram("tab1", (NP, R1))
        K.tab2 = dram("tab2", (NP, R2))
        K.tab3 = dram("tab3", (NP, R3))
        K.g1 = dram("g1", (P, J, D + 1))

        sort_keys(K, K.by_src, first=True)
        list_setup(K, K.by_src)
        layer0_gather(K)
        layer0_finish(K)
        sort_keys(K, K.by_dst)
        list_setup(K, K.by_dst)
        edge_pass(K)
        src_to_tiles(K)
        with nc.sbuf_tensor("atp", [P, J, 2 * H], F32) as K.atp:
            layer1_gather(K)
            layer1_softmax(K)
        with nc.sbuf_tensor("acc", [P, ACC_W, D + 1], F32) as K.acc:
            with nc.sbuf_tensor("item_rel", [P, ITEMS], F32) as K.item_rel, \
                    nc.sbuf_tensor("item_ex", [P, H, ITEMS], F32) as K.item_ex:
                layer1_items(K)
                layer1_sums(K)
            layer1_finish(K)
        renew_semaphores(K)
        layer2_gather(K)
        layer2_finish(K)
        layer3_gather(K)
        layer3_finish(K)


def renew_semaphores(K):
    K.nc.clear_and_free_semaphores(K.semaphores)
    K.nc.all_engine_barrier()
    K.semaphores = []


class Phase:

    def __init__(self, K, name):
        self.K, self.nc, self.name, self.st = K, K.nc, name, ExitStack()

    def __enter__(self):
        self.st.__enter__()
        return self

    def __exit__(self, *e):
        return self.st.__exit__(*e)

    def sb(self, n, s, d=F32):
        return self.st.enter_context(self.nc.sbuf_tensor(f"{self.name}_{n}", s, d))

    def ps(self, n, s=(P, 512), d=F32):
        return self.st.enter_context(self.nc.psum_tensor(f"{self.name}_{n}", list(s), d))

    def sem(self, n):
        s = self.nc.alloc_semaphore(name=f"{self.name}_{n}")
        self.K.semaphores.append(s)
        return s

    def sems(self, *names):
        return [self.sem(n) for n in names]


def sort_keys(K, by, first=False):
    nc = K.nc
    W = SORT_W
    with Phase(K, "sort" + by.name) as ph:
        raw = ph.sb("raw", [P, W], I32)
        cid = ph.sb("cid", [P, W], I32)
        X = [ph.sb("x0", [P, W]), ph.sb("x1", [P, W])]
        pcol = ph.sb("pcol", [P, 1], I32)
        bits = ph.sb("bits", [P, 8], I32)
        sgn = ph.sb("sgn", [P, 8])
        flip = ph.sb("flip", [P, 8])
        neg = ph.sb("neg", [P, 1])
        turn_ps = [ph.ps(f"turn{i}") for i in range(2)]
        loaded, consts, cleared, step, turned, swapped, done_, stored = ph.sems(
            "loaded", "consts", "cleared", "step", "turned", "swapped", "done", "stored")
        swaps = []
        final = [None]

        with nc.Block() as block:
            @block.gpsimd
            def _(pool):
                nc.gpsimd.iota(cid[:, :], [[1, W]], base=KEY_ONE, channel_multiplier=W)
                if first:
                    nc.gpsimd.memset(K.x[:, NT - 1, :], 0.0).then_inc(cleared, 1)
                    nc.gpsimd.memset(K.ident[:, :], 0.0).then_inc(cleared, 1)
                    pool.wait_ge(cleared, 2)
                    nc.gpsimd.affine_select(out=K.ident[:, :], in_=K.ident[:, :], compare_op=ALU.not_equal, fill=1.0,
                                            base=0, pattern=[[-1, P]], channel_multiplier=1)
                nc.gpsimd.iota(pcol[:, :], [[1, 1]], base=0, channel_multiplier=1).then_inc(consts, 1)

            @block.vector
            def _(dve):
                n = 0

                def did(ins):
                    nonlocal n
                    n += 1
                    ins.then_inc(step, 1)

                def settle():
                    dve.wait_ge(step, n)

                dve.wait_ge(consts, 1)
                dve.wait_ge(loaded, 16)
                for b in range(7):
                    did(nc.vector.tensor_scalar(bits[:, b:b + 1], pcol[:, :], b, 1, ALU.logical_shift_right, ALU.bitwise_and))
                did(nc.vector.tensor_scalar(raw[:, :], raw[:, :], 16, None, ALU.logical_shift_left))
                settle()
                did(nc.vector.tensor_scalar(sgn[:, 0:7], bits[:, 0:7], -2.0, 1.0, ALU.mult, ALU.add))
                did(nc.vector.memset(sgn[:, 7:8], 1.0))
                did(nc.vector.tensor_tensor(X[0][:, :].bitcast(I32), raw[:, :], cid[:, :], ALU.bitwise_or))
                settle()
                did(nc.vector.tensor_tensor(flip[:, 0:7], sgn[:, 1:8], sgn[:, 0:7], ALU.mult))
                did(nc.vector.tensor_scalar(neg[:, :], sgn[:, 0:1], -1.0, None, ALU.mult))
                settle()
                cur, other = X
                for k in range(1, 17):
                    if k <= 8:
                        half = 2 ** (k - 1)
                        v = cur[:, :].rearrange("p (a x) -> p a x", x=4 * half)
                        part = v[:, :, 2 * half:] if k == 1 else v[:, :, half:3 * half]
                        did(nc.vector.tensor_scalar(part, part, -1.0, None, ALU.mult))
                    elif k == 9:
                        did(nc.vector.tensor_scalar(cur[:, 0:256], cur[:, 0:256], sgn[:, 0:1], None, ALU.mult))
                        did(nc.vector.tensor_scalar(cur[:, 256:512], cur[:, 256:512], neg[:, 0:1], None, ALU.mult))
                    else:
                        did(nc.vector.tensor_scalar(cur[:, :], cur[:, :], flip[:, k - 10:k - 9], None, ALU.mult))
                    settle()
                    for b in range(k - 1, -1, -1):
                        if k >= 10 and b in (k - 1, 8):
                            swaps.append((cur, other, n))
                            dve.wait_ge(swapped, len(swaps))
                            cur, other = other, cur
                        d = 2 ** (b - 9) if b >= 9 else 2 ** b
                        s = cur[:, :].rearrange("p (a two d) -> p a two d", two=2, d=d)
                        t = other[:, :].rearrange("p (a two d) -> p a two d", two=2, d=d)
                        did(nc.vector.tensor_tensor(t[:, :, 0, :], s[:, :, 0, :], s[:, :, 1, :], ALU.min))
                        did(nc.vector.tensor_tensor(t[:, :, 1, :], s[:, :, 0, :], s[:, :, 1, :], ALU.max))
                        settle()
                        cur, other = other, cur
                nc.vector.tensor_scalar(raw[:, :], cur[:, :].bitcast(I32), KEY_ONE - 1, None,
                                        ALU.bitwise_and).then_inc(done_, 1)

            @block.tensor
            def _(pe):
                pe.wait_ge(consts, 1)
                for m, (c, t, at) in enumerate(swaps):
                    pe.wait_ge(step, at)
                    for g in range(4):
                        last = nc.tensor.transpose(turn_ps[m % 2][:, g * P:(g + 1) * P], c[:, g * P:(g + 1) * P], K.ident[:, :])
                    last.then_inc(turned, 1)

            @block.scalar
            def _(act):
                for m, (c, t, at) in enumerate(swaps):
                    act.wait_ge(turned, m + 1)
                    nc.scalar.copy(t[:, :], turn_ps[m % 2][:, :]).then_inc(swapped, 1)

            @block.sync
            def _(sp):
                sp.dma_start(raw[:, :], K.a["nodes" + by.name].rearrange("(p f) -> p f", p=P)).then_inc(loaded, 16)
                if first:
                    sp.dma_start(K.x[:, 0:NT - 1, :], K.a["x"][0:(NT - 1) * P, :].rearrange("(w p) d -> p w d", p=P)).then_inc(stored, 16)
                    sp.wait_ge(cleared, 2)
                    sp.dma_start(K.x[0:N - (NT - 1) * P, NT - 1, :], K.a["x"][(NT - 1) * P:N, :]).then_inc(stored, 16)
                sp.wait_ge(done_, 1)
                sp.dma_start(by.key.rearrange("(p f) -> p f", p=P), raw[:, :]).then_inc(stored, 16)
                sp.wait_ge(stored, 48 if first else 16)


def list_setup(K, by):
    nc = K.nc
    HI, LO = 50, 64
    with Phase(K, "set" + by.name) as ph:
        key = ph.sb("key", [P, J], I32)
        nxt = ph.sb("nxt", [P, 1], I32)
        ent = ph.sb("ent", [P, J], I32)
        nodei = ph.sb("nodei", [P, J], I32)
        lo_i = ph.sb("lo_i", [P, J], I32)
        node = ph.sb("node", [P, J])
        hi = ph.sb("hi", [P, J])
        lo = ph.sb("lo", [P, J])
        t0 = ph.sb("t0", [P, J])
        t1 = ph.sb("t1", [P, J])
        c = ph.sb("c", [P, 8])
        iot = ph.sb("iot", [P, LO])
        one_hi = ph.sb("one_hi", [P, 2, TB, HI], BF16)
        one_lo = ph.sb("one_lo", [P, 2, TB, LO], BF16)
        zero = ph.sb("zero", [P, LO], BF16)
        lower = ph.sb("lower", [HI, HI])
        cnt = ph.sb("cnt", [HI, LO])
        run = ph.sb("run", [HI, LO])
        start = ph.sb("start", [HI, LO])
        ones = ph.sb("ones", [HI, LO])
        base = ph.sb("base", [HI, 1])
        endf = ph.sb("endf", [P, NT])
        hist = ph.ps("hist")
        basep = ph.ps("basep")
        loaded, consts, fill, hot, used, dn, d2, p2, stored, lded = ph.sems(
            "loaded", "consts", "fill", "hot", "used", "dn", "d2", "p2", "stored", "lded")
        kd = by.key
        keep, node0, fk, nm = by.keep, by.node0, by.fk, by.nm
        with nc.Block() as block:
            @block.sync
            def _(sp):
                sp.dma_start(key[:, :], kd[0:L].rearrange("(p j) -> p j", p=P)).then_inc(loaded, 16)
                with nc.allow_non_contiguous_dma(reason="one value per partition"):
                    sp.dma_start(nxt[:, :], kd[J:J + L].rearrange("(p j) -> p j", p=P)[:, 0:1]).then_inc(loaded, 16)
                sp.wait_ge(d2, 1)
                sp.dma_start(by.idx, ent[:, :]).then_inc(stored, 16)
                sp.wait_ge(d2, 2)
                sp.dma_start(by.endd.rearrange("(h l) -> h l", l=LO), run[:, :]).then_inc(stored, 16)
                sp.dma_start(by.startd.rearrange("(h l) -> h l", l=LO), start[:, :]).then_inc(stored, 16)
                sp.dma_start(by.cntd.rearrange("(h l) -> h l", l=LO), cnt[:, :]).then_inc(stored, 16)
                sp.wait_ge(stored, 64)
                ends = by.endd.rearrange("(w p) -> p w", p=P)
                counts = by.cntd.rearrange("(w p) -> p w", p=P)
                with nc.allow_non_contiguous_dma(reason="one value per node, once"):
                    sp.dma_start(endf[:, :], ends).then_inc(lded, 16)
                    sp.dma_start(by.cnt[:, 0:NT - 1], counts[:, 0:NT - 1]).then_inc(lded, 16)
                    sp.dma_start(by.cnt[0:N - (NT - 1) * P, NT - 1:], counts[0:N - (NT - 1) * P, NT - 1:]).then_inc(lded, 16)
                sp.wait_ge(lded, 48)

            @block.gpsimd
            def _(pool):
                nc.gpsimd.iota(iot[:, :], [[1, LO]], base=0, channel_multiplier=0, allow_small_or_imprecise_dtypes=True)
                nc.gpsimd.memset(lower[:, :], 0.0).then_inc(fill, 1)
                pool.wait_ge(fill, 1)
                nc.gpsimd.affine_select(out=lower[:, :], in_=lower[:, :], compare_op=ALU.is_ge, fill=1.0,
                                        base=0, pattern=[[-1, HI]], channel_multiplier=1).then_inc(consts, 1)

            @block.vector
            def _(dve):
                v = nc.vector
                v.memset(zero[:, :], 0.0).then_inc(dn, 1)
                v.memset(ones[:, :], 1.0)
                v.memset(by.cnt[:, :], 0.0)
                dve.wait_ge(loaded, 32)
                dve.wait_ge(consts, 1)
                v.tensor_scalar(ent[:, :], key[:, :], 0xFFFF, None, ALU.bitwise_and)
                v.tensor_scalar(nodei[:, :], key[:, :], 16, None, ALU.logical_shift_right)
                v.tensor_scalar(nxt[:, :], nxt[:, :], 0xFFFF, None, ALU.bitwise_and)
                v.drain()
                v.tensor_scalar(lo_i[:, :], nodei[:, :], 63, None, ALU.bitwise_and)
                v.tensor_copy(node[:, :], nodei[:, :])
                v.tensor_scalar(t0[:, :], ent[:, :], float(N), None, ALU.is_ge)
                v.tensor_scalar(t1[:, :], ent[:, :], float(M), None, ALU.is_lt)
                v.tensor_scalar(c[:, 0:1], nxt[:, :], float(N), None, ALU.is_ge)
                v.tensor_scalar(c[:, 1:2], nxt[:, :], float(M), None, ALU.is_lt)
                v.drain()
                v.tensor_scalar(nodei[:, :], nodei[:, :], 6, None, ALU.logical_shift_right)
                v.tensor_copy(lo[:, :], lo_i[:, :])
                v.tensor_tensor(keep[:, :], t0[:, :], t1[:, :], ALU.mult)
                v.tensor_tensor(c[:, 2:3], c[:, 0:1], c[:, 1:2], ALU.mult)
                v.tensor_tensor(c[:, 3:4], node[:, 0:1], node[:, J - 1:J], ALU.is_equal)
                v.tensor_copy(node0[:, :], node[:, 0:1])
                if by is K.by_src:
                    v.tensor_copy(K.nodes[:, :], node[:, :])
                v.drain().then_inc(d2, 1)
                v.tensor_copy(hi[:, :], nodei[:, :])
                v.tensor_tensor(nm[:, :], keep[:, 0:1], c[:, 3:4], ALU.mult)
                v.drain()
                v.tensor_tensor(c[:, 4:5], nm[:, :], c[:, 2:3], ALU.mult)
                v.drain()
                v.tensor_scalar(c[:, 5:6], c[:, 4:5], -1.0, 1.0, ALU.mult, ALU.add)
                v.tensor_scalar(c[:, 6:7], node[:, 0:1], 1.0, None, ALU.add)
                v.drain()
                v.tensor_tensor(c[:, 5:6], c[:, 5:6], keep[:, 0:1], ALU.mult)
                v.drain()
                v.tensor_tensor(c[:, 5:6], c[:, 5:6], c[:, 6:7], ALU.mult)
                v.drain()
                v.tensor_scalar(fk[:, :], c[:, 5:6], -1.0, None, ALU.add)
                with dve.Fori(0, NBLK // 2) as it:
                    for s in range(2):
                        dve.wait_ge(used, it * 2 + s + 1)
                        js = bass.ds((it * 2 + s) * TB, TB)
                        v.tensor_tensor(one_hi[:, s], hi[:, js].unsqueeze(2).to_broadcast([P, TB, HI]),
                                        iot[:, 0:HI].unsqueeze(1).to_broadcast([P, TB, HI]), ALU.is_equal)
                        v.tensor_tensor(one_lo[:, s], lo[:, js].unsqueeze(2).to_broadcast([P, TB, LO]),
                                        iot[:, :].unsqueeze(1).to_broadcast([P, TB, LO]), ALU.is_equal).then_inc(hot, 1)
                dve.wait_ge(p2, 1)
                v.tensor_copy(cnt[:, :], hist[0:HI, 0:LO])
                v.drain()
                v.tensor_tensor_scan(run[:, :], ones[:, :], cnt[:, :], 0.0, ALU.mult, ALU.add)
                v.drain().then_inc(dn, 1)
                dve.wait_ge(p2, 2)
                v.tensor_copy(base[:, :], basep[0:HI, 0:1])
                v.drain()
                v.tensor_scalar(run[:, :], run[:, :], base[:, :], -1.0, ALU.add, ALU.add)
                v.drain()
                v.tensor_tensor(start[:, :], run[:, :], cnt[:, :], ALU.subtract)
                v.drain()
                v.tensor_scalar(start[:, :], start[:, :], 1.0, None, ALU.add)
                v.tensor_scalar(cnt[:, :], cnt[:, :], -1.0, 0.0, ALU.add, ALU.max)
                v.drain().then_inc(d2, 1)
                dve.wait_ge(lded, 48)
                v.tensor_copy(by.end[:, :], endf[:, :])

            @block.tensor
            def _(pe):
                pe.wait_ge(dn, 1)
                nc.tensor.matmul(hist[0:HI, 0:LO], zero[:, 0:HI], zero[:, :], start=True, stop=False).then_inc(used, 2)
                with pe.Fori(0, NBLK // 2) as it:
                    for s in range(2):
                        pe.wait_ge(hot, it * 2 + s + 1)
                        for j in range(TB):
                            last = nc.tensor.matmul(hist[0:HI, 0:LO], one_hi[:, s, j, :], one_lo[:, s, j, :],
                                                    start=False, stop=False)
                        last.then_inc(used, 1)
                nc.tensor.matmul(hist[0:HI, 0:LO], zero[:, 0:HI], zero[:, :], start=False, stop=True).then_inc(p2, 1)
                pe.wait_ge(dn, 2)
                nc.tensor.matmul(basep[0:HI, 0:1], lower[:, :], run[:, LO - 1:LO], start=True, stop=True).then_inc(p2, 1)


def rounds(engine, body, n=None):
    body(0, True)
    with engine.Fori(1, n or NBLK // RING) as it:
        body(it, False)


class Ring:

    def __init__(self, ph, width, dt=F32):
        self.rows = ph.sb("rows", [P, RING, TB, width], dt)
        self.idx = ph.sb("ring_idx", [P, RING, TB], I32)
        self.indexed = [ph.sem(f"indexed{s}") for s in range(RING)]
        self.gathered = [ph.sem(f"gathered{s}") for s in range(RING)]
        self.begun = ph.sem("begun")


def block_cols(it, s):
    return bass.ds((it * RING + s) * TB, TB)


def gather_rounds(nc, pool, ring, table, freed):
    def body(it, first):
        for s in range(RING):
            pool.wait_ge(ring.indexed[s], (it + 1) * 16)
            if not first:
                for sem, per in freed:
                    pool.wait_ge(sem[s], it * per)
            pool.sem_inc(ring.begun, 1)
            for j in range(TB):
                nc.gpsimd.indirect_dma_start(
                    out=ring.rows[:, s, j, :], out_offset=None, in_=table,
                    in_offset=bass.IndirectOffsetOnAxis(ap=ring.idx[:, s, j:j + 1], axis=0)
                ).then_inc(ring.gathered[s], 16)
    rounds(pool, body)


def load_idx(sp, ring, idx, it, s, first):
    if not first:
        sp.wait_ge(ring.gathered[s], it * TB * 16)
    sp.dma_start(ring.idx[:, s, :], idx[:, block_cols(it, s)]).then_inc(ring.indexed[s], 16)


def seg_masks(v, keep, js, kb, mb=None, nb=None, mk=None):
    v.tensor_copy(kb[:, :], keep[:, js])
    v.drain()
    if nb is not None:
        v.tensor_scalar(nb[:, :], kb[:, :], -1.0, BIG, ALU.add, ALU.mult)
    if mb is not None:
        v.tensor_scalar(mb[:, :], kb[:, :], 2.0, -1.0, ALU.mult, ALU.add)
        v.drain()
        v.tensor_scalar(mb[:, :], mb[:, :], BIG, None, ALU.mult)
    if mk is not None:
        v.tensor_scalar(mk[:, :], kb[:, :], -1.0, 1.0, ALU.mult, ALU.add)
    v.drain()


def layer0_gather(K):
    nc = K.nc
    with Phase(K, "l0g") as ph:
        ring = Ring(ph, R0, I32)
        sums = ph.sb("sums", [P, RING, TB, D])
        dsts = ph.sb("dsts", [P, J], I32)
        kb = ph.sb("kb", [P, TB])
        mb = ph.sb("mb", [P, TB])
        nb = ph.sb("nb", [P, TB])
        scanned = [ph.sem(f"scanned{s}") for s in range(RING)]
        carried = [ph.sem(f"carried{s}") for s in range(RING)]
        kept = [ph.sem(f"kept{s}") for s in range(RING)]
        stored = [ph.sem(f"stored{s}") for s in range(RING)]
        meta_stored = ph.sem("meta_stored")
        out = K.sums0.rearrange("(p j) d -> p j d", p=P)
        half = D // 2

        def store(sp, it, s):
            sp.dma_start(out[:, block_cols(it, s), :], sums[:, s]).then_inc(stored[s], 16)

        with nc.Block() as block:
            @block.gpsimd
            def _(pool):
                gather_rounds(nc, pool, ring, K.a["rec_s"], [(carried, 1), (kept, 2)])

            @block.sync
            def _(sp):
                def body(it, first):
                    for s in range(RING):
                        load_idx(sp, ring, K.by_src.idx, it, s, first)
                        if not first:
                            sp.wait_ge(scanned[s], it)
                            store(sp, it - 1, s)
                rounds(sp, body)
                for s in range(RING):
                    sp.wait_ge(scanned[s], NBLK // RING)
                    store(sp, NBLK // RING - 1, s)
                for s in range(RING):
                    sp.wait_ge(stored[s], NBLK // RING * 16)

            @block.scalar
            def _(act):
                def body(it, first):
                    for s in range(RING):
                        act.wait_ge(ring.gathered[s], (it + 1) * TB * 16)
                        nc.scalar.copy(dsts[:, block_cols(it, s)], ring.rows[:, s, :, half + 2]).then_inc(kept[s], 1)
                        nc.scalar.copy(K.meta[:, block_cols(it, s), :], ring.rows[:, s, :, half:half + 2]).then_inc(kept[s], 1)
                rounds(act, body)
                for s in range(RING):
                    act.wait_ge(kept[s], 2 * NBLK // RING)
                act.dma_start(K.idxdst, dsts[:, :]).then_inc(meta_stored, 16)
                act.wait_ge(meta_stored, 16)

            @block.vector
            def _(dve):
                v = nc.vector
                v.memset(K.st[:, 0:half], 0.0)
                v.memset(K.st[:, half:D], -BIG)

                def body(it, first):
                    for s in range(RING):
                        r = ring.rows[:, s, :, 0:half].bitcast(F32)
                        dve.wait_ge(ring.gathered[s], (it + 1) * TB * 16)
                        if not first:
                            dve.wait_ge(stored[s], it * 16)
                        seg_masks(v, K.by_src.keep, block_cols(it, s), kb, mb=mb, nb=nb)
                        for f in range(half):
                            v.tensor_tensor_scan(sums[:, s, :, f], kb[:, :], r[:, :, f], K.st[:, f:f + 1], ALU.mult, ALU.add)
                        v.drain()
                        v.tensor_tensor(r, r, nb[:, :].unsqueeze(2).to_broadcast([P, TB, half]), ALU.add)
                        v.drain()
                        for f in range(half):
                            v.tensor_tensor_scan(sums[:, s, :, half + f], mb[:, :], r[:, :, f], K.st[:, half + f:half + f + 1],
                                                 ALU.min, ALU.max)
                        v.drain().then_inc(scanned[s], 1)
                        v.tensor_copy(K.st[:, :], sums[:, s, TB - 1, :]).then_inc(carried[s], 1)
                rounds(dve, body)


def collect(K, by, table, nsum, res):
    nc = K.nc
    act_name = table.tensor.name
    with Phase(K, "col" + act_name) as ph:
        iot = ph.sb("iot", [P, NP])
        sel = ph.sb("sel", [P, NP])
        nmb = ph.sb("nmb", [P, D])
        act = ph.sb("act", [P, 1])
        nmt = ph.sb("nmt", [D, P])
        tot = ph.sb("tot", [D, P])
        shf = ph.sb("shf", [D, P])
        car = ph.sb("car", [P, D + 1])
        has = ph.sb("has", [P, NT])
        tmp = ph.sb("tmp", [P, NT, D + 1])
        nmp = ph.ps("nmp")
        stp = ph.ps("stp")
        bp = [ph.ps(f"bp{i}") for i in range(4)]
        ready, made, pm, got = ph.sems("ready", "made", "pm", "got")
        nm, fk, end = by.nm, by.fk, by.end
        with nc.Block() as block:
            @block.gpsimd
            def _(pool):
                nc.gpsimd.iota(iot[:, :], [[1, NP]], base=0, channel_multiplier=0,
                               allow_small_or_imprecise_dtypes=True).then_inc(ready, 1)
                for w in range(NT):
                    nc.gpsimd.indirect_dma_start(out=res[:, w, :], out_offset=None, in_=table,
                                                 in_offset=bass.IndirectOffsetOnAxis(ap=end[:, w:w + 1], axis=0)).then_inc(got, 16)

            @block.tensor
            def _(pe):
                pe.wait_ge(made, 1)
                nc.tensor.matmul(nmp[0:D, 0:P], nmb[:, :], K.ident[:, :], start=True, stop=True)
                nc.tensor.transpose(stp[0:D, 0:P], K.st[:, :], K.ident[:, :]).then_inc(pm, 1)
                pe.wait_ge(made, 2)
                nc.tensor.transpose(stp[:, P:P + D], shf[:, :], K.ident[0:D, 0:D]).then_inc(pm, 1)
                pe.wait_ge(made, 3)
                for w in range(NT):
                    last = nc.tensor.matmul(bp[w // 7][:, w % 7 * (D + 1):(w % 7 + 1) * (D + 1)], sel[:, w * P:(w + 1) * P], car[:, :],
                                            start=True, stop=True)
                last.then_inc(pm, 1)

            @block.vector
            def _(dve):
                v = nc.vector
                v.tensor_copy(nmb[:, :], nm[:, 0:1].to_broadcast([P, D]))
                v.tensor_scalar(act[:, :], fk[:, :], 0.0, None, ALU.is_ge)
                v.memset(shf[:, 0:1], 0.0)
                v.memset(car[:, D:D + 1], 1.0)
                v.drain().then_inc(made, 1)
                dve.wait_ge(pm, 1)
                v.tensor_copy(nmt[:, :], nmp[0:D, 0:P])
                v.drain()
                if nsum < D:
                    v.tensor_scalar(nmt[nsum:, :], nmt[nsum:, :], 2.0, -1.0, ALU.mult, ALU.add)
                    v.drain()
                    v.tensor_scalar(nmt[nsum:, :], nmt[nsum:, :], BIG, None, ALU.mult)
                    v.drain()
                    v.tensor_tensor_scan(tot[nsum:, :], nmt[nsum:, :], stp[nsum:D, 0:P], -BIG, ALU.min, ALU.max)
                v.tensor_tensor_scan(tot[0:nsum, :], nmt[0:nsum, :], stp[0:nsum, 0:P], 0.0, ALU.mult, ALU.add)
                v.drain()
                v.tensor_copy(shf[:, 1:P], tot[:, 0:P - 1])
                v.drain().then_inc(made, 1)
                dve.wait_ge(ready, 1)
                v.tensor_scalar(sel[:, :], iot[:, :], fk[:, 0:1], None, ALU.is_equal)
                dve.wait_ge(pm, 2)
                v.tensor_scalar(car[:, 0:D], stp[:, P:P + D], act[:, 0:1], None, ALU.mult)
                v.drain().then_inc(made, 1)
                dve.wait_ge(got, NT * 16)
                dve.wait_ge(pm, 3)
                for g in range(4):
                    w0, w1 = 7 * g, min(7 * g + 7, NT)
                    b = bp[g][:, 0:(w1 - w0) * (D + 1)].rearrange("p (w d) -> p w d", d=D + 1)
                    v.tensor_tensor(res[:, w0:w1, 0:nsum], res[:, w0:w1, 0:nsum], b[:, :, 0:nsum], ALU.add)
                    if nsum < D:
                        v.tensor_copy(tmp[:, w0:w1, nsum:], b[:, :, nsum:])
                if nsum < D:
                    v.drain()
                    v.tensor_scalar(has[:, :], tmp[:, :, D], -1.0, BIG, ALU.add, ALU.mult)
                    v.drain()
                    v.tensor_tensor(tmp[:, :, nsum:D], tmp[:, :, nsum:D], has[:, :].unsqueeze(2).to_broadcast([P, NT, D - nsum]), ALU.add)
                    v.drain()
                    v.tensor_tensor(res[:, :, nsum:], res[:, :, nsum:], tmp[:, :, nsum:D], ALU.max)


def node_dense(K, name, feat, F, w1, hid, func, b1, w2, put, after=None, loads=(), w1d=None):
    nc = K.nc
    with Phase(K, name) as ph:
        W1 = ph.sb("W1", [F, hid]) if w1 is not None else w1d
        W2 = ph.sb("W2", [hid, D]) if w2 is not None else None
        B1 = ph.sb("B1", [hid, 1]) if w2 is not None else None
        ft = ph.sb("ft", [F, 2, P])
        ht = ph.sb("ht", [hid, 2, P])
        pa, pb, pc = ([ph.ps(f"{n}{i}") for i in range(2)] for n in "abc")
        loaded, turned, moved, first, acted, second, used = ph.sems(
            "loaded", "turned", "moved", "first", "acted", "second", "used")
        two = w2 is not None
        nl = (w1 is not None) + 2 * two
        C = D if two else hid
        with nc.Block() as block:
            @block.sync
            def _(sp):
                if w1 is not None:
                    sp.dma_start(W1[:, :], w1).then_inc(loaded, 16)
                if two:
                    sp.dma_start(W2[:, :], w2).then_inc(loaded, 16)
                    with nc.allow_non_contiguous_dma(reason="a bias as a column"):
                        sp.dma_start(B1[:, :], b1.unsqueeze(1)).then_inc(loaded, 16)
                if nl:
                    sp.wait_ge(loaded, 16 * nl)

            @block.tensor
            def _(pe):
                if nl:
                    pe.wait_ge(loaded, 16 * nl)
                for w in range(NT + 2):
                    if w < NT:
                        if w >= 2:
                            pe.wait_ge(moved, w - 1)
                        nc.tensor.transpose(pa[w % 2][0:F, 0:P], feat[:, w, :], K.ident[:, :]).then_inc(turned, 1)
                    if 1 <= w <= NT:
                        u = w - 1
                        pe.wait_ge(moved, u + 1)
                        if two:
                            if u >= 2:
                                pe.wait_ge(acted, u - 1)
                            nc.tensor.matmul(pb[u % 2][0:hid, 0:P], W1[:, :], ft[:, u % 2, :], start=True, stop=True).then_inc(first, 1)
                        else:
                            if u >= 2:
                                pe.wait_ge(used, u - 1)
                            nc.tensor.matmul(pc[u % 2][:, 0:hid], ft[:, u % 2, :], W1[:, :], start=True, stop=True).then_inc(second, 1)
                    if two and w >= 2:
                        u = w - 2
                        pe.wait_ge(acted, u + 1)
                        if u >= 2:
                            pe.wait_ge(used, u - 1)
                        nc.tensor.matmul(pc[u % 2][:, 0:D], ht[:, u % 2, :], W2[:, :], start=True, stop=True).then_inc(second, 1)

            @block.scalar
            def _(act):
                if nl:
                    act.wait_ge(loaded, 16 * nl)
                for w in range(NT + 1):
                    if w < NT:
                        act.wait_ge(turned, w + 1)
                        if w >= 2:
                            act.wait_ge(first if two else second, w - 1)
                        nc.scalar.copy(ft[:, w % 2, :], pa[w % 2][0:F, 0:P]).then_inc(moved, 1)
                    if two and w >= 1:
                        u = w - 1
                        act.wait_ge(first, u + 1)
                        if u >= 2:
                            act.wait_ge(second, u - 1)
                        nc.scalar.activation(ht[:, u % 2, :], pb[u % 2][0:hid, 0:P], func, bias=B1[:, 0:1]).then_inc(acted, 1)

            @block.vector
            def _(dve):
                for w in range(NT):
                    dve.wait_ge(second, w + 1)
                    put(nc.vector, w, pc[w % 2][:, 0:C]).then_inc(used, 1)


def normalise(K, name):
    nc = K.nc
    with Phase(K, name) as ph:
        mean = ph.sb("mean", [P, NT])
        var = ph.sb("var", [P, NT])
        sq = ph.sb("sq", [P, NT, D])
        d1, rooted = ph.sems("d1", "rooted")
        with nc.Block() as block:
            @block.vector
            def _(dve):
                v = nc.vector
                wide = lambda t: t[:, :].unsqueeze(2).to_broadcast([P, NT, D])
                v.tensor_reduce(mean[:, :], K.x[:, :, :], AX.X, ALU.add)
                v.drain()
                v.tensor_scalar(mean[:, :], mean[:, :], 1.0 / D, None, ALU.mult)
                v.drain()
                v.tensor_tensor(K.hn[:, :, :], K.x[:, :, :], wide(mean), ALU.subtract)
                v.drain()
                v.tensor_tensor(sq[:, :, :], K.hn[:, :, :], K.hn[:, :, :], ALU.mult)
                v.drain()
                v.tensor_reduce(var[:, :], sq[:, :, :], AX.X, ALU.add)
                v.drain()
                v.tensor_scalar(var[:, :], var[:, :], 1.0 / D, 1e-5, ALU.mult, ALU.add)
                v.drain().then_inc(d1, 1)
                dve.wait_ge(rooted, 1)
                v.reciprocal(var[:, :], var[:, :])
                v.drain()
                v.tensor_tensor(K.hn[:, :, :], K.hn[:, :, :], wide(var), ALU.mult)
                v.drain()
                v.tensor_scalar(K.hn[:, :, :], K.hn[:, :, :], 0.0, None, ALU.max)

            @block.scalar
            def _(act):
                act.wait_ge(d1, 1)
                nc.scalar.sqrt(var[:, :], var[:, :]).then_inc(rooted, 1)


def layer0_finish(K):
    nc = K.nc
    with Phase(K, "l0f") as ph:
        res = ph.sb("res", [P, NT, D])
        feat = ph.sb("feat", [P, NT, 97])
        b2 = ph.sb("b2", [P, D])
        u0 = ph.sb("u0", [P, 1])
        m = ph.sb("m", [P, NT, 2])
        loaded = ph.sem("loaded")
        collect(K, K.by_src, K.sums0, D // 2, res)
        half = D // 2
        with nc.Block() as block:
            @block.sync
            def _(sp):
                sp.dma_start(b2[:, :], K.a["L0_gnn_b2"].unsqueeze(0).to_broadcast([P, D])).then_inc(loaded, 16)
                sp.dma_start(u0[:, :], K.a["L0_gnn_u"][0:1, :].to_broadcast([P, 1])).then_inc(loaded, 16)

            @block.vector
            def _(dve):
                v = nc.vector
                dve.wait_ge(loaded, 32)
                wide = lambda t, n: t.unsqueeze(2).to_broadcast([P, NT, n])
                v.tensor_scalar(m[:, :, 0], K.by_src.cnt[:, :], 1.0, None, ALU.max)
                v.tensor_scalar(m[:, :, 1], K.by_src.cnt[:, :], 0.0, None, ALU.is_gt)
                v.tensor_tensor(K.x[:, :, :], K.x[:, :, :], b2[:, :].unsqueeze(1).to_broadcast([P, NT, D]), ALU.add)
                v.drain()
                v.reciprocal(m[:, :, 0], m[:, :, 0])
                v.tensor_tensor(feat[:, :, 0:half], res[:, :, 0:half], wide(m[:, :, 1], half), ALU.mult)
                v.tensor_tensor(feat[:, :, half:D], res[:, :, half:D], wide(m[:, :, 1], half), ALU.mult)
                v.tensor_copy(feat[:, :, 96], u0[:, 0:1].to_broadcast([P, NT]))
                v.drain()
                v.tensor_tensor(feat[:, :, D:96], feat[:, :, 0:half], wide(m[:, :, 0], half), ALU.mult)

        def put(v, w, ps):
            return v.tensor_tensor(K.x[:, w, :], K.x[:, w, :], ps, ALU.add)
        node_dense(K, "l0m", feat, 97, K.a["L0_gnn_W1"], 128, ACT.Relu, K.a["L0_gnn_b1"], K.a["L0_gnn_W2"], put)
    normalise(K, "n1")
    with Phase(K, "t1") as ph:
        W = ph.sb("W", [D, H, D])
        at = ph.sb("at", [D, 2, H, D])
        V = ph.sb("V", [D, 2 * H])
        pr = ph.sb("pr", [D, 2, H, D])
        tab = ph.sb("tab", [P, NT, R1])
        loaded, stored = ph.sems("loaded", "stored")
        with nc.Block() as block:
            @block.sync
            def _(sp):
                sp.dma_start(W[:, :, :], K.a["L1_gnn_W"].rearrange("k (h c) -> k h c", h=H)).then_inc(loaded, 16)
                for i, n in enumerate(("L1_gnn_att_src", "L1_gnn_att_dst")):
                    sp.dma_start(at[:, i], K.a[n].unsqueeze(0).to_broadcast([D, H, D])).then_inc(loaded, 16)

            @block.vector
            def _(dve):
                v = nc.vector
                v.tensor_copy(tab[:, :, 0:D], K.hn[:, :, :])
                v.memset(tab[:, :, D:D + 1], 1.0)
                v.memset(tab[:, :, D + 17:], 0.0)
                dve.wait_ge(loaded, 48)
                for i in range(2):
                    v.tensor_tensor(pr[:, i], at[:, i], W[:, :, :], ALU.mult)
                v.drain()
                for i in range(2):
                    v.tensor_reduce(V[:, i * H:(i + 1) * H], pr[:, i], AX.X, ALU.add)

        def put(v, w, ps):
            return v.tensor_copy(tab[:, w, D + 1:D + 17], ps)
        node_dense(K, "t1m", K.hn, D, None, 2 * H, None, None, None, put, w1d=V)
        store_table(K, K.tab1, tab)


def store_table(K, table, tab):
    nc = K.nc
    with Phase(K, "st" + table.tensor.name) as ph:
        stored = ph.sem("stored")
        with nc.Block() as block:
            @block.sync
            def _(sp):
                sp.dma_start(table.rearrange("(w p) r -> p w r", p=P), tab[:, :, :]).then_inc(stored, 16)
                sp.wait_ge(stored, 16)


def edge_pass(K):
    nc = K.nc
    GRP = 4
    with Phase(K, "ep") as ph:
        ring = Ring(ph, RE, I32)
        proj = ph.sb("proj", [P, RING, TB, D])
        wm = ph.sb("wm", [D, D])
        b1 = ph.sb("b1", [P, D])
        at = ph.sb("at", [D, 2, GRP * P])
        srcs = ph.sb("srcs", [P, J], I32)
        pt = [ph.ps(f"pt{i}") for i in range(2)]
        pu = [ph.ps(f"pu{i}") for i in range(2)]
        loaded, turned, moved, times, added, srcst = ph.sems("loaded", "turned", "moved", "times", "added", "srcst")
        kept = [ph.sem(f"kept{s}") for s in range(RING)]
        read = [ph.sem(f"read{s}") for s in range(RING)]
        projd = [ph.sem(f"projd{s}") for s in range(RING)]
        stored = [ph.sem(f"stored{s}") for s in range(RING)]
        G = TB // GRP
        with nc.Block() as block:
            @block.gpsimd
            def _(pool):
                gather_rounds(nc, pool, ring, K.a["rec_d"], [(kept, 1), (read, 1)])

            @block.sync
            def _(sp):
                sp.dma_start(wm[:, :], K.a["L2_gnn_W1_msg"][0:D, :]).then_inc(loaded, 16)
                sp.dma_start(b1[:, :], K.a["L2_gnn_b1_msg"].unsqueeze(0).to_broadcast([P, D])).then_inc(loaded, 16)

                def store(it, s):
                    sp.dma_start(K.edgeu[:, block_cols(it, s), :], proj[:, s]).then_inc(stored[s], 16)

                def body(it, first):
                    for s in range(RING):
                        load_idx(sp, ring, K.by_dst.idx, it, s, first)
                        if not first:
                            sp.wait_ge(projd[s], it)
                            store(it - 1, s)
                rounds(sp, body)
                for s in range(RING):
                    sp.wait_ge(projd[s], NBLK // RING)
                    store(NBLK // RING - 1, s)
                for s in range(RING):
                    sp.wait_ge(stored[s], NBLK // RING * 16)

            @block.tensor
            def _(pe):
                pe.wait_ge(loaded, 32)

                def body(it, first):
                    for s in range(RING):
                        pe.wait_ge(ring.gathered[s], (it + 1) * TB * 16)
                        r = ring.rows[:, s].bitcast(F32)
                        base = (it * RING + s) * G
                        for g in range(G + 1):
                            if g < G:
                                if not first or s or g >= 2:
                                    pe.wait_ge(moved, base + g - 1)
                                for k in range(GRP):
                                    last = nc.tensor.transpose(pt[(s * G + g) % 2][0:RE, k * P:(k + 1) * P], r[:, GRP * g + k, :], K.ident[:, :])
                                last.then_inc(turned, 1)
                            if g >= 1:
                                u = g - 1
                                pe.wait_ge(moved, base + u + 1)
                                if not first or s or u >= 2:
                                    pe.wait_ge(added, base + u - 1)
                                for k in range(GRP):
                                    last = nc.tensor.matmul(pu[(s * G + u) % 2][:, k * D:(k + 1) * D],
                                                            at[:, (s * G + u) % 2, k * P:(k + 1) * P], wm[:, :], start=True, stop=True)
                                last.then_inc(times, 1)
                rounds(pe, body)

            @block.scalar
            def _(act):
                def body(it, first):
                    for s in range(RING):
                        base = (it * RING + s) * G
                        act.wait_ge(ring.gathered[s], (it + 1) * TB * 16)
                        nc.scalar.copy(srcs[:, block_cols(it, s)], ring.rows[:, s, :, D]).then_inc(kept[s], 1)
                        for g in range(G):
                            act.wait_ge(turned, base + g + 1)
                            if not first or s or g >= 2:
                                act.wait_ge(times, base + g - 1)
                            nc.scalar.copy(at[:, (s * G + g) % 2, :], pt[(s * G + g) % 2][0:D, :]).then_inc(moved, 1)
                        act.wait_ge(moved, base + G)
                        nc.scalar.copy(srcs[:, 0:1], srcs[:, 0:1]).then_inc(read[s], 1)
                rounds(act, body)
                act.wait_ge(read[1], NBLK // RING)
                act.dma_start(K.srcd.rearrange("(p j) -> p j", p=P), srcs[:, :]).then_inc(srcst, 16)
                act.wait_ge(srcst, 16)

            @block.vector
            def _(dve):
                v = nc.vector
                dve.wait_ge(loaded, 32)

                def body(it, first):
                    for s in range(RING):
                        base = (it * RING + s) * G
                        if not first:
                            dve.wait_ge(stored[s], it * 16)
                        for g in range(G):
                            dve.wait_ge(times, base + g + 1)
                            v.tensor_tensor(proj[:, s, GRP * g:GRP * (g + 1), :],
                                            pu[(s * G + g) % 2][:, 0:2 * P].rearrange("p (t d) -> p t d", d=D),
                                            b1[:, :].unsqueeze(1).to_broadcast([P, GRP, D]), ALU.add).then_inc(added, 1)
                        v.drain().then_inc(projd[s], 1)
                rounds(dve, body)


def src_to_tiles(K):
    nc = K.nc
    with Phase(K, "s2t") as ph:
        keyc = ph.sb("keyc", [CP, SORT_W], I32)
        nodei = ph.sb("nodei", [CP, SORT_W], I32)
        srci = ph.sb("srci", [CP, SORT_W], I32)
        srcf = ph.sb("srcf", [CP, SORT_W])
        nxt = ph.sb("nxt", [CP, 1], I32)
        t = ph.sb("t", [CP, SORT_W])
        c = ph.sb("c", [CP, 4])
        srct = ph.sb("srct", [P, J], I32)
        tp = ph.ps("tp")
        loaded, ready, turned, done, stored = ph.sems("loaded", "ready", "turned", "done", "stored")
        with nc.Block() as block:
            @block.sync
            def _(sp):
                kd = K.by_dst.key
                sp.dma_start(keyc[:, :], kd[0:L].rearrange("(p j) -> p j", p=CP)).then_inc(loaded, 16)
                sp.dma_start(srci[:, :], K.srcd.rearrange("(p j) -> p j", p=CP)).then_inc(loaded, 16)
                with nc.allow_non_contiguous_dma(reason="one value per partition"):
                    sp.dma_start(nxt[:, :], kd[SORT_W:SORT_W + L].rearrange("(p j) -> p j", p=CP)[:, 0:1]).then_inc(loaded, 16)
                sp.wait_ge(done, 1)
                sp.dma_start(K.idxtp, srct[:, :]).then_inc(stored, 16)
                sp.wait_ge(stored, 16)

            @block.vector
            def _(dve):
                v = nc.vector
                dve.wait_ge(loaded, 48)
                v.tensor_scalar(nodei[:, :], keyc[:, :], 16, None, ALU.logical_shift_right)
                v.tensor_scalar(keyc[:, :], keyc[:, :], 0xFFFF, None, ALU.bitwise_and)
                v.tensor_scalar(nxt[:, :], nxt[:, :], 0xFFFF, None, ALU.bitwise_and)
                v.tensor_copy(srcf[:, :], srci[:, :])
                v.drain()
                v.tensor_copy(K.nodec[:, :], nodei[:, :])
                v.drain().then_inc(ready, 1)
                v.tensor_scalar(t[:, :], keyc[:, :], float(N), None, ALU.is_ge)
                v.tensor_scalar(K.keepc[:, :], keyc[:, :], float(M), None, ALU.is_lt)
                v.tensor_scalar(c[:, 0:1], nxt[:, :], float(N), None, ALU.is_ge)
                v.tensor_scalar(c[:, 1:2], nxt[:, :], float(M), None, ALU.is_lt)
                v.tensor_tensor(c[:, 2:3], K.nodec[:, 0:1], K.nodec[:, SORT_W - 1:], ALU.is_equal)
                v.tensor_copy(K.node0c[:, :], nodei[:, 0:1])
                v.drain()
                v.tensor_tensor(K.keepc[:, :], K.keepc[:, :], t[:, :], ALU.mult)
                v.tensor_tensor(K.nxc[:, :], c[:, 0:1], c[:, 1:2], ALU.mult)
                v.drain()
                v.tensor_tensor(K.nmc[:, 0:1], K.keepc[:, 0:1], c[:, 2:3], ALU.mult)
                v.tensor_tensor(K.nmc[:, 1:2], K.nxc[:, :], c[:, 2:3], ALU.mult)
                dve.wait_ge(turned, 1)
                v.tensor_copy(srct[:, :].rearrange("q (p g) -> q g p", g=4),
                              tp[:, :].rearrange("q (g p) -> q g p", g=4)[:, :, 0:CP])
                v.drain().then_inc(done, 1)

            @block.tensor
            def _(pe):
                pe.wait_ge(ready, 1)
                for g in range(4):
                    last = nc.tensor.transpose(tp[:, g * P:g * P + CP], srcf[:, g * P:(g + 1) * P], K.ident[0:CP, 0:CP])
                last.then_inc(turned, 1)


def layer1_gather(K):
    nc = K.nc
    with Phase(K, "l1g") as ph:
        ring = Ring(ph, R1)
        kept = [ph.sem(f"kept{s}") for s in range(RING)]
        stored = [ph.sem(f"stored{s}") for s in range(RING)]
        with nc.Block() as block:
            @block.gpsimd
            def _(pool):
                gather_rounds(nc, pool, ring, K.tab1, [(kept, 1), (stored, 16)])

            @block.sync
            def _(sp):
                def body(it, first):
                    for s in range(RING):
                        load_idx(sp, ring, K.idxtp, it, s, first)
                rounds(sp, body)

            @block.scalar
            def _(act):
                def body(it, first):
                    for s in range(RING):
                        act.wait_ge(ring.gathered[s], (it + 1) * TB * 16)
                        act.dma_start(K.g1[:, block_cols(it, s), :], ring.rows[:, s, :, 0:D + 1]).then_inc(stored[s], 16)
                        nc.scalar.copy(K.atp[:, block_cols(it, s), :], ring.rows[:, s, :, D + 1:D + 17]).then_inc(kept[s], 1)
                rounds(act, body)
                for s in range(RING):
                    act.wait_ge(stored[s], NBLK // RING * 16)


def layer1_softmax(K):
    nc = K.nc
    W = SORT_W
    with Phase(K, "l1s") as ph:
        A = ph.sb("A", [CP, 2 * H, W])
        F = K.F
        first = ph.sb("first", [P, R1])
        mk = ph.sb("mk", [CP, W])
        mb = ph.sb("mb", [CP, W])
        mr = ph.sb("mr", [CP, W])
        nmb = ph.sb("nmb", [CP, 2, H])
        nmt = ph.sb("nmt", [H, 2, CP])
        last = ph.sb("last", [CP, H])
        tot = ph.sb("tot", [H, CP])
        shf = ph.sb("shf", [H, CP])
        ini = ph.sb("ini", [CP, 2, H])
        bank = [ph.ps(f"bank{i}") for i in range(4)]
        small = ph.ps("small")
        turned, moved, got, made, crossed, ready, expd = ph.sems(
            "turned", "moved", "got", "made", "crossed", "ready", "expd")
        with nc.Block() as block:
            @block.gpsimd
            def _(pool):
                nc.gpsimd.indirect_dma_start(out=first[0:CP, :], out_offset=None, in_=K.tab1,
                                             in_offset=bass.IndirectOffsetOnAxis(ap=K.node0c[:, 0:1], axis=0)).then_inc(got, 16)

            @block.tensor
            def _(pe):
                for r in range(2 * H):
                    if r >= 4:
                        pe.wait_ge(moved, r - 3)
                    for g in range(4):
                        lt = nc.tensor.transpose(bank[r % 4][0:CP, g * P:(g + 1) * P], K.atp[:, g::4, r], K.ident[:, :])
                    lt.then_inc(turned, 1)
                pe.wait_ge(made, 1)
                for i in range(2):
                    nc.tensor.matmul(small[0:H, i * P:i * P + CP], nmb[:, i, :], K.ident[0:CP, 0:CP], start=True, stop=True)
                nc.tensor.transpose(small[0:H, 2 * P:2 * P + CP], last[:, :], K.ident[0:CP, 0:CP]).then_inc(crossed, 1)
                pe.wait_ge(made, 2)
                nc.tensor.transpose(small[0:CP, 3 * P:3 * P + H], shf[:, :], K.ident[0:H, 0:H]).then_inc(crossed, 1)
                pe.wait_ge(made, 3)
                nc.tensor.transpose(small[0:H, 2 * P:2 * P + CP], last[:, :], K.ident[0:CP, 0:CP]).then_inc(crossed, 1)
                pe.wait_ge(made, 4)
                nc.tensor.transpose(small[0:CP, 3 * P:3 * P + H], shf[:, :], K.ident[0:H, 0:H]).then_inc(crossed, 1)

            @block.scalar
            def _(act):
                for r in range(2 * H):
                    act.wait_ge(turned, r + 1)
                    nc.scalar.copy(A[:, r, :], bank[r % 4][0:CP, :]).then_inc(moved, 1)
                for h in range(H):
                    act.wait_ge(ready, h + 1)
                    nc.scalar.activation(F[:, h, :], F[:, h, :], ACT.Exp).then_inc(expd, 1)

            @block.vector
            def _(dve):
                v = nc.vector
                v.tensor_scalar(mk[:, :], K.keepc[:, :], -1.0, 1.0, ALU.mult, ALU.add)
                v.tensor_scalar(mb[:, :], K.keepc[:, :], 2.0, -1.0, ALU.mult, ALU.add)
                v.tensor_copy(nmb[:, :, :], K.nmc[:, :].unsqueeze(2).to_broadcast([CP, 2, H]))
                v.tensor_scalar(mr[:, W - 1:], K.nxc[:, :], 2.0, -1.0, ALU.mult, ALU.add)
                v.drain()
                v.tensor_scalar(mb[:, :], mb[:, :], BIG, None, ALU.mult)
                v.drain()
                v.tensor_copy(mr[:, 0:W - 1], mb[:, 1:W])
                v.tensor_scalar(mr[:, W - 1:], mr[:, W - 1:], BIG, None, ALU.mult)
                dve.wait_ge(moved, 2 * H)
                dve.wait_ge(got, 16)
                v.tensor_tensor(A[:, H:, :], A[:, H:, :], mk[:, :].unsqueeze(1).to_broadcast([CP, H, W]), ALU.mult)
                v.drain()
                for h in range(H):
                    v.tensor_tensor_scan(A[:, H + h, :], K.keepc[:, :], A[:, H + h, :], first[0:CP, D + 9 + h:D + 10 + h], ALU.mult, ALU.add)
                v.drain()
                v.tensor_tensor(A[:, 0:H, :], A[:, 0:H, :], A[:, H:, :], ALU.add)
                v.drain()
                v.scalar_tensor_tensor(A[:, 0:H, :], A[:, 0:H, :], 0.2, A[:, 0:H, :], ALU.mult, ALU.max)
                v.drain()
                for h in range(H):
                    v.tensor_tensor_scan(F[:, h, :], mb[:, :], A[:, h, :], -BIG, ALU.min, ALU.max)
                v.drain()
                v.tensor_copy(last[:, :], F[:, :, W - 1])
                v.drain().then_inc(made, 1)
                dve.wait_ge(crossed, 1)
                for i in range(2):
                    v.tensor_scalar(nmt[:, i, :], small[0:H, i * P:i * P + CP], 2.0, -1.0, ALU.mult, ALU.add)
                v.drain()
                v.tensor_scalar(nmt[:, :, :], nmt[:, :, :], BIG, None, ALU.mult)
                v.drain()
                v.tensor_tensor_scan(tot[:, :], nmt[:, 0, :], small[0:H, 2 * P:2 * P + CP], -BIG, ALU.min, ALU.max)
                v.memset(shf[:, 0:1], -BIG)
                v.drain()
                v.tensor_copy(shf[:, 1:CP], tot[:, 0:CP - 1])
                v.drain().then_inc(made, 1)
                dve.wait_ge(crossed, 2)
                v.tensor_copy(ini[:, 0, :], small[0:CP, 3 * P:3 * P + H])
                v.drain()
                for h in range(H):
                    v.tensor_tensor_scan(A[:, H + h, :], mb[:, :], A[:, h, :], ini[:, 0, h:h + 1], ALU.min, ALU.max)
                v.drain()
                for h in range(H):
                    v.tensor_tensor_scan(F[:, h, ::-1], mr[:, ::-1], A[:, H + h, ::-1], -BIG, ALU.min, ALU.max)
                v.drain()
                v.tensor_copy(last[:, :], F[:, :, 0])
                v.drain().then_inc(made, 1)
                dve.wait_ge(crossed, 3)
                v.tensor_tensor_scan(tot[:, ::-1], nmt[:, 1, ::-1], small[0:H, 2 * P:2 * P + CP][:, ::-1], -BIG, ALU.min, ALU.max)
                v.memset(shf[:, CP - 1:], -BIG)
                v.drain()
                v.tensor_copy(shf[:, 0:CP - 1], tot[:, 1:CP])
                v.drain().then_inc(made, 1)
                dve.wait_ge(crossed, 4)
                v.tensor_copy(ini[:, 1, :], small[0:CP, 3 * P:3 * P + H])
                v.drain()
                for h in range(H):
                    v.tensor_tensor_scan(F[:, h, ::-1], mr[:, ::-1], A[:, H + h, ::-1], ini[:, 1, h:h + 1], ALU.min, ALU.max)
                v.drain()
                for h in range(H):
                    v.tensor_tensor(F[:, h, :], A[:, h, :], F[:, h, :], ALU.subtract).then_inc(ready, 1)


def layer1_items(K):
    nc = K.nc
    HI = ITEMS // 2
    with Phase(K, "l1i") as ph:
        wst = ph.sb("wst", [P, 2])
        wsi = ph.sb("wsi", [P, 2], I32)
        widx = ph.sb("widx", [P, 2])
        kio = ph.sb("kio", [P, ITEMS])
        cmp = ph.sb("cmp", [P, 2, ITEMS])
        ones = ph.sb("ones", [P, P])
        wa = ph.sb("wa", [P, ITEMS])
        ta = ph.sb("ta", [P, ITEMS])
        first = ph.sb("first", [1, BODIES])
        slot = ph.sb("slot", [1, ITEMS])
        tile_no = ph.sb("tile_no", [P, 4])
        sel = ph.sb("sel", [P, 4, ITEMS])
        count = [ph.ps(f"count{i}") for i in range(2)]
        bank = [ph.ps(f"bank{i}") for i in range(4)]
        far, consts, loaded, compared, counted, selected, spread, placed, kept = ph.sems(
            "far", "consts", "loaded", "compared", "counted", "selected", "spread", "placed", "kept")
        with nc.Block() as block:
            @block.gpsimd
            def _(pool):
                small = dict(allow_small_or_imprecise_dtypes=True)
                nc.gpsimd.iota(widx[:, :], [[P, 2]], base=1, channel_multiplier=1, **small)
                nc.gpsimd.iota(tile_no[:, :], [[1, 4]], base=0, channel_multiplier=4, **small)
                nc.gpsimd.iota(K.iota16[:, :], [[1, WIN]], base=0, channel_multiplier=0, **small)
                nc.gpsimd.iota(kio[:, :], [[1, ITEMS]], base=0, channel_multiplier=0, **small).then_inc(consts, 1)

            @block.sync
            def _(sp):
                st = K.by_dst.startd.rearrange("(w s) -> w s", s=WIN)
                sp.wait_ge(far, 1)
                with nc.allow_non_contiguous_dma(reason="one value per window"):
                    sp.dma_start(wst[:, 0:1], st[1:1 + P, 0:1]).then_inc(loaded, 16)
                    sp.dma_start(wst[0:NWIN - 1 - P, 1:2], st[1 + P:NWIN, 0:1]).then_inc(loaded, 16)

            @block.vector
            def _(dve):
                v = nc.vector
                v.memset(ones[:, :], 1.0)
                v.memset(wst[:, :], float(4 * ITEMS * P))
                v.drain().then_inc(far, 1)
                for i in range(4):
                    v.memset(K.acc[:, i * ACC_W // 4:(i + 1) * ACC_W // 4, :], 0.0)
                dve.wait_ge(consts, 1)
                dve.wait_ge(loaded, 32)
                v.tensor_copy(wsi[:, :], wst[:, :])
                v.drain()
                v.tensor_scalar(wsi[:, :], wsi[:, :], 7, None, ALU.logical_shift_right)
                v.drain()
                v.tensor_copy(wst[:, :], wsi[:, :])
                v.drain()
                v.tensor_scalar(wst[:, 0:1], wst[:, 0:1], float(J - 1), None, ALU.min)
                v.tensor_scalar(wst[0:NWIN - 1 - P, 1:2], wst[0:NWIN - 1 - P, 1:2], float(J - 1), None, ALU.min)
                v.drain()
                v.tensor_tensor(wst[:, :], wst[:, :], widx[:, :], ALU.add)
                v.drain()
                for i in range(2):
                    v.tensor_scalar(cmp[:, i, :], kio[:, :], wst[:, i:i + 1], None, ALU.is_ge)
                v.drain().then_inc(compared, 1)
                dve.wait_ge(counted, 1)
                for i in range(2):
                    v.tensor_copy(wa[:, i * HI:(i + 1) * HI], count[i][:, 0:HI])
                v.drain()
                v.tensor_tensor(ta[:, :], kio[:, :], wa[:, :], ALU.subtract)
                v.drain()
                v.memset(wa[:, J + NWIN - 1:], float(NWIN))
                v.memset(ta[:, J + NWIN - 1:], float(J - 1))
                v.drain()
                for g in range(4):
                    v.tensor_scalar(sel[:, g, :], ta[:, :], tile_no[:, g:g + 1], None, ALU.is_equal)
                v.drain().then_inc(selected, 1)
                v.tensor_scalar(first[:, :], ta[0:1, ::IB], float(J - IB), None, ALU.min)
                v.tensor_copy(K.item_w[:, :], wa[0:1, :])
                v.drain()
                v.tensor_tensor(slot[:, :].rearrange("p (b i) -> p b i", i=IB), ta[0:1, :].rearrange("p (b i) -> p b i", i=IB),
                                first[:, :].unsqueeze(2).to_broadcast([1, BODIES, IB]), ALU.subtract)
                v.tensor_copy(K.item_first[:, :], first[:, :])
                v.drain()
                v.tensor_copy(K.item_slot[:, :], slot[:, :])
                for i in range(2):
                    dve.wait_ge(spread, i + 1)
                    hs = slice(i * HI, (i + 1) * HI)
                    v.scalar_tensor_tensor(K.item_rel[:, hs], wa[:, hs], -float(WIN), bank[i][:, 0:HI], ALU.mult, ALU.add).then_inc(placed, 1)

            @block.tensor
            def _(pe):
                pe.wait_ge(compared, 1)
                for i in range(2):
                    for c in range(2):
                        lt = nc.tensor.matmul(count[i][:, 0:HI], ones[:, :], cmp[:, c, i * HI:(i + 1) * HI], start=(c == 0), stop=(c == 1))
                lt.then_inc(counted, 1)
                pe.wait_ge(selected, 1)
                for n in range(2 * (H + 1)):
                    f, i = n // 2, n % 2
                    if n in (4, 5):
                        pe.wait_ge(placed, n - 3)
                    if n >= 6:
                        pe.wait_ge(kept, n - 5)
                    for g in range(4):
                        src = K.nodec[:, g * P:(g + 1) * P] if f == 0 else K.F[:, f - 1, g * P:(g + 1) * P]
                        lt = nc.tensor.matmul(bank[n % 4][:, 0:HI], src, sel[0:CP, g, i * HI:(i + 1) * HI], start=(g == 0), stop=(g == 3))
                    lt.then_inc(spread, 1)

            @block.scalar
            def _(act):
                for n in range(2, 2 * (H + 1)):
                    f, i = n // 2, n % 2
                    act.wait_ge(spread, n + 1)
                    nc.scalar.copy(K.item_ex[:, f - 1, i * HI:(i + 1) * HI], bank[n % 4][:, 0:HI]).then_inc(kept, 1)


def layer1_sums(K):
    nc = K.nc
    with Phase(K, "l1a") as ph:
        g = ph.sb("g", [P, 2, IB, D + 1])
        place = ph.sb("place", [P, 2, IB, WIN])
        wt = ph.sb("wt", [P, 2, IB, H, WIN])
        pa = [[ph.ps(f"pa{b}{i}") for i in range(2)] for b in range(2)]
        fetched = [ph.sem(f"fetched{b}") for b in range(2)]
        weighed, multiplied, added, settled = ph.sems("weighed", "multiplied", "added", "settled")
        part = lambda b, u: pa[b][u // 7][:, u % 7 * (D + 1):(u % 7 + 1) * (D + 1)]
        with nc.Block() as block:
            @block.sync
            def _(sp):
                def body(it, first):
                    for b in range(2):
                        n = it * 2 + b
                        t, = values(nc, K.item_first[0:1, bass.ds(n, 1)], mybir.EngineType.SP, J - IB)
                        if not first:
                            sp.wait_ge(multiplied, n - 1)
                        sp.dma_start(g[:, b], K.g1[:, bass.ds(t, IB), :]).then_inc(fetched[b], 16)
                rounds(sp, body, BODIES // 2)

            @block.tensor
            def _(pe):
                def body(it, first):
                    for b in range(2):
                        n = it * 2 + b
                        slots = values(nc, K.item_slot[0:1, bass.ds(n * IB, IB)], mybir.EngineType.PE, IB - 1)
                        pe.wait_ge(weighed, n + 1)
                        pe.wait_ge(fetched[b], (it + 1) * 16)
                        if not first:
                            pe.wait_ge(added, n - 1)
                        for u in range(IB):
                            lt = nc.tensor.matmul(part(b, u), wt[:, b, u].rearrange("p h s -> p (h s)"),
                                                  g[:, b, bass.ds(slots[u], 1), :].rearrange("p o d -> p (o d)"), start=True, stop=True)
                        lt.then_inc(multiplied, 1)
                rounds(pe, body, BODIES // 2)

            @block.vector
            def _(dve):
                v = nc.vector

                def weigh(n, b):
                    v.tensor_tensor(place[:, b], K.iota16[:, :].unsqueeze(1).to_broadcast([P, IB, WIN]),
                                    K.item_rel[:, bass.ds(n * IB, IB)].unsqueeze(2).to_broadcast([P, IB, WIN]), ALU.is_equal)
                    v.drain()
                    v.tensor_tensor(wt[:, b], place[:, b].unsqueeze(2).to_broadcast([P, IB, H, WIN]),
                                    K.item_ex[:, :, bass.ds(n * IB, IB)].rearrange("p h i -> p i h").unsqueeze(3).to_broadcast([P, IB, H, WIN]),
                                    ALU.mult).then_inc(weighed, 1)

                def add(n, b):
                    windows = values(nc, K.item_w[0:1, bass.ds(n * IB, IB)], mybir.EngineType.DVE, NWIN)
                    dve.wait_ge(multiplied, n + 1)
                    for u in range(IB):
                        dst = K.acc[:, bass.ds(windows[u], 1), :].rearrange("p o d -> p (o d)")
                        v.tensor_tensor(dst, dst, part(b, u), ALU.add)
                        v.drain()
                    v.sem_inc(added, 1)

                weigh(0, 0)
                weigh(1, 1)
                with dve.Fori(1, BODIES // 2) as it:
                    for b in range(2):
                        add(it * 2 + b - 2, b)
                        weigh(it * 2 + b, b)
                for b in range(2):
                    add(BODIES - 2 + b, b)


def values(nc, ap, engine, most):
    return nc.values_load_multi_w_load_instructions(ap, engines=[engine], min_val=0, max_val=most,
                                                    skip_runtime_bounds_check_because="the table is clamped where it is made")[1]


def layer1_finish(K):
    nc = K.nc
    with Phase(K, "l1f") as ph:
        rec = ph.sb("rec", [P, ACC_W])
        bias = ph.sb("bias", [P, D])
        W = ph.sb("W", [D, H * D])
        nrm = ph.sb("nrm", [P, 2, H, D])
        at = ph.sb("at", [D, 2, H, 8, WIN])
        pt = [[ph.ps(f"pt{i}{j}") for j in range(2)] for i in range(2)]
        po = [ph.ps(f"po{i}") for i in range(2)]
        loaded, scaled, turned, moved, times, added = ph.sems("loaded", "scaled", "turned", "moved", "times", "added")
        with nc.Block() as block:
            @block.sync
            def _(sp):
                sp.dma_start(bias[:, :], K.a["L1_gnn_bias"].unsqueeze(0).to_broadcast([P, D])).then_inc(loaded, 16)
                sp.dma_start(W[:, :], K.a["L1_gnn_W"]).then_inc(loaded, 16)
                sp.wait_ge(loaded, 32)

            @block.vector
            def _(dve):
                v = nc.vector
                dve.wait_ge(loaded, 32)
                v.tensor_scalar(rec[:, :], K.acc[:, :, D], 1e-30, None, ALU.max)
                v.tensor_tensor(K.x[:, :, :], K.x[:, :, :], bias[:, :].unsqueeze(1).to_broadcast([P, NT, D]), ALU.add)
                v.drain()
                v.reciprocal(rec[:, :], rec[:, :])
                v.drain()
                for w in range(NT + 1):
                    if w < NT:
                        if w >= 2:
                            dve.wait_ge(turned, w - 1)
                        v.tensor_tensor(nrm[:, w % 2], K.acc[:, 8 * w:8 * w + 8, 0:D],
                                        rec[:, 8 * w:8 * w + 8].unsqueeze(2).to_broadcast([P, 8, D]), ALU.mult).then_inc(scaled, 1)
                    if w >= 1:
                        u = w - 1
                        dve.wait_ge(times, u + 1)
                        v.scalar_tensor_tensor(K.x[:, u, :], po[u % 2][:, 0:D], 1.0 / H, K.x[:, u, :], ALU.mult, ALU.add).then_inc(added, 1)

            @block.tensor
            def _(pe):
                pe.wait_ge(loaded, 32)
                for w in range(NT + 1):
                    if w < NT:
                        pe.wait_ge(scaled, w + 1)
                        if w >= 2:
                            pe.wait_ge(moved, 2 * (w - 1))
                        for m in range(8):
                            lt = nc.tensor.transpose(pt[w % 2][m // 4][0:D, m % 4 * P:(m % 4 + 1) * P], nrm[:, w % 2, m, :], K.ident[:, :])
                        lt.then_inc(turned, 1)
                    if w >= 1:
                        u = w - 1
                        pe.wait_ge(moved, 2 * (u + 1))
                        if u >= 2:
                            pe.wait_ge(added, u - 1)
                        for h in range(H):
                            lt = nc.tensor.matmul(po[u % 2][:, 0:D],
                                                  at[:, u % 2, h].rearrange("c m s -> c (m s)"),
                                                  W[:, h * D:(h + 1) * D], start=(h == 0), stop=(h == H - 1))
                        lt.then_inc(times, 1)

            @block.scalar
            def _(act):
                for w in range(NT):
                    act.wait_ge(turned, w + 1)
                    if w >= 2:
                        act.wait_ge(times, w - 1)
                    for i in range(2):
                        nc.scalar.copy(at[:, w % 2, :, 4 * i:4 * i + 4, :],
                                       pt[w % 2][i][0:D, :].rearrange("c (m h s) -> c h m s", m=4, h=H)).then_inc(moved, 1)


def layer2_gather(K):
    nc = K.nc
    normalise(K, "n2")
    with Phase(K, "t2") as ph:
        W = ph.sb("W", [D, R2])
        tab = ph.sb("tab", [P, NT, R2])
        loaded = ph.sem("loaded")
        with nc.Block() as block:
            @block.sync
            def _(sp):
                sp.dma_start(W[:, :].rearrange("k (i d) -> k i d", i=2),
                             K.a["L2_gnn_W1_msg"][D:3 * D, :].rearrange("(i k) d -> k i d", i=2)).then_inc(loaded, 16)
                sp.wait_ge(loaded, 16)
        node_dense(K, "t2m", K.hn, D, None, R2, None, None, None,
                   lambda v, w, ps: v.tensor_copy(tab[:, w, :], ps), w1d=W)
        store_table(K, K.tab2, tab)
    with Phase(K, "l2g") as ph:
        ring = Ring(ph, R2)
        u = ph.sb("u", [P, RING, TB, D])
        sums = ph.sb("sums", [P, RING, TB, D])
        first = ph.sb("first", [P, R2])
        q = ph.sb("q", [P, D])
        fidx = ph.sb("fidx", [P, 1], I32)
        kb = ph.sb("kb", [P, TB])
        mk = ph.sb("mk", [P, TB])
        idxed, got = ph.sems("idxed", "got")
        fetched, mixed, acted, scanned, freed, stored = (
            [ph.sem(f"{n}{s}") for s in range(RING)] for n in ("fetched", "mixed", "acted", "scanned", "freed", "stored"))
        out = K.sums2.rearrange("(p j) d -> p j d", p=P)
        with nc.Block() as block:
            @block.gpsimd
            def _(pool):
                pool.wait_ge(idxed, 1)
                nc.gpsimd.indirect_dma_start(out=first[:, :], out_offset=None, in_=K.tab2,
                                             in_offset=bass.IndirectOffsetOnAxis(ap=fidx[:, 0:1], axis=0)).then_inc(got, 16)
                gather_rounds(nc, pool, ring, K.tab2, [(freed, 1)])

            @block.sync
            def _(sp):
                idx = K.srcd.rearrange("(p j) -> p j", p=P)

                def body(it, isfirst):
                    for s in range(RING):
                        load_idx(sp, ring, idx, it, s, isfirst)
                        if not isfirst:
                            sp.wait_ge(mixed[s], it)
                        sp.dma_start(u[:, s], K.edgeu[:, block_cols(it, s), :]).then_inc(fetched[s], 16)
                        if not isfirst:
                            sp.wait_ge(scanned[s], it)
                            sp.dma_start(out[:, block_cols(it - 1, s), :], sums[:, s]).then_inc(stored[s], 16)
                rounds(sp, body)
                for s in range(RING):
                    sp.wait_ge(scanned[s], NBLK // RING)
                    sp.dma_start(out[:, block_cols(NBLK // RING - 1, s), :], sums[:, s]).then_inc(stored[s], 16)
                for s in range(RING):
                    sp.wait_ge(stored[s], NBLK // RING * 16)

            @block.scalar
            def _(act):
                def body(it, isfirst):
                    for s in range(RING):
                        act.wait_ge(mixed[s], it + 1)
                        nc.scalar.activation(sums[:, s], sums[:, s], ACT.Silu).then_inc(acted[s], 1)
                rounds(act, body)

            @block.vector
            def _(dve):
                v = nc.vector
                v.memset(K.st[:, :], 0.0)
                v.tensor_copy(fidx[:, :], K.by_dst.node0[:, :])
                v.drain().then_inc(idxed, 1)
                dve.wait_ge(got, 16)
                v.tensor_copy(q[:, :], first[:, D:])

                def body(it, isfirst):
                    for s in range(RING):
                        r = ring.rows
                        seg_masks(v, K.by_dst.keep, block_cols(it, s), kb, mk=mk)
                        dve.wait_ge(ring.gathered[s], (it + 1) * TB * 16)
                        v.tensor_tensor(r[:, s, :, D:], r[:, s, :, D:], mk[:, :].unsqueeze(2).to_broadcast([P, TB, D]), ALU.mult)
                        dve.wait_ge(fetched[s], (it + 1) * 16)
                        v.tensor_tensor(r[:, s, :, 0:D], r[:, s, :, 0:D], u[:, s], ALU.add)
                        v.drain()
                        for f in range(D):
                            v.tensor_tensor_scan(r[:, s, :, D + f], kb[:, :], r[:, s, :, D + f], q[:, f:f + 1], ALU.mult, ALU.add)
                        v.drain()
                        if not isfirst:
                            dve.wait_ge(stored[s], it * 16)
                        v.tensor_tensor(sums[:, s], r[:, s, :, 0:D], r[:, s, :, D:], ALU.add)
                        v.tensor_copy(q[:, :], r[:, s, TB - 1, D:])
                        v.drain().then_inc(mixed[s], 1)
                        dve.wait_ge(acted[s], it + 1)
                        v.tensor_tensor(sums[:, s], sums[:, s], kb[:, :].unsqueeze(2).to_broadcast([P, TB, D]), ALU.mult).then_inc(freed[s], 1)
                        v.drain()
                        for f in range(D):
                            v.tensor_tensor_scan(sums[:, s, :, f], kb[:, :], sums[:, s, :, f], K.st[:, f:f + 1], ALU.mult, ALU.add)
                        v.drain().then_inc(scanned[s], 1)
                        v.tensor_copy(K.st[:, :], sums[:, s, TB - 1, :])
                rounds(dve, body)


def layer2_finish(K):
    nc = K.nc
    with Phase(K, "l2f") as ph:
        res = ph.sb("res", [P, NT, D])
        feat = ph.sb("feat", [P, NT, 2 * D])
        b2m = ph.sb("b2m", [P, D])
        b2u = ph.sb("b2u", [P, D])
        W2m = ph.sb("W2m", [D, D])
        r = ph.sb("r", [P, 2, NT])
        loaded = ph.sem("loaded")
        collect(K, K.by_dst, K.sums2, D, res)
        with nc.Block() as block:
            @block.sync
            def _(sp):
                for t, n in ((b2m, "L2_gnn_b2_msg"), (b2u, "L2_gnn_b2_upd")):
                    sp.dma_start(t[:, :], K.a[n].unsqueeze(0).to_broadcast([P, D])).then_inc(loaded, 16)
                sp.dma_start(W2m[:, :], K.a["L2_gnn_W2_msg"]).then_inc(loaded, 16)
                sp.wait_ge(loaded, 48)

            @block.vector
            def _(dve):
                v = nc.vector
                wide = lambda t, n: t.unsqueeze(2).to_broadcast([P, NT, n])
                row = lambda t: t[:, :].unsqueeze(1).to_broadcast([P, NT, D])
                dve.wait_ge(loaded, 48)
                v.tensor_scalar(r[:, 0], K.by_dst.cnt[:, :], 1e-6, None, ALU.add)
                v.tensor_scalar(r[:, 1], K.by_dst.cnt[:, :], 0.0, None, ALU.is_gt)
                v.tensor_tensor(K.x[:, :, :], K.x[:, :, :], row(b2u), ALU.add)
                v.tensor_copy(feat[:, :, 0:D], K.hn[:, :, :])
                v.drain()
                v.reciprocal(r[:, 0], r[:, 0])
                v.drain()
                v.tensor_tensor(r[:, 1], r[:, 1], r[:, 0], ALU.mult)
                v.tensor_tensor(r[:, 0], K.by_dst.cnt[:, :], r[:, 0], ALU.mult)
                v.drain()
                v.tensor_tensor(res[:, :, :], res[:, :, :], wide(r[:, 1], D), ALU.mult)
                v.tensor_tensor(feat[:, :, D:], row(b2m), wide(r[:, 0], D), ALU.mult)
        node_dense(K, "l2a", res, D, None, D, None, None, None,
                   lambda v, w, ps: v.tensor_tensor(feat[:, w, D:], feat[:, w, D:], ps, ALU.add), w1d=W2m)
        node_dense(K, "l2m", feat, 2 * D, K.a["L2_gnn_W1_upd"], D, ACT.Silu, K.a["L2_gnn_b1_upd"], K.a["L2_gnn_W2_upd"],
                   lambda v, w, ps: v.tensor_tensor(K.x[:, w, :], K.x[:, w, :], ps, ALU.add))


def layer3_gather(K):
    nc = K.nc
    normalise(K, "n3")
    C1 = D + 1
    with Phase(K, "t3") as ph:
        b = ph.sb("b", [P, D])
        W = ph.sb("W", [D, D])
        sq = ph.sb("sq", [P, NT, D])
        dstf = ph.sb("dstf", [P, J])
        dsti = ph.sb("dsti", [P, J], I32)
        y = ph.sb("y", [P, J])
        z = ph.sb("z", [P, J])
        co = ph.sb("co", [P, 8])
        loaded, d1, d2, a1, a2, a3 = ph.sems("loaded", "d1", "d2", "a1", "a2", "a3")
        with nc.Block() as block:
            @block.sync
            def _(sp):
                row = lambda n, k: K.a[n].unsqueeze(0).to_broadcast([P, k])
                sp.dma_start(b[:, :], row("L3_gnn_b", D)).then_inc(loaded, 16)
                sp.dma_start(W[:, :], K.a["L3_gnn_W"]).then_inc(loaded, 16)
                sp.dma_start(dsti[:, :], K.idxdst).then_inc(loaded, 16)
                sp.dma_start(co[:, 0:3], row("L3_gnn_coeff_param", 3)).then_inc(loaded, 16)
                sp.dma_start(co[:, 4:6], row("L3_gnn_deg_coeff", 2)).then_inc(loaded, 16)
                sp.dma_start(co[:, 6:7], row("L3_gnn_scale_param", 1)).then_inc(loaded, 16)
                sp.wait_ge(loaded, 96)

            @block.vector
            def _(dve):
                v = nc.vector
                dve.wait_ge(loaded, 96)
                meta = K.meta[:, :, :].bitcast(F32)
                v.tensor_copy(dstf[:, :], dsti[:, :])
                v.tensor_scalar(y[:, :], meta[:, :, 1], co[:, 4:5], co[:, 5:6], ALU.mult, ALU.add)
                v.tensor_copy(co[:, 7:8], co[:, 6:7])
                v.tensor_reduce(co[:, 3:4], co[:, 0:3], AX.X, ALU.max)
                v.drain()
                v.tensor_scalar(z[:, :], y[:, :], -1.0, None, ALU.mult)
                v.tensor_scalar(K.co[:, 4:5], co[:, 7:8], -1.0, None, ALU.mult)
                v.tensor_scalar(co[:, 0:3], co[:, 0:3], co[:, 3:4], None, ALU.subtract)
                v.drain()
                v.tensor_tensor(z[:, :], z[:, :], y[:, :], ALU.min)
                v.tensor_tensor(K.co[:, 4:5], K.co[:, 4:5], co[:, 7:8], ALU.min)
                v.drain().then_inc(d1, 1)
                dve.wait_ge(a1, 3)
                v.tensor_scalar(z[:, :], z[:, :], 1.0, None, ALU.add)
                v.tensor_scalar(K.co[:, 4:5], K.co[:, 4:5], 1.0, None, ALU.add)
                v.tensor_reduce(co[:, 3:4], co[:, 0:3], AX.X, ALU.add)
                v.drain().then_inc(d2, 1)
                v.reciprocal(co[:, 3:4], co[:, 3:4])
                v.tensor_scalar(y[:, :], y[:, :], 0.0, None, ALU.max)
                v.tensor_scalar(co[:, 7:8], co[:, 7:8], 0.0, None, ALU.max)
                v.tensor_tensor(dstf[:, :], dstf[:, :], K.nodes[:, :], ALU.not_equal)
                v.drain()
                v.tensor_scalar(K.co[:, 0:3], co[:, 0:3], co[:, 3:4], None, ALU.mult)
                v.tensor_tensor(dstf[:, :], dstf[:, :], meta[:, :, 0], ALU.mult)
                dve.wait_ge(a2, 2)
                v.tensor_tensor(y[:, :], y[:, :], z[:, :], ALU.add)
                v.tensor_tensor(K.co[:, 3:4], co[:, 7:8], K.co[:, 4:5], ALU.add)
                v.drain()
                v.tensor_tensor(K.base[:, :], dstf[:, :], y[:, :], ALU.mult)

            @block.scalar
            def _(act):
                act.wait_ge(d1, 1)
                nc.scalar.activation(z[:, :], z[:, :], ACT.Exp).then_inc(a1, 1)
                nc.scalar.activation(K.co[:, 4:5], K.co[:, 4:5], ACT.Exp).then_inc(a1, 1)
                nc.scalar.activation(co[:, 0:3], co[:, 0:3], ACT.Exp).then_inc(a1, 1)
                act.wait_ge(d2, 1)
                nc.scalar.activation(z[:, :], z[:, :], ACT.Ln).then_inc(a2, 1)
                nc.scalar.activation(K.co[:, 4:5], K.co[:, 4:5], ACT.Ln).then_inc(a2, 1)
        wh = K.wh
        node_dense(K, "t3m", K.hn, D, None, D, None, None, None,
                   lambda v, w, ps: v.tensor_tensor(wh[:, w, 0:D], ps, b[:, :], ALU.add), w1d=W)
        with nc.Block() as block:
            @block.vector
            def _(dve):
                v = nc.vector
                v.tensor_tensor(sq[:, :, :], wh[:, :, 0:D], wh[:, :, 0:D], ALU.mult)
                v.memset(wh[:, :, C1:], 0.0)
                v.drain()
                v.tensor_reduce(wh[:, :, D], sq[:, :, :], AX.X, ALU.add)
                v.drain().then_inc(d1, 1)

            @block.scalar
            def _(act):
                act.wait_ge(d1, 2)
                nc.scalar.sqrt(wh[:, :, D], wh[:, :, D]).then_inc(a3, 1)
                act.wait_ge(a3, 1)
        store_table(K, K.tab3, wh)
    with Phase(K, "l3g") as ph:
        ring = Ring(ph, R3)
        own = ph.sb("own", [P, TB, C1])
        prod = ph.sb("prod", [P, TB, D])
        sums = ph.sb("sums", [P, RING, TB, D])
        first = ph.sb("first", [P, R3])
        q = ph.sb("q", [P, C1])
        fidx = ph.sb("fidx", [P, 1], I32)
        kb = ph.sb("kb", [P, TB])
        mk = ph.sb("mk", [P, TB])
        dot = ph.sb("dot", [P, TB])
        nn = ph.sb("nn", [P, TB])
        neg = ph.sb("neg", [P, TB])
        bb = ph.sb("bb", [P, TB])
        idxed, got = ph.sems("idxed", "got")
        scanned, freed, stored = ([ph.sem(f"{n}{s}") for s in range(RING)] for n in ("scanned", "freed", "stored"))
        out = K.sums3.rearrange("(p j) d -> p j d", p=P)
        with nc.Block() as block:
            @block.gpsimd
            def _(pool):
                pool.wait_ge(idxed, 1)
                nc.gpsimd.indirect_dma_start(out=first[:, :], out_offset=None, in_=K.tab3,
                                             in_offset=bass.IndirectOffsetOnAxis(ap=fidx[:, 0:1], axis=0)).then_inc(got, 16)
                gather_rounds(nc, pool, ring, K.tab3, [(freed, 1)])

            @block.sync
            def _(sp):
                def body(it, isfirst):
                    for s in range(RING):
                        load_idx(sp, ring, K.idxdst, it, s, isfirst)
                        if not isfirst:
                            sp.wait_ge(scanned[s], it)
                            sp.dma_start(out[:, block_cols(it - 1, s), :], sums[:, s]).then_inc(stored[s], 16)
                rounds(sp, body)
                for s in range(RING):
                    sp.wait_ge(scanned[s], NBLK // RING)
                    sp.dma_start(out[:, block_cols(NBLK // RING - 1, s), :], sums[:, s]).then_inc(stored[s], 16)
                for s in range(RING):
                    sp.wait_ge(stored[s], NBLK // RING * 16)

            @block.vector
            def _(dve):
                v = nc.vector
                v.memset(K.st[:, :], 0.0)
                v.tensor_copy(fidx[:, :], K.by_src.node0[:, :])
                v.drain().then_inc(idxed, 1)
                dve.wait_ge(got, 16)
                v.tensor_copy(q[:, :], first[:, 0:C1])

                def body(it, isfirst):
                    for s in range(RING):
                        r = ring.rows
                        seg_masks(v, K.by_src.keep, block_cols(it, s), kb, mk=mk)
                        dve.wait_ge(ring.gathered[s], (it + 1) * TB * 16)
                        v.tensor_tensor(own[:, :, :], r[:, s, :, 0:C1], mk[:, :].unsqueeze(2).to_broadcast([P, TB, C1]), ALU.mult)
                        v.drain()
                        for f in range(C1):
                            v.tensor_tensor_scan(own[:, :, f], kb[:, :], own[:, :, f], q[:, f:f + 1], ALU.mult, ALU.add)
                        v.drain()
                        v.tensor_copy(q[:, :], own[:, TB - 1, :])
                        v.tensor_tensor(prod[:, :, :], own[:, :, 0:D], r[:, s, :, 0:D], ALU.mult)
                        v.tensor_tensor(nn[:, :], own[:, :, D], r[:, s, :, D], ALU.mult)
                        v.drain()
                        v.tensor_reduce(dot[:, :], prod[:, :, :], AX.X, ALU.add)
                        v.tensor_scalar(nn[:, :], nn[:, :], 1e-8, None, ALU.max)
                        v.drain()
                        v.reciprocal(nn[:, :], nn[:, :])
                        v.drain()
                        v.tensor_tensor(dot[:, :], dot[:, :], nn[:, :], ALU.mult)
                        v.drain()
                        v.tensor_scalar(neg[:, :], dot[:, :], 0.0, K.co[:, 1:2], ALU.min, ALU.mult)
                        v.tensor_scalar(nn[:, :], dot[:, :], 0.0, K.co[:, 0:1], ALU.max, ALU.mult)
                        v.drain()
                        v.tensor_tensor(dot[:, :], nn[:, :], neg[:, :], ALU.add)
                        v.tensor_copy(bb[:, :], K.base[:, block_cols(it, s)])
                        v.drain()
                        v.tensor_tensor(dot[:, :], dot[:, :], bb[:, :], ALU.mult)
                        v.drain()
                        if not isfirst:
                            dve.wait_ge(stored[s], it * 16)
                        v.tensor_tensor(sums[:, s], r[:, s, :, 0:D], dot[:, :].unsqueeze(2).to_broadcast([P, TB, D]), ALU.mult).then_inc(freed[s], 1)
                        v.drain()
                        for f in range(D):
                            v.tensor_tensor_scan(sums[:, s, :, f], kb[:, :], sums[:, s, :, f], K.st[:, f:f + 1], ALU.mult, ALU.add)
                        v.drain().then_inc(scanned[s], 1)
                        v.tensor_copy(K.st[:, :], sums[:, s, TB - 1, :])
                rounds(dve, body)


def layer3_finish(K):
    nc = K.nc
    with Phase(K, "l3f") as ph:
        res = ph.sb("res", [P, NT, D])
        has = ph.sb("has", [P, NT])
        done, stored = ph.sems("done", "stored")
        collect(K, K.by_src, K.sums3, D, res)
        with nc.Block() as block:
            @block.vector
            def _(dve):
                v = nc.vector
                v.tensor_scalar(has[:, :], K.by_src.cnt[:, :], 0.0, None, ALU.is_gt)
                v.tensor_scalar(K.wh[:, :, 0:D], K.wh[:, :, 0:D], K.co[:, 2:3], None, ALU.mult)
                v.drain()
                v.tensor_tensor(res[:, :, :], res[:, :, :], has[:, :].unsqueeze(2).to_broadcast([P, NT, D]), ALU.mult)
                v.drain()
                v.tensor_tensor(res[:, :, :], res[:, :, :], K.wh[:, :, 0:D], ALU.add)
                v.drain()
                v.scalar_tensor_tensor(K.x[:, :, :], res[:, :, :], K.co[:, 3:4], K.x[:, :, :], ALU.mult, ALU.add).then_inc(done, 1)

            @block.sync
            def _(sp):
                sp.wait_ge(done, 1)
                sp.dma_start(K.out[0:(NT - 1) * P, :].rearrange("(w p) d -> p w d", p=P), K.x[:, 0:NT - 1, :]).then_inc(stored, 16)
                sp.dma_start(K.out[(NT - 1) * P:N, :], K.x[0:N - (NT - 1) * P, NT - 1, :]).then_inc(stored, 16)
                sp.wait_ge(stored, 32)


def kernel(**inputs):
    import numpy as np
    import concourse.bacc as _bacc
    from concourse.bass_utils import run_bass_kernel_spmd as _run
    nc = _bacc.Bacc("TRN2", target_bir_lowering=False, num_devices=1)
    i = {k: np.ascontiguousarray(v) for k, v in inputs.items()}
    i32 = np.int32
    ids = np.arange(N, dtype=i32)
    pad = np.full(L - M, N, i32)
    rest = np.full(SORT_L - L, 4095, i32)
    arrays = {k: v for k, v in i.items() if k[0] == "L" or k == "x"}
    arrays["nodess"] = np.concatenate([ids, i["src"], pad, rest])
    arrays["nodesd"] = np.concatenate([ids, i["dst"], pad, rest])

    def rows(columns, other, width):
        body = np.concatenate([c.view(i32).reshape(E, -1) for c in columns] + [other.reshape(E, 1)], axis=1)
        r = np.zeros((L, width), i32)
        r[N:M, :body.shape[1]] = body
        r[:N, body.shape[1] - 1] = ids
        r[M:, body.shape[1] - 1] = N
        return r
    arrays["rec_s"] = rows([i["edge_attr_32"], i["edge_weight"], i["edge_weight_n2"]], i["dst"], R0)
    arrays["rec_d"] = rows([i["edge_attr_64"]], i["src"], RE)
    a = {k: nc.dram_tensor("in_" + k, v.shape, mybir.dt.from_np(v.dtype), kind="ExternalInput").ap()
         for k, v in arrays.items()}
    out = nc.dram_tensor("out_0", (N, D), F32, kind="ExternalOutput").ap()
    build(nc, a, out)
    r = _run(nc, [{"in_" + k: v for k, v in arrays.items()}], core_ids=[0])
    return r.results[0]["out_0"]
```

```python
import concourse.bass as bass
from concourse import mybir
from contextlib import ExitStack

F32 = mybir.dt.float32
BF16 = mybir.dt.bfloat16
I32 = mybir.dt.int32
ALU = mybir.AluOpType
ACT = mybir.ActivationFunctionType
AX = mybir.AxisListType

P = 128
N = 3125
E = 53125
NT = 25
NP = NT * P
M = N + E
J = 440
L = P * J
SORT_W = 512
SORT_L = P * SORT_W
CP = L // SORT_W
TB = 44
NBLK = J // TB
RING = 2
BIG = 3.4028235e38
KEY_ONE = 1 << 28
D = 64
H = 8
WIN = 16
NWIN = 196
ACC_W = 200
IB = 14
BODIES = 46
ITEMS = IB * BODIES
R0 = 36
RE = 66
R1 = 82
R2 = 128
R3 = 66


def bc(ap, shape):
    return ap.to_broadcast(shape)


class Kern:
    pass


class Order:

    def __init__(self, name, sb, dram):
        self.name = name
        self.keep = sb("keep" + name, [P, J])
        self.node0 = sb("node0" + name, [P, 1])
        self.fk = sb("fk" + name, [P, 1])
        self.nm = sb("nm" + name, [P, 1])
        self.cnt = sb("cnt" + name, [P, NT])
        self.end = sb("end" + name, [P, NT], I32)
        self.key = dram("key" + name, (SORT_L,), I32)
        self.ent = sb("ent" + name, [P, J], I32)
        self.other = sb("other" + name, [P, J], I32)
        self.endd = dram("endd" + name, (NP,))
        self.startd = dram("startd" + name, (NP,))
        self.cntd = dram("cntd" + name, (NP,))


def build(nc, a, out):
    top = ExitStack()
    with top:
        K = Kern()
        K.nc, K.a, K.out = nc, a, out
        K.semaphores = []

        def sb(n, s, d=F32):
            return top.enter_context(nc.sbuf_tensor(n, s, d))

        def dram(n, s, d=F32):
            return nc.dram_tensor(n, s, d, kind="Internal").ap()

        K.ident = sb("ident", [P, P])
        K.x = sb("x", [P, NT, D])
        K.hn = sb("hn", [P, NT, D])
        K.by_src = Order("s", sb, dram)
        K.by_dst = Order("d", sb, dram)
        K.meta = sb("meta", [P, J, 2], I32)
        K.st = sb("st", [P, D])
        K.nodes = sb("nodes", [P, J])
        K.keepc = sb("keepc", [CP, SORT_W])
        K.nxc = sb("nxc", [CP, 1])
        K.nmc = sb("nmc", [CP, 2])
        K.node0c = sb("node0c", [CP, 1], I32)
        K.nodec = sb("nodec", [CP, SORT_W])
        K.base = sb("base", [P, J])
        K.co = sb("co", [P, 5])
        K.item_w = sb("item_w", [1, ITEMS], I32)
        K.item_slot = sb("item_slot", [1, ITEMS], I32)
        K.item_first = sb("item_first", [1, BODIES], I32)
        K.iota16 = sb("iota16", [P, WIN])
        K.srct = sb("srct", [P, J], I32)
        K.cid = sb("cid", [P, SORT_W], I32)
        K.pcol = sb("pcol", [P, 1], I32)
        K.iot = sb("iot", [P, NP])
        K.lower = sb("lower", [NP // 64, NP // 64])
        K.sums0 = dram("sums0", (L, D))
        K.sums2 = dram("sums2", (L, D))
        K.sums3 = dram("sums3", (L, D))
        K.edgeu = dram("edgeu", (P, J, D))
        K.srcd = dram("srcd", (L,), I32)
        K.tab1 = dram("tab1", (NP, R1))
        K.tab2 = dram("tab2", (NP, R2))
        K.tab3 = dram("tab3", (NP, R3))
        K.g1 = dram("g1", (P, J, D + 1))

        sort_keys(K, K.by_src, first=True)
        layer0_pass(K)
        layer0_finish_and_edge_pass(K)
        src_to_tiles(K)
        with nc.sbuf_tensor("F", [CP, H, SORT_W], F32) as K.F:
            with nc.sbuf_tensor("atp", [P, J, 2 * H], F32) as K.atp:
                layer1_gather(K)
                layer1_softmax(K)
            with nc.sbuf_tensor("acc", [P, ACC_W, D + 1], F32) as K.acc:
                with nc.sbuf_tensor("item_rel", [P, ITEMS], F32) as K.item_rel, \
                        nc.sbuf_tensor("item_ex", [P, H, ITEMS], F32) as K.item_ex:
                    layer1_items(K)
                    layer1_sums(K)
                layer1_finish(K)
        renew_semaphores(K)
        layer2_gather(K)
        layer2_finish(K)
        with nc.sbuf_tensor("wh", [P, NT, R3], F32) as K.wh:
            layer3_gather(K)
            layer3_finish(K)


def renew_semaphores(K):
    K.nc.clear_and_free_semaphores(K.semaphores)
    K.nc.all_engine_barrier()
    K.semaphores = []


class Step:

    def __init__(self, nc, pool_ahead=False):
        self.nc, self.pool_ahead = nc, pool_ahead

    def __enter__(self):
        return self

    def __exit__(self, kind, *rest):
        if kind is None:
            ET = mybir.EngineType
            if self.pool_ahead:
                self.nc.multi_engine_barrier([ET.DVE, ET.Activation, ET.PE, ET.SP])
            else:
                self.nc.all_engine_barrier()

    def vector(self, program):
        program(self.nc.vector)

    def tensor(self, program):
        program(self.nc.tensor)

    def scalar(self, program):
        program(self.nc.scalar)

    def sync(self, program):
        program(self.nc.sync)

    def gpsimd(self, program):
        program(self.nc.gpsimd)


class Phase:

    def __init__(self, K, name):
        self.K, self.nc, self.name, self.st = K, K.nc, name, ExitStack()

    def __enter__(self):
        self.st.__enter__()
        return self

    def __exit__(self, *e):
        return self.st.__exit__(*e)

    def sb(self, n, s, d=F32):
        return self.st.enter_context(self.nc.sbuf_tensor(f"{self.name}_{n}", s, d))

    def ps(self, n, s=(P, 512), d=F32):
        return self.st.enter_context(self.nc.psum_tensor(f"{self.name}_{n}", list(s), d))

    def sem(self, n):
        s = self.nc.alloc_semaphore(name=f"{self.name}_{n}")
        self.K.semaphores.append(s)
        return s

    def sems(self, *names):
        return [self.sem(n) for n in names]


def sort_keys(K, by, first=False):
    nc = K.nc
    W = SORT_W
    with Phase(K, "sort" + by.name) as ph:
        raw = ph.sb("raw", [P, W], I32)
        X = [ph.sb("x0", [P, W]), ph.sb("x1", [P, W])]
        bits = ph.sb("bits", [P, 8], I32)
        sgn = ph.sb("sgn", [P, 8])
        flip = ph.sb("flip", [P, 8])
        neg = ph.sb("neg", [P, 1])
        turn_ps = [ph.ps(f"turn{i}") for i in range(2)]
        loaded, consts, cleared, step, turned, swapped, done_, stored = ph.sems(
            "loaded", "consts", "cleared", "step", "turned", "swapped", "done", "stored")
        swaps = []
        final = [None]

        with Step(nc, pool_ahead=not first) as block:
            @block.gpsimd
            def _(pool):
                if first:
                    nc.gpsimd.iota(K.cid[:, :], [[1, W]], base=KEY_ONE, channel_multiplier=W)
                    nc.gpsimd.memset(K.x[:, NT - 1, :], 0.0).then_inc(cleared, 1)
                    nc.gpsimd.memset(K.ident[:, :], 0.0).then_inc(cleared, 1)
                    pool.wait_ge(cleared, 2)
                    nc.gpsimd.affine_select(out=K.ident[:, :], in_=K.ident[:, :], compare_op=ALU.not_equal, fill=1.0,
                                            base=0, pattern=[[-1, P]], channel_multiplier=1)
                    nc.gpsimd.iota(K.pcol[:, :], [[1, 1]], base=0, channel_multiplier=1).then_inc(consts, 1)
                    nc.gpsimd.iota(K.iot[:, :], [[1, NP]], base=0, channel_multiplier=0, allow_small_or_imprecise_dtypes=True)
                    nc.gpsimd.memset(K.lower[:, :], 0.0).then_inc(cleared, 1)
                    pool.wait_ge(cleared, 3)
                    nc.gpsimd.affine_select(out=K.lower[:, :], in_=K.lower[:, :], compare_op=ALU.is_ge, fill=1.0,
                                            base=0, pattern=[[-1, NP // 64]], channel_multiplier=1)

            @block.vector
            def _(dve):
                n = 0

                def did(ins):
                    nonlocal n
                    n += 1
                    ins.then_inc(step, 1)

                def settle():
                    dve.wait_ge(step, n)

                if first:
                    dve.wait_ge(consts, 1)
                dve.wait_ge(loaded, 16)
                for b in range(7):
                    did(nc.vector.tensor_scalar(bits[:, b:b + 1], K.pcol[:, :], b, 1, ALU.logical_shift_right, ALU.bitwise_and))
                did(nc.vector.tensor_scalar(raw[:, :], raw[:, :], 16, None, ALU.logical_shift_left))
                settle()
                did(nc.vector.tensor_scalar(sgn[:, 0:7], bits[:, 0:7], -2.0, 1.0, ALU.mult, ALU.add))
                did(nc.vector.memset(sgn[:, 7:8], 1.0))
                did(nc.vector.tensor_tensor(X[0][:, :].bitcast(I32), raw[:, :], K.cid[:, :], ALU.bitwise_or))
                settle()
                did(nc.vector.tensor_tensor(flip[:, 0:7], sgn[:, 1:8], sgn[:, 0:7], ALU.mult))
                did(nc.vector.tensor_scalar(neg[:, :], sgn[:, 0:1], -1.0, None, ALU.mult))
                settle()
                cur, other = X
                for k in range(1, 17):
                    if k <= 8:
                        half = 2 ** (k - 1)
                        v = cur[:, :].rearrange("p (a x) -> p a x", x=4 * half)
                        part = v[:, :, 2 * half:] if k == 1 else v[:, :, half:3 * half]
                        did(nc.vector.tensor_scalar(part, part, -1.0, None, ALU.mult))
                    elif k == 9:
                        did(nc.vector.tensor_scalar(cur[:, 0:256], cur[:, 0:256], sgn[:, 0:1], None, ALU.mult))
                        did(nc.vector.tensor_scalar(cur[:, 256:512], cur[:, 256:512], neg[:, 0:1], None, ALU.mult))
                    else:
                        did(nc.vector.tensor_scalar(cur[:, :], cur[:, :], flip[:, k - 10:k - 9], None, ALU.mult))
                    settle()
                    for b in range(k - 1, -1, -1):
                        if k >= 10 and b in (k - 1, 8):
                            swaps.append((cur, other, n))
                            dve.wait_ge(swapped, len(swaps))
                            cur, other = other, cur
                        d = 2 ** (b - 9) if b >= 9 else 2 ** b
                        s = cur[:, :].rearrange("p (a two d) -> p a two d", two=2, d=d)
                        t = other[:, :].rearrange("p (a two d) -> p a two d", two=2, d=d)
                        did(nc.vector.tensor_tensor(t[:, :, 0, :], s[:, :, 0, :], s[:, :, 1, :], ALU.min))
                        did(nc.vector.tensor_tensor(t[:, :, 1, :], s[:, :, 0, :], s[:, :, 1, :], ALU.max))
                        settle()
                        cur, other = other, cur
                nc.vector.tensor_scalar(raw[:, :], cur[:, :].bitcast(I32), KEY_ONE - 1, None,
                                        ALU.bitwise_and).then_inc(done_, 1)

            @block.tensor
            def _(pe):
                if first:
                    pe.wait_ge(consts, 1)
                for m, (c, t, at) in enumerate(swaps):
                    pe.wait_ge(step, at)
                    for g in range(4):
                        last = nc.tensor.transpose(turn_ps[m % 2][:, g * P:(g + 1) * P], c[:, g * P:(g + 1) * P], K.ident[:, :])
                    last.then_inc(turned, 1)

            @block.scalar
            def _(act):
                for m, (c, t, at) in enumerate(swaps):
                    act.wait_ge(turned, m + 1)
                    nc.scalar.copy(t[:, :], turn_ps[m % 2][:, :]).then_inc(swapped, 1)

            @block.sync
            def _(sp):
                sp.dma_start(raw[:, :], K.a["nodes" + by.name].rearrange("(p f) -> p f", p=P)).then_inc(loaded, 16)
                if first:
                    sp.dma_start(K.x[:, 0:NT - 1, :], K.a["x"][0:(NT - 1) * P, :].rearrange("(w p) d -> p w d", p=P)).then_inc(stored, 16)
                    sp.wait_ge(cleared, 2)
                    sp.dma_start(K.x[0:N - (NT - 1) * P, NT - 1, :], K.a["x"][(NT - 1) * P:N, :]).then_inc(stored, 16)
                sp.wait_ge(done_, 1)
                sp.dma_start(by.key.rearrange("(p f) -> p f", p=P), raw[:, :]).then_inc(stored, 16)
                sp.wait_ge(stored, 48 if first else 16)


def list_setup(K, by):
    nc = K.nc
    HI, LO = 50, 64
    with Phase(K, "set" + by.name) as ph:
        key = ph.sb("key", [P, J], I32)
        nxt = ph.sb("nxt", [P, 1], I32)
        nodei = ph.sb("nodei", [P, J], I32)
        lo_i = ph.sb("lo_i", [P, J], I32)
        node = ph.sb("node", [P, J])
        hi = ph.sb("hi", [P, J])
        lo = ph.sb("lo", [P, J])
        t0 = ph.sb("t0", [P, J])
        t1 = ph.sb("t1", [P, J])
        c = ph.sb("c", [P, 8])
        one_hi = ph.sb("one_hi", [P, 2, TB, HI], BF16)
        one_lo = ph.sb("one_lo", [P, 2, TB, LO], BF16)
        zero = ph.sb("zero", [P, LO], BF16)
        cnt = ph.sb("cnt", [HI, LO])
        run = ph.sb("run", [HI, LO])
        start = ph.sb("start", [HI, LO])
        ones = ph.sb("ones", [HI, LO])
        base = ph.sb("base", [HI, 1])
        endf = ph.sb("endf", [P, NT])
        hist = ph.ps("hist")
        basep = ph.ps("basep")
        loaded, hot, used, dn, d2, p2, stored, lded = ph.sems("loaded", "hot", "used", "dn", "d2", "p2", "stored", "lded")
        by.indexed = ph.sem("indexed")
        ent = by.ent
        kd = by.key
        keep, node0, fk, nm = by.keep, by.node0, by.fk, by.nm
        with Step(nc, pool_ahead=True) as block:
            @block.sync
            def _(sp):
                sp.dma_start(key[:, :], kd[0:L].rearrange("(p j) -> p j", p=P)).then_inc(loaded, 16)
                with nc.allow_non_contiguous_dma(reason="one value per partition"):
                    sp.dma_start(nxt[:, :], kd[J:J + L].rearrange("(p j) -> p j", p=P)[:, 0:1]).then_inc(loaded, 16)
                sp.wait_ge(d2, 1)
                sp.dma_start(by.endd.rearrange("(h l) -> h l", l=LO), run[:, :]).then_inc(stored, 16)
                sp.dma_start(by.startd.rearrange("(h l) -> h l", l=LO), start[:, :]).then_inc(stored, 16)
                sp.dma_start(by.cntd.rearrange("(h l) -> h l", l=LO), cnt[:, :]).then_inc(stored, 16)
                sp.wait_ge(stored, 48)
                ends = by.endd.rearrange("(w p) -> p w", p=P)
                counts = by.cntd.rearrange("(w p) -> p w", p=P)
                with nc.allow_non_contiguous_dma(reason="one value per node, once"):
                    sp.dma_start(endf[:, :], ends).then_inc(lded, 16)
                    sp.dma_start(by.cnt[:, 0:NT - 1], counts[:, 0:NT - 1]).then_inc(lded, 16)
                    sp.dma_start(by.cnt[0:N - (NT - 1) * P, NT - 1:], counts[0:N - (NT - 1) * P, NT - 1:]).then_inc(lded, 16)
                sp.wait_ge(lded, 48)

            @block.vector
            def _(dve):
                v = nc.vector
                v.memset(zero[:, :], 0.0).then_inc(dn, 1)
                v.memset(ones[:, :], 1.0)
                v.memset(by.cnt[:, :], 0.0)
                dve.wait_ge(loaded, 32)
                v.tensor_scalar(ent[:, :], key[:, :], 0xFFFF, None, ALU.bitwise_and)
                v.tensor_scalar(nodei[:, :], key[:, :], 16, None, ALU.logical_shift_right)
                v.tensor_scalar(nxt[:, :], nxt[:, :], 0xFFFF, None, ALU.bitwise_and)
                v.drain().then_inc(by.indexed, 1)
                v.tensor_scalar(lo_i[:, :], nodei[:, :], 63, None, ALU.bitwise_and)
                v.tensor_copy(node[:, :], nodei[:, :])
                v.tensor_scalar(t0[:, :], ent[:, :], float(N), None, ALU.is_ge)
                v.tensor_scalar(t1[:, :], ent[:, :], float(M), None, ALU.is_lt)
                v.tensor_scalar(c[:, 0:1], nxt[:, :], float(N), None, ALU.is_ge)
                v.tensor_scalar(c[:, 1:2], nxt[:, :], float(M), None, ALU.is_lt)
                v.drain()
                v.tensor_scalar(nodei[:, :], nodei[:, :], 6, None, ALU.logical_shift_right)
                v.tensor_copy(lo[:, :], lo_i[:, :])
                v.tensor_tensor(keep[:, :], t0[:, :], t1[:, :], ALU.mult)
                v.tensor_tensor(c[:, 2:3], c[:, 0:1], c[:, 1:2], ALU.mult)
                v.tensor_tensor(c[:, 3:4], node[:, 0:1], node[:, J - 1:J], ALU.is_equal)
                v.tensor_copy(node0[:, :], node[:, 0:1])
                if by is K.by_src:
                    v.tensor_copy(K.nodes[:, :], node[:, :])
                v.drain()
                v.tensor_copy(hi[:, :], nodei[:, :])
                v.tensor_tensor(nm[:, :], keep[:, 0:1], c[:, 3:4], ALU.mult)
                v.drain()
                v.tensor_tensor(c[:, 4:5], nm[:, :], c[:, 2:3], ALU.mult)
                v.drain()
                v.tensor_scalar(c[:, 5:6], c[:, 4:5], -1.0, 1.0, ALU.mult, ALU.add)
                v.tensor_scalar(c[:, 6:7], node[:, 0:1], 1.0, None, ALU.add)
                v.drain()
                v.tensor_tensor(c[:, 5:6], c[:, 5:6], keep[:, 0:1], ALU.mult)
                v.drain()
                v.tensor_tensor(c[:, 5:6], c[:, 5:6], c[:, 6:7], ALU.mult)
                v.drain()
                v.tensor_scalar(fk[:, :], c[:, 5:6], -1.0, None, ALU.add)
                with dve.Fori(0, NBLK // 2) as it:
                    for s in range(2):
                        dve.wait_ge(used, it * 2 + s + 1)
                        js = bass.ds((it * 2 + s) * TB, TB)
                        v.tensor_tensor(one_hi[:, s], hi[:, js].unsqueeze(2).to_broadcast([P, TB, HI]),
                                        K.iot[:, 0:HI].unsqueeze(1).to_broadcast([P, TB, HI]), ALU.is_equal)
                        v.tensor_tensor(one_lo[:, s], lo[:, js].unsqueeze(2).to_broadcast([P, TB, LO]),
                                        K.iot[:, 0:LO].unsqueeze(1).to_broadcast([P, TB, LO]), ALU.is_equal).then_inc(hot, 1)
                dve.wait_ge(p2, 1)
                v.tensor_copy(cnt[:, :], hist[0:HI, 0:LO])
                v.drain()
                v.tensor_tensor_scan(run[:, :], ones[:, :], cnt[:, :], 0.0, ALU.mult, ALU.add)
                v.drain().then_inc(dn, 1)
                dve.wait_ge(p2, 2)
                v.tensor_copy(base[:, :], basep[0:HI, 0:1])
                v.drain()
                v.tensor_scalar(run[:, :], run[:, :], base[:, :], -1.0, ALU.add, ALU.add)
                v.drain()
                v.tensor_tensor(start[:, :], run[:, :], cnt[:, :], ALU.subtract)
                v.drain()
                v.tensor_scalar(start[:, :], start[:, :], 1.0, None, ALU.add)
                v.tensor_scalar(cnt[:, :], cnt[:, :], -1.0, 0.0, ALU.add, ALU.max)
                v.drain().then_inc(d2, 1)
                dve.wait_ge(lded, 48)
                v.tensor_copy(by.end[:, :], endf[:, :])

            @block.tensor
            def _(pe):
                pe.wait_ge(dn, 1)
                nc.tensor.matmul(hist[0:HI, 0:LO], zero[:, 0:HI], zero[:, :], start=True, stop=False).then_inc(used, 2)
                with pe.Fori(0, NBLK // 2) as it:
                    for s in range(2):
                        pe.wait_ge(hot, it * 2 + s + 1)
                        for j in range(TB):
                            last = nc.tensor.matmul(hist[0:HI, 0:LO], one_hi[:, s, j, :], one_lo[:, s, j, :],
                                                    start=False, stop=False)
                        last.then_inc(used, 1)
                nc.tensor.matmul(hist[0:HI, 0:LO], zero[:, 0:HI], zero[:, :], start=False, stop=True).then_inc(p2, 1)
                pe.wait_ge(dn, 2)
                nc.tensor.matmul(basep[0:HI, 0:1], K.lower[:, :], run[:, LO - 1:LO], start=True, stop=True).then_inc(p2, 1)


def rounds(engine, body, n=None):
    body(0, True)
    with engine.Fori(1, n or NBLK // RING) as it:
        body(it, False)


class Ring:

    def __init__(self, ph, width, dt=F32, size=RING, rows=True):
        self.size = size
        self.rows = ph.sb("rows", [P, size, TB, width], dt) if rows else None
        self.idx = ph.sb("ring_idx", [P, size, TB], I32)
        self.indexed = ph.sem("indexed")
        self.gathered = [ph.sem(f"gathered{s}") for s in range(size)]
        self.begun = ph.sem("begun")


def block_cols(it, s, size=RING):
    return bass.ds((it * size + s) * TB, TB)


def gather_rounds(nc, pool, ring, table, idx, freed):
    def body(it, first):
        for s in range(ring.size):
            if not first:
                pool.wait_ge(ring.gathered[s], it * TB * 16)
            nc.gpsimd.tensor_copy(ring.idx[:, s, :], idx[:, block_cols(it, s, ring.size)]).then_inc(ring.indexed, 1)
            pool.wait_ge(ring.indexed, it * ring.size + s + 1)
            if not first:
                for sem, per in freed:
                    pool.wait_ge(sem[s], it * per)
            pool.sem_inc(ring.begun, 1)
            for j in range(TB):
                nc.gpsimd.indirect_dma_start(
                    out=ring.rows[:, s, j, :], out_offset=None, in_=table,
                    in_offset=bass.IndirectOffsetOnAxis(ap=ring.idx[:, s, j:j + 1], axis=0)
                ).then_inc(ring.gathered[s], 16)
    rounds(pool, body, NBLK // ring.size)


def seg_masks(v, keep, js, kb, mb=None, nb=None, mk=None):
    v.tensor_copy(kb[:, :], keep[:, js])
    v.drain()
    if nb is not None:
        v.tensor_scalar(nb[:, :], kb[:, :], -1.0, BIG, ALU.add, ALU.mult)
    if mb is not None:
        v.tensor_scalar(mb[:, :], kb[:, :], 2.0, -1.0, ALU.mult, ALU.add)
        v.drain()
        v.tensor_scalar(mb[:, :], mb[:, :], BIG, None, ALU.mult)
    if mk is not None:
        v.tensor_scalar(mk[:, :], kb[:, :], -1.0, 1.0, ALU.mult, ALU.add)
    v.drain()


def layer0_pass(K):
    nc = K.nc
    half = D // 2
    with Phase(K, "l0g") as ph:
        rows = ph.sb("rows", [P, J, R0], I32)
        gathered = [ph.sem(f"gathered{b}") for b in range(NBLK)]
        begun = ph.sem("begun")
        list_setup(K, K.by_src)
        with Step(nc, pool_ahead=True) as block:
            @block.gpsimd
            def _(pool):
                pool.wait_ge(K.by_src.indexed, 1)
                pool.sem_inc(begun, 1)
                for j in range(J):
                    nc.gpsimd.indirect_dma_start(
                        out=rows[:, j, :], out_offset=None, in_=K.a["rec_s"],
                        in_offset=bass.IndirectOffsetOnAxis(ap=K.by_src.ent[:, j:j + 1], axis=0)
                    ).then_inc(gathered[j // TB], 16)
        sort_keys(K, K.by_dst)
        list_setup(K, K.by_dst)
        with Phase(K, "l0s") as ph:
            sums = ph.sb("sums", [P, RING, TB, D])
            kb = ph.sb("kb", [P, TB])
            mb = ph.sb("mb", [P, TB])
            nb = ph.sb("nb", [P, TB])
            scanned = [ph.sem(f"scanned{s}") for s in range(RING)]
            stored = [ph.sem(f"stored{s}") for s in range(RING)]
            out = K.sums0.rearrange("(p j) d -> p j d", p=P)
            with Step(nc, pool_ahead=True) as block:
                @block.sync
                def _(sp):
                    def body(it, first):
                        for s in range(RING):
                            sp.wait_ge(scanned[s], it + 1)
                            sp.dma_start(out[:, block_cols(it, s), :], sums[:, s]).then_inc(stored[s], 16)
                    rounds(sp, body)
                    for s in range(RING):
                        sp.wait_ge(stored[s], NBLK // RING * 16)

                @block.scalar
                def _(act):
                    for b in range(NBLK):
                        act.wait_ge(gathered[b], TB * 16)
                    nc.scalar.copy(K.by_src.other[:, :], rows[:, :, half + 2])
                    nc.scalar.copy(K.meta[:, :, :], rows[:, :, half:half + 2])

                @block.vector
                def _(dve):
                    v = nc.vector
                    v.memset(K.st[:, 0:half], 0.0)
                    v.memset(K.st[:, half:D], -BIG)
                    for b in range(NBLK):
                        s, js = b % RING, slice(b * TB, (b + 1) * TB)
                        r = rows[:, js, 0:half].bitcast(F32)
                        dve.wait_ge(gathered[b], TB * 16)
                        if b >= RING:
                            dve.wait_ge(stored[s], b // RING * 16)
                        seg_masks(v, K.by_src.keep, js, kb, mb=mb, nb=nb)
                        for f in range(half):
                            v.tensor_tensor_scan(sums[:, s, :, f], kb[:, :], r[:, :, f], K.st[:, f:f + 1], ALU.mult, ALU.add)
                        v.drain()
                        v.tensor_tensor(r, r, nb[:, :].unsqueeze(2).to_broadcast([P, TB, half]), ALU.add)
                        v.drain()
                        for f in range(half):
                            v.tensor_tensor_scan(sums[:, s, :, half + f], mb[:, :], r[:, :, f], K.st[:, half + f:half + f + 1],
                                                 ALU.min, ALU.max)
                        v.drain().then_inc(scanned[s], 1)
                        v.tensor_copy(K.st[:, :], sums[:, s, TB - 1, :])
                        v.drain()


def collect(K, by, table, nsum, res, pool_ahead=False):
    nc = K.nc
    act_name = table.tensor.name
    with Phase(K, "col" + act_name) as ph:
        sel = ph.sb("sel", [P, NP])
        nmb = ph.sb("nmb", [P, D])
        act = ph.sb("act", [P, 1])
        nmt = ph.sb("nmt", [D, P])
        tot = ph.sb("tot", [D, P])
        shf = ph.sb("shf", [D, P])
        car = ph.sb("car", [P, D + 1])
        has = ph.sb("has", [P, NT])
        tmp = ph.sb("tmp", [P, NT, D + 1])
        nmp = ph.ps("nmp")
        stp = ph.ps("stp")
        bp = [ph.ps(f"bp{i}") for i in range(4)]
        ready, begun, made, pm, got = ph.sems("ready", "begun", "made", "pm", "got")
        nm, fk, end = by.nm, by.fk, by.end
        with Step(nc, pool_ahead) as block:
            @block.gpsimd
            def _(pool):
                pool.wait_ge(ready, 1)
                pool.sem_inc(begun, 1)
                for w in range(NT):
                    nc.gpsimd.indirect_dma_start(out=res[:, w, :], out_offset=None, in_=table,
                                                 in_offset=bass.IndirectOffsetOnAxis(ap=end[:, w:w + 1], axis=0)).then_inc(got, 16)

            @block.tensor
            def _(pe):
                pe.wait_ge(made, 1)
                nc.tensor.matmul(nmp[0:D, 0:P], nmb[:, :], K.ident[:, :], start=True, stop=True)
                nc.tensor.transpose(stp[0:D, 0:P], K.st[:, :], K.ident[:, :]).then_inc(pm, 1)
                pe.wait_ge(made, 2)
                nc.tensor.transpose(stp[:, P:P + D], shf[:, :], K.ident[0:D, 0:D]).then_inc(pm, 1)
                pe.wait_ge(made, 3)
                for w in range(NT):
                    last = nc.tensor.matmul(bp[w // 7][:, w % 7 * (D + 1):(w % 7 + 1) * (D + 1)], sel[:, w * P:(w + 1) * P], car[:, :],
                                            start=True, stop=True)
                last.then_inc(pm, 1)

            @block.vector
            def _(dve):
                v = nc.vector
                v.sem_inc(ready, 1)
                v.tensor_copy(nmb[:, :], nm[:, 0:1].to_broadcast([P, D]))
                v.tensor_scalar(act[:, :], fk[:, :], 0.0, None, ALU.is_ge)
                v.memset(shf[:, 0:1], 0.0)
                v.memset(car[:, D:D + 1], 1.0)
                v.drain().then_inc(made, 1)
                dve.wait_ge(pm, 1)
                v.tensor_copy(nmt[:, :], nmp[0:D, 0:P])
                v.drain()
                if nsum < D:
                    v.tensor_scalar(nmt[nsum:, :], nmt[nsum:, :], 2.0, -1.0, ALU.mult, ALU.add)
                    v.drain()
                    v.tensor_scalar(nmt[nsum:, :], nmt[nsum:, :], BIG, None, ALU.mult)
                    v.drain()
                    v.tensor_tensor_scan(tot[nsum:, :], nmt[nsum:, :], stp[nsum:D, 0:P], -BIG, ALU.min, ALU.max)
                v.tensor_tensor_scan(tot[0:nsum, :], nmt[0:nsum, :], stp[0:nsum, 0:P], 0.0, ALU.mult, ALU.add)
                v.drain()
                v.tensor_copy(shf[:, 1:P], tot[:, 0:P - 1])
                v.drain().then_inc(made, 1)
                v.tensor_scalar(sel[:, :], K.iot[:, :], fk[:, 0:1], None, ALU.is_equal)
                dve.wait_ge(pm, 2)
                v.tensor_scalar(car[:, 0:D], stp[:, P:P + D], act[:, 0:1], None, ALU.mult)
                v.drain().then_inc(made, 1)
                dve.wait_ge(got, NT * 16)
                dve.wait_ge(pm, 3)
                for g in range(4):
                    w0, w1 = 7 * g, min(7 * g + 7, NT)
                    b = bp[g][:, 0:(w1 - w0) * (D + 1)].rearrange("p (w d) -> p w d", d=D + 1)
                    v.tensor_tensor(res[:, w0:w1, 0:nsum], res[:, w0:w1, 0:nsum], b[:, :, 0:nsum], ALU.add)
                    if nsum < D:
                        v.tensor_copy(tmp[:, w0:w1, nsum:], b[:, :, nsum:])
                if nsum < D:
                    v.drain()
                    v.tensor_scalar(has[:, :], tmp[:, :, D], -1.0, BIG, ALU.add, ALU.mult)
                    v.drain()
                    v.tensor_tensor(tmp[:, :, nsum:D], tmp[:, :, nsum:D], has[:, :].unsqueeze(2).to_broadcast([P, NT, D - nsum]), ALU.add)
                    v.drain()
                    v.tensor_tensor(res[:, :, nsum:], res[:, :, nsum:], tmp[:, :, nsum:D], ALU.max)


def node_dense(K, name, feat, F, w1, hid, func, b1, w2, put, w1d=None, pool_ahead=False):
    nc = K.nc
    with Phase(K, name) as ph:
        W1 = ph.sb("W1", [F, hid]) if w1 is not None else w1d
        W2 = ph.sb("W2", [hid, D]) if w2 is not None else None
        B1 = ph.sb("B1", [hid, 1]) if w2 is not None else None
        ft = ph.sb("ft", [F, 2, P])
        ht = ph.sb("ht", [hid, 2, P])
        pa, pb, pc = ([ph.ps(f"{n}{i}") for i in range(2)] for n in "abc")
        loaded, turned, moved, first, acted, second, used = ph.sems(
            "loaded", "turned", "moved", "first", "acted", "second", "used")
        two = w2 is not None
        nl = (w1 is not None) + 2 * two
        C = D if two else hid
        with Step(nc, pool_ahead) as block:
            @block.sync
            def _(sp):
                if w1 is not None:
                    sp.dma_start(W1[:, :], w1).then_inc(loaded, 16)
                if two:
                    sp.dma_start(W2[:, :], w2).then_inc(loaded, 16)
                    with nc.allow_non_contiguous_dma(reason="a bias as a column"):
                        sp.dma_start(B1[:, :], b1.unsqueeze(1)).then_inc(loaded, 16)
                if nl:
                    sp.wait_ge(loaded, 16 * nl)

            @block.tensor
            def _(pe):
                if nl:
                    pe.wait_ge(loaded, 16 * nl)
                for w in range(NT + 2):
                    if w < NT:
                        if w >= 2:
                            pe.wait_ge(moved, w - 1)
                        nc.tensor.transpose(pa[w % 2][0:F, 0:P], feat[:, w, :], K.ident[:, :]).then_inc(turned, 1)
                    if 1 <= w <= NT:
                        u = w - 1
                        pe.wait_ge(moved, u + 1)
                        if two:
                            if u >= 2:
                                pe.wait_ge(acted, u - 1)
                            nc.tensor.matmul(pb[u % 2][0:hid, 0:P], W1[:, :], ft[:, u % 2, :], start=True, stop=True).then_inc(first, 1)
                        else:
                            if u >= 2:
                                pe.wait_ge(used, u - 1)
                            nc.tensor.matmul(pc[u % 2][:, 0:hid], ft[:, u % 2, :], W1[:, :], start=True, stop=True).then_inc(second, 1)
                    if two and w >= 2:
                        u = w - 2
                        pe.wait_ge(acted, u + 1)
                        if u >= 2:
                            pe.wait_ge(used, u - 1)
                        nc.tensor.matmul(pc[u % 2][:, 0:D], ht[:, u % 2, :], W2[:, :], start=True, stop=True).then_inc(second, 1)

            @block.scalar
            def _(act):
                if nl:
                    act.wait_ge(loaded, 16 * nl)
                for w in range(NT + 1):
                    if w < NT:
                        act.wait_ge(turned, w + 1)
                        if w >= 2:
                            act.wait_ge(first if two else second, w - 1)
                        nc.scalar.copy(ft[:, w % 2, :], pa[w % 2][0:F, 0:P]).then_inc(moved, 1)
                    if two and w >= 1:
                        u = w - 1
                        act.wait_ge(first, u + 1)
                        if u >= 2:
                            act.wait_ge(second, u - 1)
                        nc.scalar.activation(ht[:, u % 2, :], pb[u % 2][0:hid, 0:P], func, bias=B1[:, 0:1]).then_inc(acted, 1)

            @block.vector
            def _(dve):
                for w in range(NT):
                    dve.wait_ge(second, w + 1)
                    put(nc.vector, w, pc[w % 2][:, 0:C]).then_inc(used, 1)


def normalise(K, name, pool_ahead=False):
    nc = K.nc
    with Phase(K, name) as ph:
        mean = ph.sb("mean", [P, NT])
        var = ph.sb("var", [P, NT])
        sq = ph.sb("sq", [P, NT, D])
        d1, rooted = ph.sems("d1", "rooted")
        with Step(nc, pool_ahead) as block:
            @block.vector
            def _(dve):
                v = nc.vector
                wide = lambda t: t[:, :].unsqueeze(2).to_broadcast([P, NT, D])
                v.tensor_reduce(mean[:, :], K.x[:, :, :], AX.X, ALU.add)
                v.drain()
                v.tensor_scalar(mean[:, :], mean[:, :], 1.0 / D, None, ALU.mult)
                v.drain()
                v.tensor_tensor(K.hn[:, :, :], K.x[:, :, :], wide(mean), ALU.subtract)
                v.drain()
                v.tensor_tensor(sq[:, :, :], K.hn[:, :, :], K.hn[:, :, :], ALU.mult)
                v.drain()
                v.tensor_reduce(var[:, :], sq[:, :, :], AX.X, ALU.add)
                v.drain()
                v.tensor_scalar(var[:, :], var[:, :], 1.0 / D, 1e-5, ALU.mult, ALU.add)
                v.drain().then_inc(d1, 1)
                dve.wait_ge(rooted, 1)
                v.reciprocal(var[:, :], var[:, :])
                v.drain()
                v.tensor_tensor(K.hn[:, :, :], K.hn[:, :, :], wide(var), ALU.mult)
                v.drain()
                v.tensor_scalar(K.hn[:, :, :], K.hn[:, :, :], 0.0, None, ALU.max)

            @block.scalar
            def _(act):
                act.wait_ge(d1, 1)
                nc.scalar.sqrt(var[:, :], var[:, :]).then_inc(rooted, 1)


def layer0_finish(K, start_edge_gathers):
    nc = K.nc
    with Phase(K, "l0f") as ph:
        res = ph.sb("res", [P, NT, D])
        feat = ph.sb("feat", [P, NT, 97])
        b2 = ph.sb("b2", [P, D])
        u0 = ph.sb("u0", [P, 1])
        m = ph.sb("m", [P, NT, 2])
        loaded = ph.sem("loaded")
        collect(K, K.by_src, K.sums0, D // 2, res, True)
        start_edge_gathers()
        half = D // 2
        with Step(nc, True) as block:
            @block.sync
            def _(sp):
                sp.dma_start(b2[:, :], K.a["L0_gnn_b2"].unsqueeze(0).to_broadcast([P, D])).then_inc(loaded, 16)
                sp.dma_start(u0[:, :], K.a["L0_gnn_u"][0:1, :].to_broadcast([P, 1])).then_inc(loaded, 16)

            @block.vector
            def _(dve):
                v = nc.vector
                dve.wait_ge(loaded, 32)
                wide = lambda t, n: t.unsqueeze(2).to_broadcast([P, NT, n])
                v.tensor_scalar(m[:, :, 0], K.by_src.cnt[:, :], 1.0, None, ALU.max)
                v.tensor_scalar(m[:, :, 1], K.by_src.cnt[:, :], 0.0, None, ALU.is_gt)
                v.tensor_tensor(K.x[:, :, :], K.x[:, :, :], b2[:, :].unsqueeze(1).to_broadcast([P, NT, D]), ALU.add)
                v.drain()
                v.reciprocal(m[:, :, 0], m[:, :, 0])
                v.tensor_tensor(feat[:, :, 0:half], res[:, :, 0:half], wide(m[:, :, 1], half), ALU.mult)
                v.tensor_tensor(feat[:, :, half:D], res[:, :, half:D], wide(m[:, :, 1], half), ALU.mult)
                v.tensor_copy(feat[:, :, 96], u0[:, 0:1].to_broadcast([P, NT]))
                v.drain()
                v.tensor_tensor(feat[:, :, D:96], feat[:, :, 0:half], wide(m[:, :, 0], half), ALU.mult)

        def put(v, w, ps):
            return v.tensor_tensor(K.x[:, w, :], K.x[:, w, :], ps, ALU.add)
        node_dense(K, "l0m", feat, 97, K.a["L0_gnn_W1"], 128, ACT.Relu, K.a["L0_gnn_b1"], K.a["L0_gnn_W2"], put, pool_ahead=True)
    normalise(K, "n1", True)
    with Phase(K, "t1") as ph:
        W = ph.sb("W", [D, H, D])
        at = ph.sb("at", [D, 2, H, D])
        V = ph.sb("V", [D, 2 * H])
        pr = ph.sb("pr", [D, 2, H, D])
        tab = ph.sb("tab", [P, NT, R1])
        loaded, stored = ph.sems("loaded", "stored")
        with Step(nc, True) as block:
            @block.sync
            def _(sp):
                sp.dma_start(W[:, :, :], K.a["L1_gnn_W"].rearrange("k (h c) -> k h c", h=H)).then_inc(loaded, 16)
                for i, n in enumerate(("L1_gnn_att_src", "L1_gnn_att_dst")):
                    sp.dma_start(at[:, i], K.a[n].unsqueeze(0).to_broadcast([D, H, D])).then_inc(loaded, 16)

            @block.vector
            def _(dve):
                v = nc.vector
                v.tensor_copy(tab[:, :, 0:D], K.hn[:, :, :])
                v.memset(tab[:, :, D:D + 1], 1.0)
                v.memset(tab[:, :, D + 17:], 0.0)
                dve.wait_ge(loaded, 48)
                for i in range(2):
                    v.tensor_tensor(pr[:, i], at[:, i], W[:, :, :], ALU.mult)
                v.drain()
                for i in range(2):
                    v.tensor_reduce(V[:, i * H:(i + 1) * H], pr[:, i], AX.X, ALU.add)

        def put(v, w, ps):
            return v.tensor_copy(tab[:, w, D + 1:D + 17], ps)
        node_dense(K, "t1m", K.hn, D, None, 2 * H, None, None, None, put, w1d=V, pool_ahead=True)
        store_table(K, K.tab1, tab, True)


def store_table(K, table, tab, pool_ahead=False):
    nc = K.nc
    with Phase(K, "st" + table.tensor.name) as ph:
        stored = ph.sem("stored")
        with Step(nc, pool_ahead) as block:
            @block.sync
            def _(sp):
                sp.dma_start(table.rearrange("(w p) r -> p w r", p=P), tab[:, :, :]).then_inc(stored, 16)
                sp.wait_ge(stored, 16)


def layer0_finish_and_edge_pass(K):
    nc = K.nc
    GRP = 4
    SIZE = 5
    with Phase(K, "ep") as ph:
        ring = Ring(ph, RE, I32, size=SIZE)
        kept = [ph.sem(f"kept{s}") for s in range(SIZE)]
        read = [ph.sem(f"read{s}") for s in range(SIZE)]

        def start_edge_gathers():
            with Step(nc, True) as block:
                @block.gpsimd
                def _(pool):
                    pool.wait_ge(K.by_dst.indexed, 1)
                    pool.sem_inc(ring.begun, 1)
                    gather_rounds(nc, pool, ring, K.a["rec_d"], K.by_dst.ent, [(kept, 1), (read, 1)])

        layer0_finish(K, start_edge_gathers)
        proj = ph.sb("proj", [P, SIZE, TB, D])
        wm = ph.sb("wm", [D, D])
        b1 = ph.sb("b1", [P, D])
        at = ph.sb("at", [D, 2, GRP * P])
        srcs = K.by_dst.other
        pt = [ph.ps(f"pt{i}") for i in range(2)]
        pu = [ph.ps(f"pu{i}") for i in range(2)]
        loaded, turned, moved, times, added, srcst = ph.sems("loaded", "turned", "moved", "times", "added", "srcst")
        projd = [ph.sem(f"projd{s}") for s in range(SIZE)]
        stored = [ph.sem(f"stored{s}") for s in range(SIZE)]
        G = TB // GRP
        with Step(nc) as block:
            @block.sync
            def _(sp):
                sp.dma_start(wm[:, :], K.a["L2_gnn_W1_msg"][0:D, :]).then_inc(loaded, 16)
                sp.dma_start(b1[:, :], K.a["L2_gnn_b1_msg"].unsqueeze(0).to_broadcast([P, D])).then_inc(loaded, 16)

                def store(it, s):
                    sp.dma_start(K.edgeu[:, block_cols(it, s, SIZE), :], proj[:, s]).then_inc(stored[s], 16)

                def body(it, first):
                    for s in range(SIZE):
                        sp.wait_ge(projd[s], it + 1)
                        store(it, s)
                rounds(sp, body, NBLK // SIZE)
                for s in range(SIZE):
                    sp.wait_ge(stored[s], NBLK // SIZE * 16)

            @block.tensor
            def _(pe):
                pe.wait_ge(loaded, 32)

                def body(it, first):
                    for s in range(SIZE):
                        pe.wait_ge(ring.gathered[s], (it + 1) * TB * 16)
                        r = ring.rows[:, s].bitcast(F32)
                        base = (it * SIZE + s) * G
                        for g in range(G + 1):
                            if g < G:
                                if not first or s or g >= 2:
                                    pe.wait_ge(moved, base + max(g - 1, 0))
                                for k in range(GRP):
                                    last = nc.tensor.transpose(pt[g % 2][0:RE, k * P:(k + 1) * P], r[:, GRP * g + k, :], K.ident[:, :])
                                last.then_inc(turned, 1)
                            if g >= 1:
                                u = g - 1
                                pe.wait_ge(moved, base + u + 1)
                                if not first or s or u >= 2:
                                    pe.wait_ge(added, base + max(u - 1, 0))
                                for k in range(GRP):
                                    last = nc.tensor.matmul(pu[u % 2][:, k * D:(k + 1) * D],
                                                            at[:, u % 2, k * P:(k + 1) * P], wm[:, :], start=True, stop=True)
                                last.then_inc(times, 1)
                rounds(pe, body, NBLK // SIZE)

            @block.scalar
            def _(act):
                def body(it, first):
                    for s in range(SIZE):
                        base = (it * SIZE + s) * G
                        act.wait_ge(ring.gathered[s], (it + 1) * TB * 16)
                        nc.scalar.copy(srcs[:, block_cols(it, s, SIZE)], ring.rows[:, s, :, D]).then_inc(kept[s], 1)
                        for g in range(G):
                            act.wait_ge(turned, base + g + 1)
                            if not first or s or g >= 2:
                                act.wait_ge(times, base + max(g - 1, 0))
                            nc.scalar.copy(at[:, g % 2, :], pt[g % 2][0:D, :]).then_inc(moved, 1)
                        act.wait_ge(moved, base + G)
                        nc.scalar.copy(srcs[:, 0:1], srcs[:, 0:1]).then_inc(read[s], 1)
                rounds(act, body, NBLK // SIZE)
                act.wait_ge(read[SIZE - 1], NBLK // SIZE)
                act.dma_start(K.srcd.rearrange("(p j) -> p j", p=P), srcs[:, :]).then_inc(srcst, 16)
                act.wait_ge(srcst, 16)

            @block.vector
            def _(dve):
                v = nc.vector
                dve.wait_ge(loaded, 32)

                def body(it, first):
                    for s in range(SIZE):
                        base = (it * SIZE + s) * G
                        if not first:
                            dve.wait_ge(stored[s], it * 16)
                        for g in range(G):
                            dve.wait_ge(times, base + g + 1)
                            v.tensor_tensor(proj[:, s, GRP * g:GRP * (g + 1), :],
                                            pu[g % 2][:, 0:2 * P].rearrange("p (t d) -> p t d", d=D),
                                            b1[:, :].unsqueeze(1).to_broadcast([P, GRP, D]), ALU.add).then_inc(added, 1)
                        v.drain().then_inc(projd[s], 1)
                rounds(dve, body, NBLK // SIZE)


def src_to_tiles(K):
    nc = K.nc
    with Phase(K, "s2t") as ph:
        keyc = ph.sb("keyc", [CP, SORT_W], I32)
        nodei = ph.sb("nodei", [CP, SORT_W], I32)
        srci = ph.sb("srci", [CP, SORT_W], I32)
        srcf = ph.sb("srcf", [CP, SORT_W])
        nxt = ph.sb("nxt", [CP, 1], I32)
        t = ph.sb("t", [CP, SORT_W])
        c = ph.sb("c", [CP, 4])
        tp = ph.ps("tp")
        loaded, ready, turned = ph.sems("loaded", "ready", "turned")
        with Step(nc) as block:
            @block.sync
            def _(sp):
                kd = K.by_dst.key
                sp.dma_start(keyc[:, :], kd[0:L].rearrange("(p j) -> p j", p=CP)).then_inc(loaded, 16)
                sp.dma_start(srci[:, :], K.srcd.rearrange("(p j) -> p j", p=CP)).then_inc(loaded, 16)
                with nc.allow_non_contiguous_dma(reason="one value per partition"):
                    sp.dma_start(nxt[:, :], kd[SORT_W:SORT_W + L].rearrange("(p j) -> p j", p=CP)[:, 0:1]).then_inc(loaded, 16)

            @block.vector
            def _(dve):
                v = nc.vector
                dve.wait_ge(loaded, 48)
                v.tensor_scalar(nodei[:, :], keyc[:, :], 16, None, ALU.logical_shift_right)
                v.tensor_scalar(keyc[:, :], keyc[:, :], 0xFFFF, None, ALU.bitwise_and)
                v.tensor_scalar(nxt[:, :], nxt[:, :], 0xFFFF, None, ALU.bitwise_and)
                v.tensor_copy(srcf[:, :], srci[:, :])
                v.drain()
                v.tensor_copy(K.nodec[:, :], nodei[:, :])
                v.drain().then_inc(ready, 1)
                v.tensor_scalar(t[:, :], keyc[:, :], float(N), None, ALU.is_ge)
                v.tensor_scalar(K.keepc[:, :], keyc[:, :], float(M), None, ALU.is_lt)
                v.tensor_scalar(c[:, 0:1], nxt[:, :], float(N), None, ALU.is_ge)
                v.tensor_scalar(c[:, 1:2], nxt[:, :], float(M), None, ALU.is_lt)
                v.tensor_tensor(c[:, 2:3], K.nodec[:, 0:1], K.nodec[:, SORT_W - 1:], ALU.is_equal)
                v.tensor_copy(K.node0c[:, :], nodei[:, 0:1])
                v.drain()
                v.tensor_tensor(K.keepc[:, :], K.keepc[:, :], t[:, :], ALU.mult)
                v.tensor_tensor(K.nxc[:, :], c[:, 0:1], c[:, 1:2], ALU.mult)
                v.drain()
                v.tensor_tensor(K.nmc[:, 0:1], K.keepc[:, 0:1], c[:, 2:3], ALU.mult)
                v.tensor_tensor(K.nmc[:, 1:2], K.nxc[:, :], c[:, 2:3], ALU.mult)
                dve.wait_ge(turned, 1)
                v.tensor_copy(K.srct[:, :].rearrange("q (p g) -> q g p", g=4),
                              tp[:, :].rearrange("q (g p) -> q g p", g=4)[:, :, 0:CP])
                v.drain()

            @block.tensor
            def _(pe):
                pe.wait_ge(ready, 1)
                for g in range(4):
                    last = nc.tensor.transpose(tp[:, g * P:g * P + CP], srcf[:, g * P:(g + 1) * P], K.ident[0:CP, 0:CP])
                last.then_inc(turned, 1)


def layer1_gather(K):
    nc = K.nc
    with Phase(K, "l1g") as ph:
        ring = Ring(ph, R1)
        kept = [ph.sem(f"kept{s}") for s in range(RING)]
        stored = [ph.sem(f"stored{s}") for s in range(RING)]
        with Step(nc) as block:
            @block.gpsimd
            def _(pool):
                gather_rounds(nc, pool, ring, K.tab1, K.srct, [(kept, 1), (stored, 16)])

            @block.scalar
            def _(act):
                def body(it, first):
                    for s in range(RING):
                        act.wait_ge(ring.gathered[s], (it + 1) * TB * 16)
                        act.dma_start(K.g1[:, block_cols(it, s), :], ring.rows[:, s, :, 0:D + 1]).then_inc(stored[s], 16)
                        nc.scalar.copy(K.atp[:, block_cols(it, s), :], ring.rows[:, s, :, D + 1:D + 17]).then_inc(kept[s], 1)
                rounds(act, body)
                for s in range(RING):
                    act.wait_ge(stored[s], NBLK // RING * 16)


def layer1_softmax(K):
    nc = K.nc
    W = SORT_W
    with Phase(K, "l1s") as ph:
        A = ph.sb("A", [CP, 2 * H, W])
        F = K.F
        first = ph.sb("first", [P, R1])
        mk = ph.sb("mk", [CP, W])
        mb = ph.sb("mb", [CP, W])
        mr = ph.sb("mr", [CP, W])
        nmb = ph.sb("nmb", [CP, 2, H])
        nmt = ph.sb("nmt", [H, 2, CP])
        last = ph.sb("last", [CP, H])
        tot = ph.sb("tot", [H, CP])
        shf = ph.sb("shf", [H, CP])
        ini = ph.sb("ini", [CP, 2, H])
        bank = [ph.ps(f"bank{i}") for i in range(4)]
        small = ph.ps("small")
        turned, moved, got, made, crossed, ready, expd = ph.sems(
            "turned", "moved", "got", "made", "crossed", "ready", "expd")
        with Step(nc) as block:
            @block.gpsimd
            def _(pool):
                nc.gpsimd.indirect_dma_start(out=first[0:CP, :], out_offset=None, in_=K.tab1,
                                             in_offset=bass.IndirectOffsetOnAxis(ap=K.node0c[:, 0:1], axis=0)).then_inc(got, 16)

            @block.tensor
            def _(pe):
                for r in range(2 * H):
                    if r >= 4:
                        pe.wait_ge(moved, r - 3)
                    for g in range(4):
                        lt = nc.tensor.transpose(bank[r % 4][0:CP, g * P:(g + 1) * P], K.atp[:, g::4, r], K.ident[:, :])
                    lt.then_inc(turned, 1)
                pe.wait_ge(made, 1)
                for i in range(2):
                    nc.tensor.matmul(small[0:H, i * P:i * P + CP], nmb[:, i, :], K.ident[0:CP, 0:CP], start=True, stop=True)
                nc.tensor.transpose(small[0:H, 2 * P:2 * P + CP], last[:, :], K.ident[0:CP, 0:CP]).then_inc(crossed, 1)
                pe.wait_ge(made, 2)
                nc.tensor.transpose(small[0:CP, 3 * P:3 * P + H], shf[:, :], K.ident[0:H, 0:H]).then_inc(crossed, 1)
                pe.wait_ge(made, 3)
                nc.tensor.transpose(small[0:H, 2 * P:2 * P + CP], last[:, :], K.ident[0:CP, 0:CP]).then_inc(crossed, 1)
                pe.wait_ge(made, 4)
                nc.tensor.transpose(small[0:CP, 3 * P:3 * P + H], shf[:, :], K.ident[0:H, 0:H]).then_inc(crossed, 1)

            @block.scalar
            def _(act):
                for r in range(2 * H):
                    act.wait_ge(turned, r + 1)
                    nc.scalar.copy(A[:, r, :], bank[r % 4][0:CP, :]).then_inc(moved, 1)
                for h in range(H):
                    act.wait_ge(ready, h + 1)
                    nc.scalar.activation(F[:, h, :], F[:, h, :], ACT.Exp).then_inc(expd, 1)

            @block.vector
            def _(dve):
                v = nc.vector
                v.tensor_scalar(mk[:, :], K.keepc[:, :], -1.0, 1.0, ALU.mult, ALU.add)
                v.tensor_scalar(mb[:, :], K.keepc[:, :], 2.0, -1.0, ALU.mult, ALU.add)
                v.tensor_copy(nmb[:, :, :], K.nmc[:, :].unsqueeze(2).to_broadcast([CP, 2, H]))
                v.tensor_scalar(mr[:, W - 1:], K.nxc[:, :], 2.0, -1.0, ALU.mult, ALU.add)
                v.drain()
                v.tensor_scalar(mb[:, :], mb[:, :], BIG, None, ALU.mult)
                v.drain()
                v.tensor_copy(mr[:, 0:W - 1], mb[:, 1:W])
                v.tensor_scalar(mr[:, W - 1:], mr[:, W - 1:], BIG, None, ALU.mult)
                dve.wait_ge(moved, 2 * H)
                dve.wait_ge(got, 16)
                v.tensor_tensor(A[:, H:, :], A[:, H:, :], mk[:, :].unsqueeze(1).to_broadcast([CP, H, W]), ALU.mult)
                v.drain()
                for h in range(H):
                    v.tensor_tensor_scan(A[:, H + h, :], K.keepc[:, :], A[:, H + h, :], first[0:CP, D + 9 + h:D + 10 + h], ALU.mult, ALU.add)
                v.drain()
                v.tensor_tensor(A[:, 0:H, :], A[:, 0:H, :], A[:, H:, :], ALU.add)
                v.drain()
                v.scalar_tensor_tensor(A[:, 0:H, :], A[:, 0:H, :], 0.2, A[:, 0:H, :], ALU.mult, ALU.max)
                v.drain()
                for h in range(H):
                    v.tensor_tensor_scan(F[:, h, :], mb[:, :], A[:, h, :], -BIG, ALU.min, ALU.max)
                v.drain()
                v.tensor_copy(last[:, :], F[:, :, W - 1])
                v.drain().then_inc(made, 1)
                dve.wait_ge(crossed, 1)
                for i in range(2):
                    v.tensor_scalar(nmt[:, i, :], small[0:H, i * P:i * P + CP], 2.0, -1.0, ALU.mult, ALU.add)
                v.drain()
                v.tensor_scalar(nmt[:, :, :], nmt[:, :, :], BIG, None, ALU.mult)
                v.drain()
                v.tensor_tensor_scan(tot[:, :], nmt[:, 0, :], small[0:H, 2 * P:2 * P + CP], -BIG, ALU.min, ALU.max)
                v.memset(shf[:, 0:1], -BIG)
                v.drain()
                v.tensor_copy(shf[:, 1:CP], tot[:, 0:CP - 1])
                v.drain().then_inc(made, 1)
                dve.wait_ge(crossed, 2)
                v.tensor_copy(ini[:, 0, :], small[0:CP, 3 * P:3 * P + H])
                v.drain()
                for h in range(H):
                    v.tensor_tensor_scan(A[:, H + h, :], mb[:, :], A[:, h, :], ini[:, 0, h:h + 1], ALU.min, ALU.max)
                v.drain()
                for h in range(H):
                    v.tensor_tensor_scan(F[:, h, ::-1], mr[:, ::-1], A[:, H + h, ::-1], -BIG, ALU.min, ALU.max)
                v.drain()
                v.tensor_copy(last[:, :], F[:, :, 0])
                v.drain().then_inc(made, 1)
                dve.wait_ge(crossed, 3)
                v.tensor_tensor_scan(tot[:, ::-1], nmt[:, 1, ::-1], small[0:H, 2 * P:2 * P + CP][:, ::-1], -BIG, ALU.min, ALU.max)
                v.memset(shf[:, CP - 1:], -BIG)
                v.drain()
                v.tensor_copy(shf[:, 0:CP - 1], tot[:, 1:CP])
                v.drain().then_inc(made, 1)
                dve.wait_ge(crossed, 4)
                v.tensor_copy(ini[:, 1, :], small[0:CP, 3 * P:3 * P + H])
                v.drain()
                for h in range(H):
                    v.tensor_tensor_scan(F[:, h, ::-1], mr[:, ::-1], A[:, H + h, ::-1], ini[:, 1, h:h + 1], ALU.min, ALU.max)
                v.drain()
                for h in range(H):
                    v.tensor_tensor(F[:, h, :], A[:, h, :], F[:, h, :], ALU.subtract).then_inc(ready, 1)


def layer1_items(K):
    nc = K.nc
    HI = ITEMS // 2
    with Phase(K, "l1i") as ph:
        wst = ph.sb("wst", [P, 2])
        wsi = ph.sb("wsi", [P, 2], I32)
        widx = ph.sb("widx", [P, 2])
        kio = ph.sb("kio", [P, ITEMS])
        cmp = ph.sb("cmp", [P, 2, ITEMS])
        ones = ph.sb("ones", [P, P])
        wa = ph.sb("wa", [P, ITEMS])
        ta = ph.sb("ta", [P, ITEMS])
        first = ph.sb("first", [1, BODIES])
        slot = ph.sb("slot", [1, ITEMS])
        tile_no = ph.sb("tile_no", [P, 4])
        sel = ph.sb("sel", [P, 4, ITEMS])
        count = [ph.ps(f"count{i}") for i in range(2)]
        bank = [ph.ps(f"bank{i}") for i in range(4)]
        far, consts, loaded, compared, counted, selected, spread, placed, kept = ph.sems(
            "far", "consts", "loaded", "compared", "counted", "selected", "spread", "placed", "kept")
        with Step(nc) as block:
            @block.gpsimd
            def _(pool):
                small = dict(allow_small_or_imprecise_dtypes=True)
                nc.gpsimd.iota(widx[:, :], [[P, 2]], base=1, channel_multiplier=1, **small)
                nc.gpsimd.iota(tile_no[:, :], [[1, 4]], base=0, channel_multiplier=4, **small)
                nc.gpsimd.iota(K.iota16[:, :], [[1, WIN]], base=0, channel_multiplier=0, **small)
                nc.gpsimd.iota(kio[:, :], [[1, ITEMS]], base=0, channel_multiplier=0, **small).then_inc(consts, 1)

            @block.sync
            def _(sp):
                st = K.by_dst.startd.rearrange("(w s) -> w s", s=WIN)
                sp.wait_ge(far, 1)
                with nc.allow_non_contiguous_dma(reason="one value per window"):
                    sp.dma_start(wst[:, 0:1], st[1:1 + P, 0:1]).then_inc(loaded, 16)
                    sp.dma_start(wst[0:NWIN - 1 - P, 1:2], st[1 + P:NWIN, 0:1]).then_inc(loaded, 16)

            @block.vector
            def _(dve):
                v = nc.vector
                v.memset(ones[:, :], 1.0)
                v.memset(wst[:, :], float(4 * ITEMS * P))
                v.drain().then_inc(far, 1)
                for i in range(4):
                    v.memset(K.acc[:, i * ACC_W // 4:(i + 1) * ACC_W // 4, :], 0.0)
                dve.wait_ge(consts, 1)
                dve.wait_ge(loaded, 32)
                v.tensor_copy(wsi[:, :], wst[:, :])
                v.drain()
                v.tensor_scalar(wsi[:, :], wsi[:, :], 7, None, ALU.logical_shift_right)
                v.drain()
                v.tensor_copy(wst[:, :], wsi[:, :])
                v.drain()
                v.tensor_scalar(wst[:, 0:1], wst[:, 0:1], float(J - 1), None, ALU.min)
                v.tensor_scalar(wst[0:NWIN - 1 - P, 1:2], wst[0:NWIN - 1 - P, 1:2], float(J - 1), None, ALU.min)
                v.drain()
                v.tensor_tensor(wst[:, :], wst[:, :], widx[:, :], ALU.add)
                v.drain()
                for i in range(2):
                    v.tensor_scalar(cmp[:, i, :], kio[:, :], wst[:, i:i + 1], None, ALU.is_ge)
                v.drain().then_inc(compared, 1)
                dve.wait_ge(counted, 1)
                for i in range(2):
                    v.tensor_copy(wa[:, i * HI:(i + 1) * HI], count[i][:, 0:HI])
                v.drain()
                v.tensor_tensor(ta[:, :], kio[:, :], wa[:, :], ALU.subtract)
                v.drain()
                v.memset(wa[:, J + NWIN - 1:], float(NWIN))
                v.memset(ta[:, J + NWIN - 1:], float(J - 1))
                v.drain()
                for g in range(4):
                    v.tensor_scalar(sel[:, g, :], ta[:, :], tile_no[:, g:g + 1], None, ALU.is_equal)
                v.drain().then_inc(selected, 1)
                v.tensor_scalar(first[:, :], ta[0:1, ::IB], float(J - IB), None, ALU.min)
                v.tensor_copy(K.item_w[:, :], wa[0:1, :])
                v.drain()
                v.tensor_tensor(slot[:, :].rearrange("p (b i) -> p b i", i=IB), ta[0:1, :].rearrange("p (b i) -> p b i", i=IB),
                                first[:, :].unsqueeze(2).to_broadcast([1, BODIES, IB]), ALU.subtract)
                v.tensor_copy(K.item_first[:, :], first[:, :])
                v.drain()
                v.tensor_copy(K.item_slot[:, :], slot[:, :])
                for i in range(2):
                    dve.wait_ge(spread, i + 1)
                    hs = slice(i * HI, (i + 1) * HI)
                    v.scalar_tensor_tensor(K.item_rel[:, hs], wa[:, hs], -float(WIN), bank[i][:, 0:HI], ALU.mult, ALU.add).then_inc(placed, 1)

            @block.tensor
            def _(pe):
                pe.wait_ge(compared, 1)
                for i in range(2):
                    for c in range(2):
                        lt = nc.tensor.matmul(count[i][:, 0:HI], ones[:, :], cmp[:, c, i * HI:(i + 1) * HI], start=(c == 0), stop=(c == 1))
                lt.then_inc(counted, 1)
                pe.wait_ge(selected, 1)
                for n in range(2 * (H + 1)):
                    f, i = n // 2, n % 2
                    if n in (4, 5):
                        pe.wait_ge(placed, n - 3)
                    if n >= 6:
                        pe.wait_ge(kept, n - 5)
                    for g in range(4):
                        src = K.nodec[:, g * P:(g + 1) * P] if f == 0 else K.F[:, f - 1, g * P:(g + 1) * P]
                        lt = nc.tensor.matmul(bank[n % 4][:, 0:HI], src, sel[0:CP, g, i * HI:(i + 1) * HI], start=(g == 0), stop=(g == 3))
                    lt.then_inc(spread, 1)

            @block.scalar
            def _(act):
                for n in range(2, 2 * (H + 1)):
                    f, i = n // 2, n % 2
                    act.wait_ge(spread, n + 1)
                    nc.scalar.copy(K.item_ex[:, f - 1, i * HI:(i + 1) * HI], bank[n % 4][:, 0:HI]).then_inc(kept, 1)


def layer1_sums(K):
    nc = K.nc
    with Phase(K, "l1a") as ph:
        g = ph.sb("g", [P, 2, IB, D + 1])
        place = ph.sb("place", [P, 2, IB, WIN])
        wt = ph.sb("wt", [P, 2, IB, H, WIN])
        pa = [[ph.ps(f"pa{b}{i}") for i in range(2)] for b in range(2)]
        fetched = [ph.sem(f"fetched{b}") for b in range(2)]
        weighed, multiplied, added, settled = ph.sems("weighed", "multiplied", "added", "settled")
        part = lambda b, u: pa[b][u // 7][:, u % 7 * (D + 1):(u % 7 + 1) * (D + 1)]
        with Step(nc) as block:
            @block.sync
            def _(sp):
                def body(it, first):
                    for b in range(2):
                        n = it * 2 + b
                        t, = values(nc, K.item_first[0:1, bass.ds(n, 1)], mybir.EngineType.SP, J - IB)
                        if not first:
                            sp.wait_ge(multiplied, n - 1)
                        sp.dma_start(g[:, b], K.g1[:, bass.ds(t, IB), :]).then_inc(fetched[b], 16)
                rounds(sp, body, BODIES // 2)

            @block.tensor
            def _(pe):
                def body(it, first):
                    for b in range(2):
                        n = it * 2 + b
                        slots = values(nc, K.item_slot[0:1, bass.ds(n * IB, IB)], mybir.EngineType.PE, IB - 1)
                        pe.wait_ge(weighed, n + 1)
                        pe.wait_ge(fetched[b], (it + 1) * 16)
                        if not first:
                            pe.wait_ge(added, n - 1)
                        for u in range(IB):
                            lt = nc.tensor.matmul(part(b, u), wt[:, b, u].rearrange("p h s -> p (h s)"),
                                                  g[:, b, bass.ds(slots[u], 1), :].rearrange("p o d -> p (o d)"), start=True, stop=True)
                        lt.then_inc(multiplied, 1)
                rounds(pe, body, BODIES // 2)

            @block.vector
            def _(dve):
                v = nc.vector

                def weigh(n, b):
                    v.tensor_tensor(place[:, b], K.iota16[:, :].unsqueeze(1).to_broadcast([P, IB, WIN]),
                                    K.item_rel[:, bass.ds(n * IB, IB)].unsqueeze(2).to_broadcast([P, IB, WIN]), ALU.is_equal)
                    v.drain()
                    v.tensor_tensor(wt[:, b], place[:, b].unsqueeze(2).to_broadcast([P, IB, H, WIN]),
                                    K.item_ex[:, :, bass.ds(n * IB, IB)].rearrange("p h i -> p i h").unsqueeze(3).to_broadcast([P, IB, H, WIN]),
                                    ALU.mult).then_inc(weighed, 1)

                def add(n, b):
                    windows = values(nc, K.item_w[0:1, bass.ds(n * IB, IB)], mybir.EngineType.DVE, NWIN)
                    dve.wait_ge(multiplied, n + 1)
                    for u in range(IB):
                        dst = K.acc[:, bass.ds(windows[u], 1), :].rearrange("p o d -> p (o d)")
                        v.tensor_tensor(dst, dst, part(b, u), ALU.add)
                        v.drain()
                    v.sem_inc(added, 1)

                weigh(0, 0)
                weigh(1, 1)
                with dve.Fori(1, BODIES // 2) as it:
                    for b in range(2):
                        add(it * 2 + b - 2, b)
                        weigh(it * 2 + b, b)
                for b in range(2):
                    add(BODIES - 2 + b, b)


def values(nc, ap, engine, most):
    return nc.values_load_multi_w_load_instructions(ap, engines=[engine], min_val=0, max_val=most,
                                                    skip_runtime_bounds_check_because="the table is clamped where it is made")[1]


def layer1_finish(K):
    nc = K.nc
    with Phase(K, "l1f") as ph:
        rec = ph.sb("rec", [P, ACC_W])
        bias = ph.sb("bias", [P, D])
        W = ph.sb("W", [D, H * D])
        nrm = ph.sb("nrm", [P, 2, H, D])
        at = ph.sb("at", [D, 2, H, 8, WIN])
        pt = [[ph.ps(f"pt{i}{j}") for j in range(2)] for i in range(2)]
        po = [ph.ps(f"po{i}") for i in range(2)]
        loaded, scaled, turned, moved, times, added = ph.sems("loaded", "scaled", "turned", "moved", "times", "added")
        with Step(nc) as block:
            @block.sync
            def _(sp):
                sp.dma_start(bias[:, :], K.a["L1_gnn_bias"].unsqueeze(0).to_broadcast([P, D])).then_inc(loaded, 16)
                sp.dma_start(W[:, :], K.a["L1_gnn_W"]).then_inc(loaded, 16)
                sp.wait_ge(loaded, 32)

            @block.vector
            def _(dve):
                v = nc.vector
                dve.wait_ge(loaded, 32)
                v.tensor_scalar(rec[:, :], K.acc[:, :, D], 1e-30, None, ALU.max)
                v.tensor_tensor(K.x[:, :, :], K.x[:, :, :], bias[:, :].unsqueeze(1).to_broadcast([P, NT, D]), ALU.add)
                v.drain()
                v.reciprocal(rec[:, :], rec[:, :])
                v.drain()
                for w in range(NT + 1):
                    if w < NT:
                        if w >= 2:
                            dve.wait_ge(turned, w - 1)
                        v.tensor_tensor(nrm[:, w % 2], K.acc[:, 8 * w:8 * w + 8, 0:D],
                                        rec[:, 8 * w:8 * w + 8].unsqueeze(2).to_broadcast([P, 8, D]), ALU.mult).then_inc(scaled, 1)
                    if w >= 1:
                        u = w - 1
                        dve.wait_ge(times, u + 1)
                        v.scalar_tensor_tensor(K.x[:, u, :], po[u % 2][:, 0:D], 1.0 / H, K.x[:, u, :], ALU.mult, ALU.add).then_inc(added, 1)

            @block.tensor
            def _(pe):
                pe.wait_ge(loaded, 32)
                for w in range(NT + 1):
                    if w < NT:
                        pe.wait_ge(scaled, w + 1)
                        if w >= 2:
                            pe.wait_ge(moved, 2 * (w - 1))
                        for m in range(8):
                            lt = nc.tensor.transpose(pt[w % 2][m // 4][0:D, m % 4 * P:(m % 4 + 1) * P], nrm[:, w % 2, m, :], K.ident[:, :])
                        lt.then_inc(turned, 1)
                    if w >= 1:
                        u = w - 1
                        pe.wait_ge(moved, 2 * (u + 1))
                        if u >= 2:
                            pe.wait_ge(added, u - 1)
                        for h in range(H):
                            lt = nc.tensor.matmul(po[u % 2][:, 0:D],
                                                  at[:, u % 2, h].rearrange("c m s -> c (m s)"),
                                                  W[:, h * D:(h + 1) * D], start=(h == 0), stop=(h == H - 1))
                        lt.then_inc(times, 1)

            @block.scalar
            def _(act):
                for w in range(NT):
                    act.wait_ge(turned, w + 1)
                    if w >= 2:
                        act.wait_ge(times, w - 1)
                    for i in range(2):
                        nc.scalar.copy(at[:, w % 2, :, 4 * i:4 * i + 4, :],
                                       pt[w % 2][i][0:D, :].rearrange("c (m h s) -> c h m s", m=4, h=H)).then_inc(moved, 1)


def layer2_gather(K):
    nc = K.nc
    normalise(K, "n2")
    with Phase(K, "t2") as ph:
        W = ph.sb("W", [D, R2])
        tab = ph.sb("tab", [P, NT, R2])
        loaded = ph.sem("loaded")
        with Step(nc) as block:
            @block.sync
            def _(sp):
                sp.dma_start(W[:, :].rearrange("k (i d) -> k i d", i=2),
                             K.a["L2_gnn_W1_msg"][D:3 * D, :].rearrange("(i k) d -> k i d", i=2)).then_inc(loaded, 16)
                sp.wait_ge(loaded, 16)
        node_dense(K, "t2m", K.hn, D, None, R2, None, None, None,
                   lambda v, w, ps: v.tensor_copy(tab[:, w, :], ps), w1d=W)
        store_table(K, K.tab2, tab)
    with Phase(K, "l2g") as ph:
        ring = Ring(ph, R2)
        u = ph.sb("u", [P, RING, TB, D])
        sums = ph.sb("sums", [P, RING, TB, D])
        first = ph.sb("first", [P, R2])
        q = ph.sb("q", [P, D])
        fidx = ph.sb("fidx", [P, 1], I32)
        kb = ph.sb("kb", [P, TB])
        mk = ph.sb("mk", [P, TB])
        idxed, got = ph.sems("idxed", "got")
        fetched, mixed, acted, scanned, freed, stored = (
            [ph.sem(f"{n}{s}") for s in range(RING)] for n in ("fetched", "mixed", "acted", "scanned", "freed", "stored"))
        out = K.sums2.rearrange("(p j) d -> p j d", p=P)
        with Step(nc) as block:
            @block.gpsimd
            def _(pool):
                pool.wait_ge(idxed, 1)
                nc.gpsimd.indirect_dma_start(out=first[:, :], out_offset=None, in_=K.tab2,
                                             in_offset=bass.IndirectOffsetOnAxis(ap=fidx[:, 0:1], axis=0)).then_inc(got, 16)
                gather_rounds(nc, pool, ring, K.tab2, K.by_dst.other, [(freed, 1)])

            @block.sync
            def _(sp):
                def body(it, isfirst):
                    for s in range(RING):
                        if not isfirst:
                            sp.wait_ge(mixed[s], it)
                        sp.dma_start(u[:, s], K.edgeu[:, block_cols(it, s), :]).then_inc(fetched[s], 16)
                        if not isfirst:
                            sp.wait_ge(scanned[s], it)
                            sp.dma_start(out[:, block_cols(it - 1, s), :], sums[:, s]).then_inc(stored[s], 16)
                rounds(sp, body)
                for s in range(RING):
                    sp.wait_ge(scanned[s], NBLK // RING)
                    sp.dma_start(out[:, block_cols(NBLK // RING - 1, s), :], sums[:, s]).then_inc(stored[s], 16)
                for s in range(RING):
                    sp.wait_ge(stored[s], NBLK // RING * 16)

            @block.scalar
            def _(act):
                def body(it, isfirst):
                    for s in range(RING):
                        act.wait_ge(mixed[s], it + 1)
                        nc.scalar.activation(sums[:, s], sums[:, s], ACT.Silu).then_inc(acted[s], 1)
                rounds(act, body)

            @block.vector
            def _(dve):
                v = nc.vector
                v.memset(K.st[:, :], 0.0)
                v.tensor_copy(fidx[:, :], K.by_dst.node0[:, :])
                v.drain().then_inc(idxed, 1)
                dve.wait_ge(got, 16)
                v.tensor_copy(q[:, :], first[:, D:])

                def body(it, isfirst):
                    for s in range(RING):
                        r = ring.rows
                        seg_masks(v, K.by_dst.keep, block_cols(it, s), kb, mk=mk)
                        dve.wait_ge(ring.gathered[s], (it + 1) * TB * 16)
                        v.tensor_tensor(r[:, s, :, D:], r[:, s, :, D:], mk[:, :].unsqueeze(2).to_broadcast([P, TB, D]), ALU.mult)
                        dve.wait_ge(fetched[s], (it + 1) * 16)
                        v.tensor_tensor(r[:, s, :, 0:D], r[:, s, :, 0:D], u[:, s], ALU.add)
                        v.drain()
                        for f in range(D):
                            v.tensor_tensor_scan(r[:, s, :, D + f], kb[:, :], r[:, s, :, D + f], q[:, f:f + 1], ALU.mult, ALU.add)
                        v.drain()
                        if not isfirst:
                            dve.wait_ge(stored[s], it * 16)
                        v.tensor_tensor(sums[:, s], r[:, s, :, 0:D], r[:, s, :, D:], ALU.add)
                        v.tensor_copy(q[:, :], r[:, s, TB - 1, D:])
                        v.drain().then_inc(mixed[s], 1)
                        dve.wait_ge(acted[s], it + 1)
                        v.tensor_tensor(sums[:, s], sums[:, s], kb[:, :].unsqueeze(2).to_broadcast([P, TB, D]), ALU.mult).then_inc(freed[s], 1)
                        v.drain()
                        for f in range(D):
                            v.tensor_tensor_scan(sums[:, s, :, f], kb[:, :], sums[:, s, :, f], K.st[:, f:f + 1], ALU.mult, ALU.add)
                        v.drain().then_inc(scanned[s], 1)
                        v.tensor_copy(K.st[:, :], sums[:, s, TB - 1, :])
                rounds(dve, body)


def layer2_finish(K):
    nc = K.nc
    with Phase(K, "l2f") as ph:
        res = ph.sb("res", [P, NT, D])
        feat = ph.sb("feat", [P, NT, 2 * D])
        b2m = ph.sb("b2m", [P, D])
        b2u = ph.sb("b2u", [P, D])
        W2m = ph.sb("W2m", [D, D])
        r = ph.sb("r", [P, 2, NT])
        loaded = ph.sem("loaded")
        collect(K, K.by_dst, K.sums2, D, res)
        with Step(nc) as block:
            @block.sync
            def _(sp):
                for t, n in ((b2m, "L2_gnn_b2_msg"), (b2u, "L2_gnn_b2_upd")):
                    sp.dma_start(t[:, :], K.a[n].unsqueeze(0).to_broadcast([P, D])).then_inc(loaded, 16)
                sp.dma_start(W2m[:, :], K.a["L2_gnn_W2_msg"]).then_inc(loaded, 16)
                sp.wait_ge(loaded, 48)

            @block.vector
            def _(dve):
                v = nc.vector
                wide = lambda t, n: t.unsqueeze(2).to_broadcast([P, NT, n])
                row = lambda t: t[:, :].unsqueeze(1).to_broadcast([P, NT, D])
                dve.wait_ge(loaded, 48)
                v.tensor_scalar(r[:, 0], K.by_dst.cnt[:, :], 1e-6, None, ALU.add)
                v.tensor_scalar(r[:, 1], K.by_dst.cnt[:, :], 0.0, None, ALU.is_gt)
                v.tensor_tensor(K.x[:, :, :], K.x[:, :, :], row(b2u), ALU.add)
                v.tensor_copy(feat[:, :, 0:D], K.hn[:, :, :])
                v.drain()
                v.reciprocal(r[:, 0], r[:, 0])
                v.drain()
                v.tensor_tensor(r[:, 1], r[:, 1], r[:, 0], ALU.mult)
                v.tensor_tensor(r[:, 0], K.by_dst.cnt[:, :], r[:, 0], ALU.mult)
                v.drain()
                v.tensor_tensor(res[:, :, :], res[:, :, :], wide(r[:, 1], D), ALU.mult)
                v.tensor_tensor(feat[:, :, D:], row(b2m), wide(r[:, 0], D), ALU.mult)
        node_dense(K, "l2a", res, D, None, D, None, None, None,
                   lambda v, w, ps: v.tensor_tensor(feat[:, w, D:], feat[:, w, D:], ps, ALU.add), w1d=W2m)
        node_dense(K, "l2m", feat, 2 * D, K.a["L2_gnn_W1_upd"], D, ACT.Silu, K.a["L2_gnn_b1_upd"], K.a["L2_gnn_W2_upd"],
                   lambda v, w, ps: v.tensor_tensor(K.x[:, w, :], K.x[:, w, :], ps, ALU.add))


def layer3_gather(K):
    nc = K.nc
    normalise(K, "n3")
    C1 = D + 1
    with Phase(K, "t3") as ph:
        b = ph.sb("b", [P, D])
        W = ph.sb("W", [D, D])
        sq = ph.sb("sq", [P, NT, D])
        dstf = ph.sb("dstf", [P, J])
        y = ph.sb("y", [P, J])
        z = ph.sb("z", [P, J])
        co = ph.sb("co", [P, 8])
        loaded, d1, d2, a1, a2, a3 = ph.sems("loaded", "d1", "d2", "a1", "a2", "a3")
        with Step(nc) as block:
            @block.sync
            def _(sp):
                row = lambda n, k: K.a[n].unsqueeze(0).to_broadcast([P, k])
                sp.dma_start(b[:, :], row("L3_gnn_b", D)).then_inc(loaded, 16)
                sp.dma_start(W[:, :], K.a["L3_gnn_W"]).then_inc(loaded, 16)
                sp.dma_start(co[:, 0:3], row("L3_gnn_coeff_param", 3)).then_inc(loaded, 16)
                sp.dma_start(co[:, 4:6], row("L3_gnn_deg_coeff", 2)).then_inc(loaded, 16)
                sp.dma_start(co[:, 6:7], row("L3_gnn_scale_param", 1)).then_inc(loaded, 16)
                sp.wait_ge(loaded, 80)

            @block.vector
            def _(dve):
                v = nc.vector
                dve.wait_ge(loaded, 80)
                meta = K.meta[:, :, :].bitcast(F32)
                v.tensor_copy(dstf[:, :], K.by_src.other[:, :])
                v.tensor_scalar(y[:, :], meta[:, :, 1], co[:, 4:5], co[:, 5:6], ALU.mult, ALU.add)
                v.tensor_copy(co[:, 7:8], co[:, 6:7])
                v.tensor_reduce(co[:, 3:4], co[:, 0:3], AX.X, ALU.max)
                v.drain()
                v.tensor_scalar(z[:, :], y[:, :], -1.0, None, ALU.mult)
                v.tensor_scalar(K.co[:, 4:5], co[:, 7:8], -1.0, None, ALU.mult)
                v.tensor_scalar(co[:, 0:3], co[:, 0:3], co[:, 3:4], None, ALU.subtract)
                v.drain()
                v.tensor_tensor(z[:, :], z[:, :], y[:, :], ALU.min)
                v.tensor_tensor(K.co[:, 4:5], K.co[:, 4:5], co[:, 7:8], ALU.min)
                v.drain().then_inc(d1, 1)
                dve.wait_ge(a1, 3)
                v.tensor_scalar(z[:, :], z[:, :], 1.0, None, ALU.add)
                v.tensor_scalar(K.co[:, 4:5], K.co[:, 4:5], 1.0, None, ALU.add)
                v.tensor_reduce(co[:, 3:4], co[:, 0:3], AX.X, ALU.add)
                v.drain().then_inc(d2, 1)
                v.reciprocal(co[:, 3:4], co[:, 3:4])
                v.tensor_scalar(y[:, :], y[:, :], 0.0, None, ALU.max)
                v.tensor_scalar(co[:, 7:8], co[:, 7:8], 0.0, None, ALU.max)
                v.tensor_tensor(dstf[:, :], dstf[:, :], K.nodes[:, :], ALU.not_equal)
                v.drain()
                v.tensor_scalar(K.co[:, 0:3], co[:, 0:3], co[:, 3:4], None, ALU.mult)
                v.tensor_tensor(dstf[:, :], dstf[:, :], meta[:, :, 0], ALU.mult)
                dve.wait_ge(a2, 2)
                v.tensor_tensor(y[:, :], y[:, :], z[:, :], ALU.add)
                v.tensor_tensor(K.co[:, 3:4], co[:, 7:8], K.co[:, 4:5], ALU.add)
                v.drain()
                v.tensor_tensor(K.base[:, :], dstf[:, :], y[:, :], ALU.mult)

            @block.scalar
            def _(act):
                act.wait_ge(d1, 1)
                nc.scalar.activation(z[:, :], z[:, :], ACT.Exp).then_inc(a1, 1)
                nc.scalar.activation(K.co[:, 4:5], K.co[:, 4:5], ACT.Exp).then_inc(a1, 1)
                nc.scalar.activation(co[:, 0:3], co[:, 0:3], ACT.Exp).then_inc(a1, 1)
                act.wait_ge(d2, 1)
                nc.scalar.activation(z[:, :], z[:, :], ACT.Ln).then_inc(a2, 1)
                nc.scalar.activation(K.co[:, 4:5], K.co[:, 4:5], ACT.Ln).then_inc(a2, 1)
        wh = K.wh
        node_dense(K, "t3m", K.hn, D, None, D, None, None, None,
                   lambda v, w, ps: v.tensor_tensor(wh[:, w, 0:D], ps, b[:, :], ALU.add), w1d=W)
        with Step(nc) as block:
            @block.vector
            def _(dve):
                v = nc.vector
                v.tensor_tensor(sq[:, :, :], wh[:, :, 0:D], wh[:, :, 0:D], ALU.mult)
                v.memset(wh[:, :, C1:], 0.0)
                v.drain()
                v.tensor_reduce(wh[:, :, D], sq[:, :, :], AX.X, ALU.add)
                v.drain().then_inc(d1, 1)

            @block.scalar
            def _(act):
                act.wait_ge(d1, 2)
                nc.scalar.sqrt(wh[:, :, D], wh[:, :, D]).then_inc(a3, 1)
                act.wait_ge(a3, 1)
        store_table(K, K.tab3, wh)
    with Phase(K, "l3g") as ph:
        ring = Ring(ph, R3)
        own = ph.sb("own", [P, TB, C1])
        prod = ph.sb("prod", [P, TB, D])
        sums = ph.sb("sums", [P, RING, TB, D])
        first = ph.sb("first", [P, R3])
        q = ph.sb("q", [P, C1])
        fidx = ph.sb("fidx", [P, 1], I32)
        kb = ph.sb("kb", [P, TB])
        mk = ph.sb("mk", [P, TB])
        dot = ph.sb("dot", [P, TB])
        nn = ph.sb("nn", [P, TB])
        neg = ph.sb("neg", [P, TB])
        bb = ph.sb("bb", [P, TB])
        idxed, got = ph.sems("idxed", "got")
        scanned, freed, stored = ([ph.sem(f"{n}{s}") for s in range(RING)] for n in ("scanned", "freed", "stored"))
        out = K.sums3.rearrange("(p j) d -> p j d", p=P)
        with Step(nc) as block:
            @block.gpsimd
            def _(pool):
                pool.wait_ge(idxed, 1)
                nc.gpsimd.indirect_dma_start(out=first[:, :], out_offset=None, in_=K.tab3,
                                             in_offset=bass.IndirectOffsetOnAxis(ap=fidx[:, 0:1], axis=0)).then_inc(got, 16)
                gather_rounds(nc, pool, ring, K.tab3, K.by_src.other, [(freed, 1)])

            @block.sync
            def _(sp):
                def body(it, isfirst):
                    for s in range(RING):
                        if not isfirst:
                            sp.wait_ge(scanned[s], it)
                            sp.dma_start(out[:, block_cols(it - 1, s), :], sums[:, s]).then_inc(stored[s], 16)
                rounds(sp, body)
                for s in range(RING):
                    sp.wait_ge(scanned[s], NBLK // RING)
                    sp.dma_start(out[:, block_cols(NBLK // RING - 1, s), :], sums[:, s]).then_inc(stored[s], 16)
                for s in range(RING):
                    sp.wait_ge(stored[s], NBLK // RING * 16)

            @block.vector
            def _(dve):
                v = nc.vector
                v.memset(K.st[:, :], 0.0)
                v.tensor_copy(fidx[:, :], K.by_src.node0[:, :])
                v.drain().then_inc(idxed, 1)
                dve.wait_ge(got, 16)
                v.tensor_copy(q[:, :], first[:, 0:C1])

                def body(it, isfirst):
                    for s in range(RING):
                        r = ring.rows
                        seg_masks(v, K.by_src.keep, block_cols(it, s), kb, mk=mk)
                        dve.wait_ge(ring.gathered[s], (it + 1) * TB * 16)
                        v.tensor_tensor(own[:, :, :], r[:, s, :, 0:C1], mk[:, :].unsqueeze(2).to_broadcast([P, TB, C1]), ALU.mult)
                        v.drain()
                        for f in range(C1):
                            v.tensor_tensor_scan(own[:, :, f], kb[:, :], own[:, :, f], q[:, f:f + 1], ALU.mult, ALU.add)
                        v.drain()
                        v.tensor_copy(q[:, :], own[:, TB - 1, :])
                        v.tensor_tensor(prod[:, :, :], own[:, :, 0:D], r[:, s, :, 0:D], ALU.mult)
                        v.tensor_tensor(nn[:, :], own[:, :, D], r[:, s, :, D], ALU.mult)
                        v.drain()
                        v.tensor_reduce(dot[:, :], prod[:, :, :], AX.X, ALU.add)
                        v.tensor_scalar(nn[:, :], nn[:, :], 1e-8, None, ALU.max)
                        v.drain()
                        v.reciprocal(nn[:, :], nn[:, :])
                        v.drain()
                        v.tensor_tensor(dot[:, :], dot[:, :], nn[:, :], ALU.mult)
                        v.drain()
                        v.tensor_scalar(neg[:, :], dot[:, :], 0.0, K.co[:, 1:2], ALU.min, ALU.mult)
                        v.tensor_scalar(nn[:, :], dot[:, :], 0.0, K.co[:, 0:1], ALU.max, ALU.mult)
                        v.drain()
                        v.tensor_tensor(dot[:, :], nn[:, :], neg[:, :], ALU.add)
                        v.tensor_copy(bb[:, :], K.base[:, block_cols(it, s)])
                        v.drain()
                        v.tensor_tensor(dot[:, :], dot[:, :], bb[:, :], ALU.mult)
                        v.drain()
                        if not isfirst:
                            dve.wait_ge(stored[s], it * 16)
                        v.tensor_tensor(sums[:, s], r[:, s, :, 0:D], dot[:, :].unsqueeze(2).to_broadcast([P, TB, D]), ALU.mult).then_inc(freed[s], 1)
                        v.drain()
                        for f in range(D):
                            v.tensor_tensor_scan(sums[:, s, :, f], kb[:, :], sums[:, s, :, f], K.st[:, f:f + 1], ALU.mult, ALU.add)
                        v.drain().then_inc(scanned[s], 1)
                        v.tensor_copy(K.st[:, :], sums[:, s, TB - 1, :])
                rounds(dve, body)


def layer3_finish(K):
    nc = K.nc
    with Phase(K, "l3f") as ph:
        res = ph.sb("res", [P, NT, D])
        has = ph.sb("has", [P, NT])
        done, stored = ph.sems("done", "stored")
        collect(K, K.by_src, K.sums3, D, res)
        with Step(nc) as block:
            @block.vector
            def _(dve):
                v = nc.vector
                v.tensor_scalar(has[:, :], K.by_src.cnt[:, :], 0.0, None, ALU.is_gt)
                v.tensor_scalar(K.wh[:, :, 0:D], K.wh[:, :, 0:D], K.co[:, 2:3], None, ALU.mult)
                v.drain()
                v.tensor_tensor(res[:, :, :], res[:, :, :], has[:, :].unsqueeze(2).to_broadcast([P, NT, D]), ALU.mult)
                v.drain()
                v.tensor_tensor(res[:, :, :], res[:, :, :], K.wh[:, :, 0:D], ALU.add)
                v.drain()
                v.scalar_tensor_tensor(K.x[:, :, :], res[:, :, :], K.co[:, 3:4], K.x[:, :, :], ALU.mult, ALU.add).then_inc(done, 1)

            @block.sync
            def _(sp):
                sp.wait_ge(done, 1)
                sp.dma_start(K.out[0:(NT - 1) * P, :].rearrange("(w p) d -> p w d", p=P), K.x[:, 0:NT - 1, :]).then_inc(stored, 16)
                sp.dma_start(K.out[(NT - 1) * P:N, :], K.x[0:N - (NT - 1) * P, NT - 1, :]).then_inc(stored, 16)
                sp.wait_ge(stored, 32)


def kernel(**inputs):
    import numpy as np
    import concourse.bacc as _bacc
    from concourse.bass_utils import run_bass_kernel_spmd as _run
    nc = _bacc.Bacc("TRN2", target_bir_lowering=False, num_devices=1)
    i = {k: np.ascontiguousarray(v) for k, v in inputs.items()}
    i32 = np.int32
    ids = np.arange(N, dtype=i32)
    pad = np.full(L - M, N, i32)
    rest = np.full(SORT_L - L, 4095, i32)
    arrays = {k: v for k, v in i.items() if k[0] == "L" or k == "x"}
    arrays["nodess"] = np.concatenate([ids, i["src"], pad, rest])
    arrays["nodesd"] = np.concatenate([ids, i["dst"], pad, rest])

    def rows(columns, other, width):
        body = np.concatenate([c.view(i32).reshape(E, -1) for c in columns] + [other.reshape(E, 1)], axis=1)
        r = np.zeros((L, width), i32)
        r[N:M, :body.shape[1]] = body
        r[:N, body.shape[1] - 1] = ids
        r[M:, body.shape[1] - 1] = N
        return r
    arrays["rec_s"] = rows([i["edge_attr_32"], i["edge_weight"], i["edge_weight_n2"]], i["dst"], R0)
    arrays["rec_d"] = rows([i["edge_attr_64"]], i["src"], RE)
    a = {k: nc.dram_tensor("in_" + k, v.shape, mybir.dt.from_np(v.dtype), kind="ExternalInput").ap()
         for k, v in arrays.items()}
    out = nc.dram_tensor("out_0", (N, D), F32, kind="ExternalOutput").ap()
    build(nc, a, out)
    r = _run(nc, [{"in_" + k: v for k, v in arrays.items()}], core_ids=[0])
    return r.results[0]["out_0"]
```

```python
import concourse.bass as bass
from concourse import mybir
from contextlib import ExitStack

F32 = mybir.dt.float32
BF16 = mybir.dt.bfloat16
I32 = mybir.dt.int32
ALU = mybir.AluOpType
ACT = mybir.ActivationFunctionType
AX = mybir.AxisListType

P = 128
N = 3125
E = 53125
NT = 25
NP = NT * P
M = N + E
J = 440
L = P * J
SORT_W = 512
SORT_L = P * SORT_W
CP = L // SORT_W
TB = 44
NBLK = J // TB
RING = 2
BIG = 3.4028235e38
KEY_ONE = 1 << 28
D = 64
H = 8
WIN = 16
NWIN = 196
ACC_W = 200
IB = 14
BODIES = 46
ITEMS = IB * BODIES
R0 = 36
RE = 66
R1 = 82
R2 = 128
R3 = 66


class Kern:
    pass


class Order:

    def __init__(self, name, sb, dram):
        self.name = name
        self.keep = sb("keep" + name, [P, J])
        self.node0 = sb("node0" + name, [P, 1], I32)
        self.fk = sb("fk" + name, [P, 1])
        self.nm = sb("nm" + name, [P, 1])
        self.cnt = sb("cnt" + name, [P, NT])
        self.end = sb("end" + name, [P, NT], I32)
        self.key = dram("key" + name, (SORT_L,), I32)
        self.ent = sb("ent" + name, [P, J], I32)
        self.other = sb("other" + name, [P, J], I32)
        self.endd = dram("endd" + name, (NP,))
        self.startd = dram("startd" + name, (NP,))
        self.cntd = dram("cntd" + name, (NP,))


def build(nc, a, out):
    top = ExitStack()
    with top:
        K = Kern()
        K.nc, K.a, K.out = nc, a, out
        K.semaphores = []

        def sb(n, s, d=F32):
            return top.enter_context(nc.sbuf_tensor(n, s, d))

        def dram(n, s, d=F32):
            return nc.dram_tensor(n, s, d, kind="Internal").ap()

        K.ident = sb("ident", [P, P])
        K.x = sb("x", [P, NT, D])
        K.hn = sb("hn", [P, NT, D])
        K.by_src = Order("s", sb, dram)
        K.by_dst = Order("d", sb, dram)
        K.meta = sb("meta", [P, J, 2], I32)
        K.st = sb("st", [P, D])
        K.nodes = sb("nodes", [P, J])
        K.keepc = sb("keepc", [CP, SORT_W])
        K.nxc = sb("nxc", [CP, 1])
        K.nmc = sb("nmc", [CP, 2])
        K.node0c = sb("node0c", [CP, 1], I32)
        K.nodec = sb("nodec", [CP, SORT_W])
        K.base = sb("base", [P, J])
        K.co = sb("co", [P, 5])
        K.co_parts = sb("co_parts", [P, 8])
        K.item_out = sb("item_out", [1, ITEMS], I32)
        K.body_w = sb("body_w", [1, BODIES], I32)
        K.item_slot = sb("item_slot", [1, ITEMS], I32)
        K.item_first = sb("item_first", [1, BODIES], I32)
        K.srct = sb("srct", [P, J], I32)
        K.cid = sb("cid", [P, SORT_W], I32)
        K.pcol = sb("pcol", [P, 1], I32)
        K.iot = sb("iot", [P, NP])
        K.lower = sb("lower", [NP // 64, NP // 64])
        K.sums0 = dram("sums0", (L, D))
        K.sums2 = dram("sums2", (L, D))
        K.sums3 = dram("sums3", (L, D))
        K.rowsd = dram("rowsd", (P, J, RE), I32)
        K.pairs = dram("pairs", (SORT_L,), I32)
        K.tab1 = dram("tab1", (NP, R1))
        K.tab2 = dram("tab2", (NP, R2))
        K.tab3 = dram("tab3", (NP, R3))
        K.g1 = dram("g1", (P, J, D + 1))

        sort_keys(K, "s", K.a["nodess"], K.by_src.key, first=True)
        layer0_pass(K)
        layer0_finish(K)
        with Phase(K, "ep") as ph:
            ring = Ring(ph, RE, I32)
            with nc.sbuf_tensor("F", [CP, H, SORT_W], F32) as K.F, \
                    nc.sbuf_tensor("item_rel", [P, ITEMS], F32) as K.item_rel, \
                    nc.sbuf_tensor("sel", [P, 4, ITEMS], F32) as K.sel:
                with nc.sbuf_tensor("atp", [P, J, 2 * H], F32) as K.atp:
                    layer1_gather(K)
                    layer1_softmax(K)
                edge_gathers(K, ph, ring)
                with nc.sbuf_tensor("acc", [P, ACC_W, D + 1], F32) as K.acc:
                    with nc.sbuf_tensor("item_ex", [P, H, ITEMS], F32) as K.item_ex:
                        layer1_spread(K)
                        layer1_sums(K)
                    layer1_finish(K)
            layer2_tables(K)
        renew_semaphores(K)
        layer2_gather(K)
        layer2_finish(K)
        with nc.sbuf_tensor("wh", [P, NT, R3], F32) as K.wh:
            layer3_gather(K)
            layer3_finish(K)


def renew_semaphores(K):
    K.nc.clear_and_free_semaphores(K.semaphores)
    K.nc.all_engine_barrier()
    K.semaphores = []


class Step:

    def __init__(self, nc, pool_ahead=False, meet=True):
        self.nc, self.pool_ahead, self.meet = nc, pool_ahead, meet

    def __enter__(self):
        return self

    def __exit__(self, kind, *rest):
        if kind is None and self.meet:
            ET = mybir.EngineType
            if self.pool_ahead:
                self.nc.multi_engine_barrier([ET.DVE, ET.Activation, ET.PE, ET.SP])
            else:
                self.nc.all_engine_barrier()

    def vector(self, program):
        program(self.nc.vector)

    def tensor(self, program):
        program(self.nc.tensor)

    def scalar(self, program):
        program(self.nc.scalar)

    def sync(self, program):
        program(self.nc.sync)

    def gpsimd(self, program):
        program(self.nc.gpsimd)


class Phase:

    def __init__(self, K, name):
        self.K, self.nc, self.name, self.st = K, K.nc, name, ExitStack()

    def __enter__(self):
        self.st.__enter__()
        return self

    def __exit__(self, *e):
        return self.st.__exit__(*e)

    def sb(self, n, s, d=F32):
        return self.st.enter_context(self.nc.sbuf_tensor(f"{self.name}_{n}", s, d))

    def ps(self, n, s=(P, 512), d=F32):
        return self.st.enter_context(self.nc.psum_tensor(f"{self.name}_{n}", list(s), d))

    def sem(self, n):
        s = self.nc.alloc_semaphore(name=f"{self.name}_{n}")
        self.K.semaphores.append(s)
        return s

    def sems(self, *names):
        return [self.sem(n) for n in names]


def sort_keys(K, name, nodes, key, first=False, pairs=False, alone=False):
    nc = K.nc
    W = SORT_W
    with Phase(K, "sort" + name) as ph:
        raw = ph.sb("raw", [P, W], I32)
        other = ph.sb("other", [P, 2, W], I32) if pairs else None
        X = [ph.sb("x0", [P, W]), ph.sb("x1", [P, W])]
        bits = ph.sb("bits", [P, 8], I32)
        sgn = ph.sb("sgn", [P, 8])
        flip = ph.sb("flip", [P, 8])
        neg = ph.sb("neg", [P, 1])
        turn_ps = [ph.ps(f"turn{i}") for i in range(2)]
        loaded, consts, cleared, step, turned, swapped, done_, stored = ph.sems(
            "loaded", "consts", "cleared", "step", "turned", "swapped", "done", "stored")
        swaps = []

        with Step(nc, pool_ahead=not first) as block:
            @block.gpsimd
            def _(pool):
                if first:
                    nc.gpsimd.iota(K.cid[:, :], [[1, W]], base=KEY_ONE, channel_multiplier=W)
                    nc.gpsimd.memset(K.x[:, NT - 1, :], 0.0).then_inc(cleared, 1)
                    nc.gpsimd.memset(K.ident[:, :], 0.0).then_inc(cleared, 1)
                    pool.wait_ge(cleared, 2)
                    nc.gpsimd.affine_select(out=K.ident[:, :], in_=K.ident[:, :], compare_op=ALU.not_equal, fill=1.0,
                                            base=0, pattern=[[-1, P]], channel_multiplier=1)
                    nc.gpsimd.iota(K.pcol[:, :], [[1, 1]], base=0, channel_multiplier=1).then_inc(consts, 1)
                    nc.gpsimd.iota(K.iot[:, :], [[1, NP]], base=0, channel_multiplier=0, allow_small_or_imprecise_dtypes=True)
                    nc.gpsimd.memset(K.lower[:, :], 0.0).then_inc(cleared, 1)
                    pool.wait_ge(cleared, 3)
                    nc.gpsimd.affine_select(out=K.lower[:, :], in_=K.lower[:, :], compare_op=ALU.is_ge, fill=1.0,
                                            base=0, pattern=[[-1, NP // 64]], channel_multiplier=1)

            @block.vector
            def _(dve):
                n = 0

                def did(ins):
                    nonlocal n
                    n += 1
                    ins.then_inc(step, 1)

                def settle():
                    dve.wait_ge(step, n)

                if first:
                    dve.wait_ge(consts, 1)
                dve.wait_ge(loaded, 48 if pairs else 16)
                for b in range(7):
                    did(nc.vector.tensor_scalar(bits[:, b:b + 1], K.pcol[:, :], b, 1, ALU.logical_shift_right, ALU.bitwise_and))
                did(nc.vector.tensor_scalar(raw[:, :], raw[:, :], 13 if pairs else 16, None, ALU.logical_shift_left))
                settle()
                did(nc.vector.tensor_scalar(sgn[:, 0:7], bits[:, 0:7], -2.0, 1.0, ALU.mult, ALU.add))
                did(nc.vector.memset(sgn[:, 7:8], 1.0))
                if pairs:
                    did(nc.vector.tensor_tensor(other[:, 0, :], other[:, 0, :], other[:, 1, :], ALU.bitwise_or))
                    settle()
                low = other[:, 0, :] if pairs else K.cid[:, :]
                did(nc.vector.tensor_tensor(X[0][:, :].bitcast(I32), raw[:, :], low, ALU.bitwise_or))
                settle()
                did(nc.vector.tensor_tensor(flip[:, 0:7], sgn[:, 1:8], sgn[:, 0:7], ALU.mult))
                did(nc.vector.tensor_scalar(neg[:, :], sgn[:, 0:1], -1.0, None, ALU.mult))
                settle()
                cur, spare = X
                for k in range(1, 17):
                    if k <= 8:
                        half = 2 ** (k - 1)
                        v = cur[:, :].rearrange("p (a x) -> p a x", x=4 * half)
                        part = v[:, :, 2 * half:] if k == 1 else v[:, :, half:3 * half]
                        did(nc.vector.tensor_scalar(part, part, -1.0, None, ALU.mult))
                    elif k == 9:
                        did(nc.vector.tensor_scalar(cur[:, 0:256], cur[:, 0:256], sgn[:, 0:1], None, ALU.mult))
                        did(nc.vector.tensor_scalar(cur[:, 256:512], cur[:, 256:512], neg[:, 0:1], None, ALU.mult))
                    else:
                        did(nc.vector.tensor_scalar(cur[:, :], cur[:, :], flip[:, k - 10:k - 9], None, ALU.mult))
                    settle()
                    for b in range(k - 1, -1, -1):
                        if k >= 10 and b in (k - 1, 8):
                            swaps.append((cur, spare, n))
                            if alone:
                                dve.wait_ge(turned, len(swaps))
                                did(nc.vector.tensor_copy(spare[:, :], turn_ps[(len(swaps) - 1) % 2][:, :]))
                                settle()
                            else:
                                dve.wait_ge(swapped, len(swaps))
                            cur, spare = spare, cur
                        d = 2 ** (b - 9) if b >= 9 else 2 ** b
                        s = cur[:, :].rearrange("p (a two d) -> p a two d", two=2, d=d)
                        t = spare[:, :].rearrange("p (a two d) -> p a two d", two=2, d=d)
                        did(nc.vector.tensor_tensor(t[:, :, 0, :], s[:, :, 0, :], s[:, :, 1, :], ALU.min))
                        did(nc.vector.tensor_tensor(t[:, :, 1, :], s[:, :, 0, :], s[:, :, 1, :], ALU.max))
                        settle()
                        cur, spare = spare, cur
                nc.vector.tensor_scalar(raw[:, :], cur[:, :].bitcast(I32), KEY_ONE - 1, None,
                                        ALU.bitwise_and).then_inc(done_, 1)

            @block.tensor
            def _(pe):
                if first:
                    pe.wait_ge(consts, 1)
                for m, (c, t, at) in enumerate(swaps):
                    pe.wait_ge(step, at)
                    for g in range(4):
                        last = nc.tensor.transpose(turn_ps[m % 2][:, g * P:(g + 1) * P], c[:, g * P:(g + 1) * P], K.ident[:, :])
                    last.then_inc(turned, 1)

            @block.scalar
            def _(act):
                for m, (c, t, at) in enumerate(() if alone else swaps):
                    act.wait_ge(turned, m + 1)
                    nc.scalar.copy(t[:, :], turn_ps[m % 2][:, :]).then_inc(swapped, 1)

            @block.sync
            def _(sp):
                sp.dma_start(raw[:, :], nodes.rearrange("(p f) -> p f", p=P)).then_inc(loaded, 16)
                if pairs:
                    sp.dma_start(other[:, 0, :], K.a["srcs"].rearrange("(p f) -> p f", p=P)).then_inc(loaded, 16)
                    sp.dma_start(other[:, 1, :], K.a["edge_bits"].rearrange("(p f) -> p f", p=P)).then_inc(loaded, 16)
                if first:
                    sp.dma_start(K.x[:, 0:NT - 1, :], K.a["x"][0:(NT - 1) * P, :].rearrange("(w p) d -> p w d", p=P)).then_inc(stored, 16)
                    sp.wait_ge(cleared, 2)
                    sp.dma_start(K.x[0:N - (NT - 1) * P, NT - 1, :], K.a["x"][(NT - 1) * P:N, :]).then_inc(stored, 16)
                sp.wait_ge(done_, 1)
                sp.dma_start(key.rearrange("(p f) -> p f", p=P), raw[:, :]).then_inc(stored, 16)
                sp.wait_ge(stored, 48 if first else 16)


def list_setup(K, by):
    nc = K.nc
    HI, LO = 50, 64
    with Phase(K, "set" + by.name) as ph:
        key = ph.sb("key", [P, J], I32)
        nxt = ph.sb("nxt", [P, 1], I32)
        nodei = ph.sb("nodei", [P, J], I32)
        lo_i = ph.sb("lo_i", [P, J], I32)
        node = ph.sb("node", [P, J])
        hi = ph.sb("hi", [P, J])
        lo = ph.sb("lo", [P, J])
        t0 = ph.sb("t0", [P, J])
        t1 = ph.sb("t1", [P, J])
        c = ph.sb("c", [P, 8])
        one_hi = ph.sb("one_hi", [P, 2, TB, HI], BF16)
        one_lo = ph.sb("one_lo", [P, 2, TB, LO], BF16)
        zero = ph.sb("zero", [P, LO], BF16)
        cnt = ph.sb("cnt", [HI, LO])
        run = ph.sb("run", [HI, LO])
        start = ph.sb("start", [HI, LO])
        ones = ph.sb("ones", [HI, LO])
        base = ph.sb("base", [HI, 1])
        endf = ph.sb("endf", [P, NT])
        hist = ph.ps("hist")
        basep = ph.ps("basep")
        loaded, hot, used, dn, d2, p2, stored, lded = ph.sems("loaded", "hot", "used", "dn", "d2", "p2", "stored", "lded")
        by.indexed = ph.sem("indexed")
        ent = by.ent
        pairs = by is K.by_dst
        kd = K.pairs if pairs else by.key
        keep, node0, fk, nm = by.keep, by.node0, by.fk, by.nm
        with Step(nc, pool_ahead=True) as block:
            @block.sync
            def _(sp):
                sp.dma_start(key[:, :], kd[0:L].rearrange("(p j) -> p j", p=P)).then_inc(loaded, 16)
                with nc.allow_non_contiguous_dma(reason="one value per partition"):
                    sp.dma_start(nxt[:, :], kd[J:J + L].rearrange("(p j) -> p j", p=P)[:, 0:1]).then_inc(loaded, 16)
                sp.wait_ge(d2, 1)
                sp.dma_start(by.endd.rearrange("(h l) -> h l", l=LO), run[:, :]).then_inc(stored, 16)
                sp.dma_start(by.startd.rearrange("(h l) -> h l", l=LO), start[:, :]).then_inc(stored, 16)
                sp.dma_start(by.cntd.rearrange("(h l) -> h l", l=LO), cnt[:, :]).then_inc(stored, 16)
                sp.wait_ge(stored, 48)
                ends = by.endd.rearrange("(w p) -> p w", p=P)
                counts = by.cntd.rearrange("(w p) -> p w", p=P)
                with nc.allow_non_contiguous_dma(reason="one value per node, once"):
                    sp.dma_start(endf[:, :], ends).then_inc(lded, 16)
                    sp.dma_start(by.cnt[:, 0:NT - 1], counts[:, 0:NT - 1]).then_inc(lded, 16)
                    sp.dma_start(by.cnt[0:N - (NT - 1) * P, NT - 1:], counts[0:N - (NT - 1) * P, NT - 1:]).then_inc(lded, 16)
                sp.wait_ge(lded, 48)

            @block.vector
            def _(dve):
                v = nc.vector
                v.memset(zero[:, :], 0.0).then_inc(dn, 1)
                v.memset(ones[:, :], 1.0)
                v.memset(by.cnt[:, :], 0.0)
                dve.wait_ge(loaded, 32)
                v.tensor_scalar(nodei[:, :], key[:, :], 13 if pairs else 16, None, ALU.logical_shift_right)
                if pairs:
                    v.tensor_scalar(ent[:, :], key[:, :], 12, 1, ALU.logical_shift_right, ALU.bitwise_and)
                    v.tensor_scalar(nxt[:, :], nxt[:, :], 12, 1, ALU.logical_shift_right, ALU.bitwise_and)
                    v.drain()
                else:
                    v.tensor_scalar(ent[:, :], key[:, :], 0xFFFF, None, ALU.bitwise_and)
                    v.tensor_scalar(nxt[:, :], nxt[:, :], 0xFFFF, None, ALU.bitwise_and)
                    v.drain().then_inc(by.indexed, 1)
                v.tensor_scalar(lo_i[:, :], nodei[:, :], 63, None, ALU.bitwise_and)
                v.tensor_copy(node[:, :], nodei[:, :])
                v.tensor_scalar(t0[:, :], ent[:, :], 1.0 if pairs else float(N), None, ALU.is_ge)
                v.tensor_scalar(t1[:, :], ent[:, :], float(M), None, ALU.is_lt)
                v.tensor_scalar(c[:, 0:1], nxt[:, :], 1.0 if pairs else float(N), None, ALU.is_ge)
                v.tensor_scalar(c[:, 1:2], nxt[:, :], float(M), None, ALU.is_lt)
                v.drain()
                v.tensor_scalar(nodei[:, :], nodei[:, :], 6, None, ALU.logical_shift_right)
                v.tensor_copy(lo[:, :], lo_i[:, :])
                v.tensor_tensor(keep[:, :], t0[:, :], t1[:, :], ALU.mult)
                v.tensor_tensor(c[:, 2:3], c[:, 0:1], c[:, 1:2], ALU.mult)
                v.tensor_tensor(c[:, 3:4], node[:, 0:1], node[:, J - 1:J], ALU.is_equal)
                v.tensor_copy(node0[:, :], node[:, 0:1])
                if by is K.by_src:
                    v.tensor_copy(K.nodes[:, :], node[:, :])
                v.drain()
                v.tensor_copy(hi[:, :], nodei[:, :])
                v.tensor_tensor(nm[:, :], keep[:, 0:1], c[:, 3:4], ALU.mult)
                v.drain()
                v.tensor_tensor(c[:, 4:5], nm[:, :], c[:, 2:3], ALU.mult)
                v.drain()
                v.tensor_scalar(c[:, 5:6], c[:, 4:5], -1.0, 1.0, ALU.mult, ALU.add)
                v.tensor_scalar(c[:, 6:7], node[:, 0:1], 1.0, None, ALU.add)
                v.drain()
                v.tensor_tensor(c[:, 5:6], c[:, 5:6], keep[:, 0:1], ALU.mult)
                v.drain()
                v.tensor_tensor(c[:, 5:6], c[:, 5:6], c[:, 6:7], ALU.mult)
                v.drain()
                v.tensor_scalar(fk[:, :], c[:, 5:6], -1.0, None, ALU.add)
                with dve.Fori(0, NBLK // 2) as it:
                    for s in range(2):
                        dve.wait_ge(used, it * 2 + s + 1)
                        js = bass.ds((it * 2 + s) * TB, TB)
                        v.tensor_tensor(one_hi[:, s], hi[:, js].unsqueeze(2).to_broadcast([P, TB, HI]),
                                        K.iot[:, 0:HI].unsqueeze(1).to_broadcast([P, TB, HI]), ALU.is_equal)
                        v.tensor_tensor(one_lo[:, s], lo[:, js].unsqueeze(2).to_broadcast([P, TB, LO]),
                                        K.iot[:, 0:LO].unsqueeze(1).to_broadcast([P, TB, LO]), ALU.is_equal).then_inc(hot, 1)
                dve.wait_ge(p2, 1)
                v.tensor_copy(cnt[:, :], hist[0:HI, 0:LO])
                v.drain()
                v.tensor_tensor_scan(run[:, :], ones[:, :], cnt[:, :], 0.0, ALU.mult, ALU.add)
                v.drain().then_inc(dn, 1)
                dve.wait_ge(p2, 2)
                v.tensor_copy(base[:, :], basep[0:HI, 0:1])
                v.drain()
                v.tensor_scalar(run[:, :], run[:, :], base[:, :], -1.0, ALU.add, ALU.add)
                v.drain()
                v.tensor_tensor(start[:, :], run[:, :], cnt[:, :], ALU.subtract)
                v.drain()
                v.tensor_scalar(start[:, :], start[:, :], 1.0, None, ALU.add)
                v.tensor_scalar(cnt[:, :], cnt[:, :], -1.0, 0.0, ALU.add, ALU.max)
                v.drain().then_inc(d2, 1)
                dve.wait_ge(lded, 48)
                v.tensor_copy(by.end[:, :], endf[:, :])

            @block.tensor
            def _(pe):
                pe.wait_ge(dn, 1)
                nc.tensor.matmul(hist[0:HI, 0:LO], zero[:, 0:HI], zero[:, :], start=True, stop=False).then_inc(used, 2)
                with pe.Fori(0, NBLK // 2) as it:
                    for s in range(2):
                        pe.wait_ge(hot, it * 2 + s + 1)
                        for j in range(TB):
                            last = nc.tensor.matmul(hist[0:HI, 0:LO], one_hi[:, s, j, :], one_lo[:, s, j, :],
                                                    start=False, stop=False)
                        last.then_inc(used, 1)
                nc.tensor.matmul(hist[0:HI, 0:LO], zero[:, 0:HI], zero[:, :], start=False, stop=True).then_inc(p2, 1)
                pe.wait_ge(dn, 2)
                nc.tensor.matmul(basep[0:HI, 0:1], K.lower[:, :], run[:, LO - 1:LO], start=True, stop=True).then_inc(p2, 1)


def rounds(engine, body, n=None):
    body(0, True)
    with engine.Fori(1, n or NBLK // RING) as it:
        body(it, False)


class Ring:

    def __init__(self, ph, width, dt=F32, size=RING, rows=True):
        self.size = size
        self.rows = ph.sb("rows", [P, size, TB, width], dt) if rows else None
        self.idx = ph.sb("ring_idx", [P, size, TB], I32)
        self.indexed = ph.sem("indexed")
        self.gathered = [ph.sem(f"gathered{s}") for s in range(size)]
        self.begun = ph.sem("begun")


def block_cols(it, s, size=RING):
    return bass.ds((it * size + s) * TB, TB)


def gather_rounds(nc, pool, ring, table, idx, freed, taken=None):
    def body(it, first):
        for s in range(ring.size):
            if not first:
                pool.wait_ge(ring.gathered[s], it * TB * 16)
            if taken is None:
                new = idx[:, block_cols(it, s, ring.size)]
            else:
                fetched, records = taken
                pool.wait_ge(fetched[s], (it + 1) * 16)
                pool.sem_inc(ring.begun, 1)
                new = records[:, s, :, D]
            nc.gpsimd.tensor_copy(ring.idx[:, s, :], new).then_inc(ring.indexed, 1)
            pool.wait_ge(ring.indexed, it * ring.size + s + 1)
            if not first:
                for sem, per in freed:
                    pool.wait_ge(sem[s], it * per)
            pool.sem_inc(ring.begun, 1)
            for j in range(TB):
                nc.gpsimd.indirect_dma_start(
                    out=ring.rows[:, s, j, :], out_offset=None, in_=table,
                    in_offset=bass.IndirectOffsetOnAxis(ap=ring.idx[:, s, j:j + 1], axis=0)
                ).then_inc(ring.gathered[s], 16)
    rounds(pool, body, NBLK // ring.size)


def seg_masks(v, keep, js, kb, mb=None, nb=None, mk=None):
    v.tensor_copy(kb[:, :], keep[:, js])
    v.drain()
    if nb is not None:
        v.tensor_scalar(nb[:, :], kb[:, :], -1.0, BIG, ALU.add, ALU.mult)
    if mb is not None:
        v.tensor_scalar(mb[:, :], kb[:, :], 2.0, -1.0, ALU.mult, ALU.add)
        v.drain()
        v.tensor_scalar(mb[:, :], mb[:, :], BIG, None, ALU.mult)
    if mk is not None:
        v.tensor_scalar(mk[:, :], kb[:, :], -1.0, 1.0, ALU.mult, ALU.add)
    v.drain()


def layer0_pass(K):
    nc = K.nc
    half = D // 2
    with Phase(K, "l0g") as ph:
        rows = ph.sb("rows", [P, J, R0], I32)
        gathered = [ph.sem(f"gathered{b}") for b in range(NBLK)]
        begun = ph.sem("begun")
        list_setup(K, K.by_src)
        with Step(nc, pool_ahead=True) as block:
            @block.gpsimd
            def _(pool):
                pool.wait_ge(K.by_src.indexed, 1)
                pool.sem_inc(begun, 1)
                for j in range(J):
                    nc.gpsimd.indirect_dma_start(
                        out=rows[:, j, :], out_offset=None, in_=K.a["rec_s"],
                        in_offset=bass.IndirectOffsetOnAxis(ap=K.by_src.ent[:, j:j + 1], axis=0)
                    ).then_inc(gathered[j // TB], 16)
        sort_keys(K, "p", K.a["nodesd"], K.pairs, pairs=True)
        list_setup(K, K.by_dst)
        src_to_tiles(K)
        with Phase(K, "l0s") as ph:
            sums = ph.sb("sums", [P, RING, TB, D])
            kb = ph.sb("kb", [P, TB])
            mb = ph.sb("mb", [P, TB])
            nb = ph.sb("nb", [P, TB])
            scanned = [ph.sem(f"scanned{s}") for s in range(RING)]
            stored = [ph.sem(f"stored{s}") for s in range(RING)]
            out = K.sums0.rearrange("(p j) d -> p j d", p=P)
            with Step(nc, pool_ahead=True) as block:
                @block.sync
                def _(sp):
                    def body(it, first):
                        for s in range(RING):
                            sp.wait_ge(scanned[s], it + 1)
                            sp.dma_start(out[:, block_cols(it, s), :], sums[:, s]).then_inc(stored[s], 16)
                    rounds(sp, body)
                    for s in range(RING):
                        sp.wait_ge(stored[s], NBLK // RING * 16)

                @block.scalar
                def _(act):
                    for b in range(NBLK):
                        act.wait_ge(gathered[b], TB * 16)
                    nc.scalar.copy(K.by_src.other[:, :], rows[:, :, half + 2])
                    nc.scalar.copy(K.meta[:, :, :], rows[:, :, half:half + 2])

                @block.vector
                def _(dve):
                    v = nc.vector
                    v.memset(K.st[:, 0:half], 0.0)
                    v.memset(K.st[:, half:D], -BIG)
                    for b in range(NBLK):
                        s, js = b % RING, slice(b * TB, (b + 1) * TB)
                        r = rows[:, js, 0:half].bitcast(F32)
                        dve.wait_ge(gathered[b], TB * 16)
                        if b >= RING:
                            dve.wait_ge(stored[s], b // RING * 16)
                        seg_masks(v, K.by_src.keep, js, kb, mb=mb, nb=nb)
                        for f in range(half):
                            v.tensor_tensor_scan(sums[:, s, :, f], kb[:, :], r[:, :, f], K.st[:, f:f + 1], ALU.mult, ALU.add)
                        v.drain()
                        v.tensor_tensor(r, r, nb[:, :].unsqueeze(2).to_broadcast([P, TB, half]), ALU.add)
                        v.drain()
                        for f in range(half):
                            v.tensor_tensor_scan(sums[:, s, :, half + f], mb[:, :], r[:, :, f], K.st[:, half + f:half + f + 1],
                                                 ALU.min, ALU.max)
                        v.drain().then_inc(scanned[s], 1)
                        v.tensor_copy(K.st[:, :], sums[:, s, TB - 1, :])
                        v.drain()


def collect(K, by, table, nsum, res, pool_ahead=False):
    nc = K.nc
    with Phase(K, "col" + table.tensor.name) as ph:
        sel = ph.sb("sel", [P, NP])
        nmb = ph.sb("nmb", [P, D])
        act = ph.sb("act", [P, 1])
        nmt = ph.sb("nmt", [D, P])
        tot = ph.sb("tot", [D, P])
        shf = ph.sb("shf", [D, P])
        car = ph.sb("car", [P, D + 1])
        has = ph.sb("has", [P, NT])
        tmp = ph.sb("tmp", [P, NT, D + 1])
        nmp = ph.ps("nmp")
        stp = ph.ps("stp")
        bp = [ph.ps(f"bp{i}") for i in range(4)]
        ready, begun, made, pm, got = ph.sems("ready", "begun", "made", "pm", "got")
        nm, fk, end = by.nm, by.fk, by.end
        with Step(nc, pool_ahead) as block:
            @block.gpsimd
            def _(pool):
                pool.wait_ge(ready, 1)
                pool.sem_inc(begun, 1)
                for w in range(NT):
                    nc.gpsimd.indirect_dma_start(out=res[:, w, :], out_offset=None, in_=table,
                                                 in_offset=bass.IndirectOffsetOnAxis(ap=end[:, w:w + 1], axis=0)).then_inc(got, 16)

            @block.tensor
            def _(pe):
                pe.wait_ge(made, 1)
                nc.tensor.matmul(nmp[0:D, 0:P], nmb[:, :], K.ident[:, :], start=True, stop=True)
                nc.tensor.transpose(stp[0:D, 0:P], K.st[:, :], K.ident[:, :]).then_inc(pm, 1)
                pe.wait_ge(made, 2)
                nc.tensor.transpose(stp[:, P:P + D], shf[:, :], K.ident[0:D, 0:D]).then_inc(pm, 1)
                pe.wait_ge(made, 3)
                for w in range(NT):
                    last = nc.tensor.matmul(bp[w // 7][:, w % 7 * (D + 1):(w % 7 + 1) * (D + 1)], sel[:, w * P:(w + 1) * P], car[:, :],
                                            start=True, stop=True)
                last.then_inc(pm, 1)

            @block.vector
            def _(dve):
                v = nc.vector
                v.sem_inc(ready, 1)
                v.tensor_copy(nmb[:, :], nm[:, 0:1].to_broadcast([P, D]))
                v.tensor_scalar(act[:, :], fk[:, :], 0.0, None, ALU.is_ge)
                v.memset(shf[:, 0:1], 0.0)
                v.memset(car[:, D:D + 1], 1.0)
                v.drain().then_inc(made, 1)
                dve.wait_ge(pm, 1)
                v.tensor_copy(nmt[:, :], nmp[0:D, 0:P])
                v.drain()
                if nsum < D:
                    v.tensor_scalar(nmt[nsum:, :], nmt[nsum:, :], 2.0, -1.0, ALU.mult, ALU.add)
                    v.drain()
                    v.tensor_scalar(nmt[nsum:, :], nmt[nsum:, :], BIG, None, ALU.mult)
                    v.drain()
                    v.tensor_tensor_scan(tot[nsum:, :], nmt[nsum:, :], stp[nsum:D, 0:P], -BIG, ALU.min, ALU.max)
                v.tensor_tensor_scan(tot[0:nsum, :], nmt[0:nsum, :], stp[0:nsum, 0:P], 0.0, ALU.mult, ALU.add)
                v.drain()
                v.tensor_copy(shf[:, 1:P], tot[:, 0:P - 1])
                v.drain().then_inc(made, 1)
                v.tensor_scalar(sel[:, :], K.iot[:, :], fk[:, 0:1], None, ALU.is_equal)
                dve.wait_ge(pm, 2)
                v.tensor_scalar(car[:, 0:D], stp[:, P:P + D], act[:, 0:1], None, ALU.mult)
                v.drain().then_inc(made, 1)
                dve.wait_ge(got, NT * 16)
                dve.wait_ge(pm, 3)
                for g in range(4):
                    w0, w1 = 7 * g, min(7 * g + 7, NT)
                    b = bp[g][:, 0:(w1 - w0) * (D + 1)].rearrange("p (w d) -> p w d", d=D + 1)
                    v.tensor_tensor(res[:, w0:w1, 0:nsum], res[:, w0:w1, 0:nsum], b[:, :, 0:nsum], ALU.add)
                    if nsum < D:
                        v.tensor_copy(tmp[:, w0:w1, nsum:], b[:, :, nsum:])
                if nsum < D:
                    v.drain()
                    v.tensor_scalar(has[:, :], tmp[:, :, D], -1.0, BIG, ALU.add, ALU.mult)
                    v.drain()
                    v.tensor_tensor(tmp[:, :, nsum:D], tmp[:, :, nsum:D], has[:, :].unsqueeze(2).to_broadcast([P, NT, D - nsum]), ALU.add)
                    v.drain()
                    v.tensor_tensor(res[:, :, nsum:], res[:, :, nsum:], tmp[:, :, nsum:D], ALU.max)


def node_dense(K, name, feat, F, w1, hid, func, b1, w2, put, w1d=None, pool_ahead=False):
    nc = K.nc
    groups = [(w, min(4, NT - w)) for w in range(0, NT, 4)]
    n_groups = len(groups)
    with Phase(K, name) as ph:
        W1 = ph.sb("W1", [F, hid]) if w1 is not None else w1d
        W2 = ph.sb("W2", [hid, D]) if w2 is not None else None
        B1 = ph.sb("B1", [hid, 1]) if w2 is not None else None
        ft = ph.sb("ft", [F, 2, 4 * P])
        ht = ph.sb("ht", [hid, 2, 4 * P])
        pa, pb, pc = ([ph.ps(f"{n}{i}") for i in range(2)] for n in "abc")
        loaded, turned, moved, first, acted, second, used = ph.sems(
            "loaded", "turned", "moved", "first", "acted", "second", "used")
        two = w2 is not None
        nl = (w1 is not None) + 2 * two
        C = D if two else hid
        with Step(nc, pool_ahead) as block:
            @block.sync
            def _(sp):
                if w1 is not None:
                    sp.dma_start(W1[:, :], w1).then_inc(loaded, 16)
                if two:
                    sp.dma_start(W2[:, :], w2).then_inc(loaded, 16)
                    with nc.allow_non_contiguous_dma(reason="a bias as a column"):
                        sp.dma_start(B1[:, :], b1.unsqueeze(1)).then_inc(loaded, 16)
                if nl:
                    sp.wait_ge(loaded, 16 * nl)

            @block.tensor
            def _(pe):
                for t in range(n_groups + 2):
                    if t < n_groups:
                        w, n = groups[t]
                        if t >= 2:
                            pe.wait_ge(moved, t - 1)
                        for k in range(n):
                            last = nc.tensor.transpose(pa[t % 2][0:F, k * P:(k + 1) * P], feat[:, w + k, :], K.ident[:, :])
                        last.then_inc(turned, 1)
                    if t == 1 and nl:
                        pe.wait_ge(loaded, 16 * nl)
                    if 1 <= t <= n_groups:
                        u = t - 1
                        n = groups[u][1]
                        pe.wait_ge(moved, u + 1)
                        if two:
                            if u >= 2:
                                pe.wait_ge(acted, u - 1)
                            nc.tensor.matmul(pb[u % 2][0:hid, 0:n * P], W1[:, :], ft[:, u % 2, 0:n * P], start=True, stop=True).then_inc(first, 1)
                        else:
                            if u >= 2:
                                pe.wait_ge(used, u - 1)
                            for k in range(n):
                                last = nc.tensor.matmul(pc[u % 2][:, k * C:(k + 1) * C], ft[:, u % 2, k * P:(k + 1) * P], W1[:, :],
                                                        start=True, stop=True)
                            last.then_inc(second, 1)
                    if two and t >= 2:
                        u = t - 2
                        pe.wait_ge(acted, u + 1)
                        if u >= 2:
                            pe.wait_ge(used, u - 1)
                        for k in range(groups[u][1]):
                            last = nc.tensor.matmul(pc[u % 2][:, k * C:(k + 1) * C], ht[:, u % 2, k * P:(k + 1) * P], W2[:, :],
                                                    start=True, stop=True)
                        last.then_inc(second, 1)

            @block.scalar
            def _(act):
                for t in range(n_groups + 1):
                    if t < n_groups:
                        n = groups[t][1]
                        act.wait_ge(turned, t + 1)
                        if t >= 2:
                            act.wait_ge(first if two else second, t - 1)
                        nc.scalar.copy(ft[:, t % 2, 0:n * P], pa[t % 2][0:F, 0:n * P]).then_inc(moved, 1)
                    if two and t == 1:
                        act.wait_ge(loaded, 16 * nl)
                    if two and t >= 1:
                        u = t - 1
                        n = groups[u][1]
                        act.wait_ge(first, u + 1)
                        if u >= 2:
                            act.wait_ge(second, u - 1)
                        nc.scalar.activation(ht[:, u % 2, 0:n * P], pb[u % 2][0:hid, 0:n * P], func, bias=B1[:, 0:1]).then_inc(acted, 1)

            @block.vector
            def _(dve):
                for t, (w, n) in enumerate(groups):
                    dve.wait_ge(second, t + 1)
                    put(nc.vector, slice(w, w + n), pc[t % 2][:, 0:n * C].rearrange("p (w c) -> p w c", c=C)).then_inc(used, 1)


def normalise(K, name, pool_ahead=False):
    nc = K.nc
    with Phase(K, name) as ph:
        mean = ph.sb("mean", [P, NT])
        var = ph.sb("var", [P, NT])
        sq = ph.sb("sq", [P, NT, D])
        d1, rooted = ph.sems("d1", "rooted")
        with Step(nc, pool_ahead) as block:
            @block.vector
            def _(dve):
                v = nc.vector
                wide = lambda t: t[:, :].unsqueeze(2).to_broadcast([P, NT, D])
                v.tensor_reduce(mean[:, :], K.x[:, :, :], AX.X, ALU.add)
                v.drain()
                v.tensor_scalar(mean[:, :], mean[:, :], 1.0 / D, None, ALU.mult)
                v.drain()
                v.tensor_tensor(K.hn[:, :, :], K.x[:, :, :], wide(mean), ALU.subtract)
                v.drain()
                v.tensor_tensor(sq[:, :, :], K.hn[:, :, :], K.hn[:, :, :], ALU.mult)
                v.drain()
                v.tensor_reduce(var[:, :], sq[:, :, :], AX.X, ALU.add)
                v.drain()
                v.tensor_scalar(var[:, :], var[:, :], 1.0 / D, 1e-5, ALU.mult, ALU.add)
                v.drain().then_inc(d1, 1)
                dve.wait_ge(rooted, 1)
                v.reciprocal(var[:, :], var[:, :])
                v.drain()
                v.tensor_tensor(K.hn[:, :, :], K.hn[:, :, :], wide(var), ALU.mult)
                v.drain()
                v.tensor_scalar(K.hn[:, :, :], K.hn[:, :, :], 0.0, None, ALU.max)

            @block.scalar
            def _(act):
                act.wait_ge(d1, 1)
                nc.scalar.sqrt(var[:, :], var[:, :]).then_inc(rooted, 1)


def layer0_finish(K):
    nc = K.nc
    with Phase(K, "l0f") as ph:
        res = ph.sb("res", [P, NT, D])
        feat = ph.sb("feat", [P, NT, 97])
        b2 = ph.sb("b2", [P, D])
        u0 = ph.sb("u0", [P, 1])
        m = ph.sb("m", [P, NT, 2])
        loaded = ph.sem("loaded")
        collect(K, K.by_src, K.sums0, D // 2, res, True)
        half = D // 2
        with Step(nc, True) as block:
            @block.sync
            def _(sp):
                sp.dma_start(b2[:, :], K.a["L0_gnn_b2"].unsqueeze(0).to_broadcast([P, D])).then_inc(loaded, 16)
                sp.dma_start(u0[:, :], K.a["L0_gnn_u"][0:1, :].to_broadcast([P, 1])).then_inc(loaded, 16)

            @block.vector
            def _(dve):
                v = nc.vector
                dve.wait_ge(loaded, 32)
                wide = lambda t, n: t.unsqueeze(2).to_broadcast([P, NT, n])
                v.tensor_scalar(m[:, :, 0], K.by_src.cnt[:, :], 1.0, None, ALU.max)
                v.tensor_scalar(m[:, :, 1], K.by_src.cnt[:, :], 0.0, None, ALU.is_gt)
                v.tensor_tensor(K.x[:, :, :], K.x[:, :, :], b2[:, :].unsqueeze(1).to_broadcast([P, NT, D]), ALU.add)
                v.drain()
                v.reciprocal(m[:, :, 0], m[:, :, 0])
                v.tensor_tensor(feat[:, :, 0:half], res[:, :, 0:half], wide(m[:, :, 1], half), ALU.mult)
                v.tensor_tensor(feat[:, :, half:D], res[:, :, half:D], wide(m[:, :, 1], half), ALU.mult)
                v.tensor_copy(feat[:, :, 96], u0[:, 0:1].to_broadcast([P, NT]))
                v.drain()
                v.tensor_tensor(feat[:, :, D:96], feat[:, :, 0:half], wide(m[:, :, 0], half), ALU.mult)

        def put(v, w, ps):
            return v.tensor_tensor(K.x[:, w, :], K.x[:, w, :], ps, ALU.add)
        node_dense(K, "l0m", feat, 97, K.a["L0_gnn_W1"], 128, ACT.Relu, K.a["L0_gnn_b1"], K.a["L0_gnn_W2"], put, pool_ahead=True)
    normalise(K, "n1", True)
    with Phase(K, "t1") as ph:
        W = ph.sb("W", [D, H, D])
        at = ph.sb("at", [D, 2, H, D])
        V = ph.sb("V", [D, 2 * H])
        pr = ph.sb("pr", [D, 2, H, D])
        tab = ph.sb("tab", [P, NT, R1])
        loaded = ph.sem("loaded")
        with Step(nc, True) as block:
            @block.sync
            def _(sp):
                sp.dma_start(W[:, :, :], K.a["L1_gnn_W"].rearrange("k (h c) -> k h c", h=H)).then_inc(loaded, 16)
                for i, n in enumerate(("L1_gnn_att_src", "L1_gnn_att_dst")):
                    sp.dma_start(at[:, i], K.a[n].unsqueeze(0).to_broadcast([D, H, D])).then_inc(loaded, 16)

            @block.vector
            def _(dve):
                v = nc.vector
                v.tensor_copy(tab[:, :, 0:D], K.hn[:, :, :])
                v.memset(tab[:, :, D:D + 1], 1.0)
                v.memset(tab[:, :, D + 17:], 0.0)
                dve.wait_ge(loaded, 48)
                for i in range(2):
                    v.tensor_tensor(pr[:, i], at[:, i], W[:, :, :], ALU.mult)
                v.drain()
                for i in range(2):
                    v.tensor_reduce(V[:, i * H:(i + 1) * H], pr[:, i], AX.X, ALU.add)

        def put(v, w, ps):
            return v.tensor_copy(tab[:, w, D + 1:D + 17], ps)
        node_dense(K, "t1m", K.hn, D, None, 2 * H, None, None, None, put, w1d=V, pool_ahead=True)
        store_table(K, K.tab1, tab)


def store_table(K, table, tab, pool_ahead=False):
    nc = K.nc
    with Phase(K, "st" + table.tensor.name) as ph:
        stored = ph.sem("stored")
        with Step(nc, pool_ahead) as block:
            @block.sync
            def _(sp):
                sp.dma_start(table.rearrange("(w p) r -> p w r", p=P), tab[:, :, :]).then_inc(stored, 16)
                sp.wait_ge(stored, 16)


def edge_gathers(K, ph, ring):
    nc = K.nc
    stored = [ph.sem(f"stored{s}") for s in range(RING)]
    with Step(nc, meet=False) as block:
        @block.gpsimd
        def _(pool):
            def store(it, s):
                pool.wait_ge(ring.gathered[s], (it + 1) * TB * 16)
                nc.gpsimd.dma_start(K.rowsd[:, block_cols(it, s), :], ring.rows[:, s]).then_inc(stored[s], 16)

            def gather(it, s, first):
                nc.gpsimd.tensor_copy(ring.idx[:, s, :], K.by_dst.ent[:, block_cols(it, s)]).then_inc(ring.indexed, 1)
                pool.wait_ge(ring.indexed, it * RING + s + 1)
                if not first:
                    pool.wait_ge(stored[s], it * 16)
                pool.sem_inc(ring.begun, 1)
                for j in range(TB):
                    nc.gpsimd.indirect_dma_start(
                        out=ring.rows[:, s, j, :], out_offset=None, in_=K.a["rec_d"],
                        in_offset=bass.IndirectOffsetOnAxis(ap=ring.idx[:, s, j:j + 1], axis=0)
                    ).then_inc(ring.gathered[s], 16)

            pool.wait_ge(K.by_dst.indexed, 1)
            gather(0, 0, True)
            gather(0, 1, True)
            store(0, 0)
            with pool.Fori(1, NBLK // RING) as it:
                gather(it, 0, False)
                store(it - 1, 1)
                gather(it, 1, False)
                store(it, 0)
            store(NBLK // RING - 1, 1)
            for s in range(RING):
                pool.wait_ge(stored[s], NBLK // RING * 16)


def src_to_tiles(K):
    nc = K.nc
    with Phase(K, "s2t") as ph:
        keyc = ph.sb("keyc", [CP, SORT_W], I32)
        nodei = ph.sb("nodei", [CP, SORT_W], I32)
        srci = ph.sb("srci", [CP, SORT_W], I32)
        srcf = ph.sb("srcf", [CP, SORT_W])
        nxt = ph.sb("nxt", [CP, 1], I32)
        same = ph.sb("same", [CP, 1])
        turn = ph.ps("turn")
        loaded, ready, turned = ph.sems("loaded", "ready", "turned")
        with Step(nc, True) as block:
            @block.sync
            def _(sp):
                sp.dma_start(keyc[:, :], K.pairs[0:L].rearrange("(p j) -> p j", p=CP)).then_inc(loaded, 16)
                with nc.allow_non_contiguous_dma(reason="one value per partition"):
                    sp.dma_start(nxt[:, :], K.pairs[SORT_W:SORT_W + L].rearrange("(p j) -> p j", p=CP)[:, 0:1]).then_inc(loaded, 16)

            @block.vector
            def _(dve):
                v = nc.vector
                dve.wait_ge(loaded, 32)
                v.tensor_scalar(nodei[:, :], keyc[:, :], 13, None, ALU.logical_shift_right)
                v.tensor_scalar(srci[:, :], keyc[:, :], 0xFFF, None, ALU.bitwise_and)
                v.tensor_scalar(nxt[:, :], nxt[:, :], 12, 1, ALU.logical_shift_right, ALU.bitwise_and)
                v.drain()
                v.tensor_scalar(keyc[:, :], keyc[:, :], 12, 1, ALU.logical_shift_right, ALU.bitwise_and)
                v.tensor_copy(K.nodec[:, :], nodei[:, :])
                v.tensor_copy(srcf[:, :], srci[:, :])
                v.drain().then_inc(ready, 1)
                v.tensor_copy(K.keepc[:, :], keyc[:, :])
                v.tensor_copy(K.nxc[:, :], nxt[:, :])
                v.tensor_tensor(same[:, :], K.nodec[:, 0:1], K.nodec[:, SORT_W - 1:], ALU.is_equal)
                v.tensor_copy(K.node0c[:, :], nodei[:, 0:1])
                v.drain()
                v.tensor_tensor(K.nmc[:, 0:1], K.keepc[:, 0:1], same[:, :], ALU.mult)
                v.tensor_tensor(K.nmc[:, 1:2], K.nxc[:, :], same[:, :], ALU.mult)
                dve.wait_ge(turned, 1)
                v.tensor_copy(K.srct[:, :].rearrange("q (p g) -> q g p", g=4),
                              turn[:, :].rearrange("q (g p) -> q g p", g=4)[:, :, 0:CP])

            @block.tensor
            def _(pe):
                pe.wait_ge(ready, 1)
                for g in range(4):
                    last = nc.tensor.transpose(turn[:, g * P:g * P + CP], srcf[:, g * P:(g + 1) * P], K.ident[0:CP, 0:CP])
                last.then_inc(turned, 1)


def layer1_gather(K):
    nc = K.nc
    with Phase(K, "l1g") as ph:
        ring = Ring(ph, R1)
        kept = [ph.sem(f"kept{s}") for s in range(RING)]
        stored = [ph.sem(f"stored{s}") for s in range(RING)]
        with Step(nc, True, meet=False) as block:
            @block.gpsimd
            def _(pool):
                gather_rounds(nc, pool, ring, K.tab1, K.srct, [(kept, 1), (stored, 16)])

            @block.scalar
            def _(act):
                def body(it, first):
                    for s in range(RING):
                        act.wait_ge(ring.gathered[s], (it + 1) * TB * 16)
                        act.dma_start(K.g1[:, block_cols(it, s), :], ring.rows[:, s, :, 0:D + 1]).then_inc(stored[s], 16)
                        nc.scalar.copy(K.atp[:, block_cols(it, s), :], ring.rows[:, s, :, D + 1:D + 17]).then_inc(kept[s], 1)
                rounds(act, body)
                for s in range(RING):
                    act.wait_ge(stored[s], NBLK // RING * 16)
        sort_keys(K, "e", K.a["nodesd"], K.by_dst.key, alone=True)
        edge_order(K)
        layer1_items(K)


def edge_order(K):
    nc = K.nc
    with Phase(K, "eo") as ph:
        key = ph.sb("key", [P, J], I32)
        loaded = ph.sem("loaded")
        with Step(nc, True, meet=False) as block:
            @block.sync
            def _(sp):
                sp.dma_start(key[:, :], K.by_dst.key[0:L].rearrange("(p j) -> p j", p=P)).then_inc(loaded, 16)

            @block.vector
            def _(dve):
                dve.wait_ge(loaded, 16)
                nc.vector.tensor_scalar(K.by_dst.ent[:, :], key[:, :], 0xFFFF, None, ALU.bitwise_and)
                nc.vector.drain().then_inc(K.by_dst.indexed, 1)


def layer1_softmax(K):
    nc = K.nc
    W = SORT_W
    with Phase(K, "l1s") as ph:
        A = ph.sb("A", [CP, 2 * H, W])
        F = K.F
        first = ph.sb("first", [P, R1])
        mk = ph.sb("mk", [CP, W])
        mb = ph.sb("mb", [CP, W])
        mr = ph.sb("mr", [CP, W])
        nmb = ph.sb("nmb", [CP, 2, H])
        nmt = ph.sb("nmt", [H, 2, CP])
        last = ph.sb("last", [CP, H])
        tot = ph.sb("tot", [H, CP])
        shf = ph.sb("shf", [H, CP])
        ini = ph.sb("ini", [CP, 2, H])
        bank = [ph.ps(f"bank{i}") for i in range(4)]
        small = ph.ps("small")
        turned, moved, got, made, crossed, ready, expd, begin, begun = ph.sems(
            "turned", "moved", "got", "made", "crossed", "ready", "expd", "begin", "begun")
        with Step(nc, True) as block:
            @block.gpsimd
            def _(pool):
                pool.wait_ge(begin, 1)
                pool.sem_inc(begun, 1)
                nc.gpsimd.indirect_dma_start(out=first[0:CP, :], out_offset=None, in_=K.tab1,
                                             in_offset=bass.IndirectOffsetOnAxis(ap=K.node0c[:, 0:1], axis=0)).then_inc(got, 16)

            @block.tensor
            def _(pe):
                for r in range(2 * H):
                    if r >= 4:
                        pe.wait_ge(moved, r - 3)
                    for g in range(4):
                        lt = nc.tensor.transpose(bank[r % 4][0:CP, g * P:(g + 1) * P], K.atp[:, g::4, r], K.ident[:, :])
                    lt.then_inc(turned, 1)
                pe.wait_ge(made, 1)
                for i in range(2):
                    nc.tensor.matmul(small[0:H, i * P:i * P + CP], nmb[:, i, :], K.ident[0:CP, 0:CP], start=True, stop=True)
                nc.tensor.transpose(small[0:H, 2 * P:2 * P + CP], last[:, :], K.ident[0:CP, 0:CP]).then_inc(crossed, 1)
                pe.wait_ge(made, 2)
                nc.tensor.transpose(small[0:CP, 3 * P:3 * P + H], shf[:, :], K.ident[0:H, 0:H]).then_inc(crossed, 1)
                pe.wait_ge(made, 3)
                nc.tensor.transpose(small[0:H, 2 * P:2 * P + CP], last[:, :], K.ident[0:CP, 0:CP]).then_inc(crossed, 1)
                pe.wait_ge(made, 4)
                nc.tensor.transpose(small[0:CP, 3 * P:3 * P + H], shf[:, :], K.ident[0:H, 0:H]).then_inc(crossed, 1)

            @block.scalar
            def _(act):
                for r in range(2 * H):
                    act.wait_ge(turned, r + 1)
                    nc.scalar.copy(A[:, r, :], bank[r % 4][0:CP, :]).then_inc(moved, 1)
                for h in range(H):
                    act.wait_ge(ready, h + 1)
                    nc.scalar.activation(F[:, h, :], F[:, h, :], ACT.Exp).then_inc(expd, 1)

            @block.vector
            def _(dve):
                v = nc.vector
                v.sem_inc(begin, 1)
                v.tensor_scalar(mk[:, :], K.keepc[:, :], -1.0, 1.0, ALU.mult, ALU.add)
                v.tensor_scalar(mb[:, :], K.keepc[:, :], 2.0, -1.0, ALU.mult, ALU.add)
                v.tensor_copy(nmb[:, :, :], K.nmc[:, :].unsqueeze(2).to_broadcast([CP, 2, H]))
                v.tensor_scalar(mr[:, W - 1:], K.nxc[:, :], 2.0, -1.0, ALU.mult, ALU.add)
                v.drain()
                v.tensor_scalar(mb[:, :], mb[:, :], BIG, None, ALU.mult)
                v.drain()
                v.tensor_copy(mr[:, 0:W - 1], mb[:, 1:W])
                v.tensor_scalar(mr[:, W - 1:], mr[:, W - 1:], BIG, None, ALU.mult)
                dve.wait_ge(moved, 2 * H)
                dve.wait_ge(got, 16)
                v.tensor_tensor(A[:, H:, :], A[:, H:, :], mk[:, :].unsqueeze(1).to_broadcast([CP, H, W]), ALU.mult)
                v.drain()
                for h in range(H):
                    v.tensor_tensor_scan(A[:, H + h, :], K.keepc[:, :], A[:, H + h, :], first[0:CP, D + 9 + h:D + 10 + h], ALU.mult, ALU.add)
                v.drain()
                v.tensor_tensor(A[:, 0:H, :], A[:, 0:H, :], A[:, H:, :], ALU.add)
                v.drain()
                v.scalar_tensor_tensor(A[:, 0:H, :], A[:, 0:H, :], 0.2, A[:, 0:H, :], ALU.mult, ALU.max)
                v.drain()
                for h in range(H):
                    v.tensor_tensor_scan(F[:, h, :], mb[:, :], A[:, h, :], -BIG, ALU.min, ALU.max)
                v.drain()
                v.tensor_copy(last[:, :], F[:, :, W - 1])
                v.drain().then_inc(made, 1)
                dve.wait_ge(crossed, 1)
                for i in range(2):
                    v.tensor_scalar(nmt[:, i, :], small[0:H, i * P:i * P + CP], 2.0, -1.0, ALU.mult, ALU.add)
                v.drain()
                v.tensor_scalar(nmt[:, :, :], nmt[:, :, :], BIG, None, ALU.mult)
                v.drain()
                v.tensor_tensor_scan(tot[:, :], nmt[:, 0, :], small[0:H, 2 * P:2 * P + CP], -BIG, ALU.min, ALU.max)
                v.memset(shf[:, 0:1], -BIG)
                v.drain()
                v.tensor_copy(shf[:, 1:CP], tot[:, 0:CP - 1])
                v.drain().then_inc(made, 1)
                dve.wait_ge(crossed, 2)
                v.tensor_copy(ini[:, 0, :], small[0:CP, 3 * P:3 * P + H])
                v.drain()
                for h in range(H):
                    v.tensor_tensor_scan(A[:, H + h, :], mb[:, :], A[:, h, :], ini[:, 0, h:h + 1], ALU.min, ALU.max)
                v.drain()
                for h in range(H):
                    v.tensor_tensor_scan(F[:, h, ::-1], mr[:, ::-1], A[:, H + h, ::-1], -BIG, ALU.min, ALU.max)
                v.drain()
                v.tensor_copy(last[:, :], F[:, :, 0])
                v.drain().then_inc(made, 1)
                dve.wait_ge(crossed, 3)
                v.tensor_tensor_scan(tot[:, ::-1], nmt[:, 1, ::-1], small[0:H, 2 * P:2 * P + CP][:, ::-1], -BIG, ALU.min, ALU.max)
                v.memset(shf[:, CP - 1:], -BIG)
                v.drain()
                v.tensor_copy(shf[:, 0:CP - 1], tot[:, 1:CP])
                v.drain().then_inc(made, 1)
                dve.wait_ge(crossed, 4)
                v.tensor_copy(ini[:, 1, :], small[0:CP, 3 * P:3 * P + H])
                v.drain()
                for h in range(H):
                    v.tensor_tensor_scan(F[:, h, ::-1], mr[:, ::-1], A[:, H + h, ::-1], ini[:, 1, h:h + 1], ALU.min, ALU.max)
                v.drain()
                for h in range(H):
                    v.tensor_tensor(F[:, h, :], A[:, h, :], F[:, h, :], ALU.subtract).then_inc(ready, 1)


def layer1_items(K):
    nc = K.nc
    HI = ITEMS // 2
    with Phase(K, "l1i") as ph:
        wst = ph.sb("wst", [P, 2])
        wsi = ph.sb("wsi", [P, 2], I32)
        widx = ph.sb("widx", [P, 2])
        kio = ph.sb("kio", [P, ITEMS])
        cmp = ph.sb("cmp", [P, 2, ITEMS])
        ones = ph.sb("ones", [P, P])
        wa = ph.sb("wa", [P, ITEMS])
        ta = ph.sb("ta", [P, ITEMS])
        first = ph.sb("first", [1, BODIES])
        slot = ph.sb("slot", [1, ITEMS])
        place = ph.sb("place", [1, 2, ITEMS])
        first_w = ph.sb("first_w", [1, BODIES])
        tile_no = ph.sb("tile_no", [P, 4])
        count = [ph.ps(f"count{i}") for i in range(2)]
        bank = [ph.ps(f"bank{i}") for i in range(2)]
        far, loaded, compared, counted, selected, spread = ph.sems(
            "far", "loaded", "compared", "counted", "selected", "spread")
        with Step(nc, True) as block:
            @block.sync
            def _(sp):
                st = K.by_dst.startd.rearrange("(w s) -> w s", s=WIN)
                sp.wait_ge(far, 1)
                with nc.allow_non_contiguous_dma(reason="one value per window"):
                    sp.dma_start(wst[:, 0:1], st[1:1 + P, 0:1]).then_inc(loaded, 16)
                    sp.dma_start(wst[0:NWIN - 1 - P, 1:2], st[1 + P:NWIN, 0:1]).then_inc(loaded, 16)

            @block.vector
            def _(dve):
                v = nc.vector
                v.memset(ones[:, :], 1.0)
                v.memset(wst[:, :], float(4 * ITEMS * P))
                v.drain().then_inc(far, 1)
                v.tensor_copy(kio[:, :], K.iot[:, 0:ITEMS])
                for i in range(2):
                    v.tensor_scalar(widx[:, i:i + 1], K.pcol[:, :], 1.0 + i * P, None, ALU.add)
                for g in range(4):
                    v.tensor_scalar(tile_no[:, g:g + 1], K.pcol[:, :], 4.0, float(g), ALU.mult, ALU.add)
                dve.wait_ge(loaded, 32)
                v.tensor_copy(wsi[:, :], wst[:, :])
                v.drain()
                v.tensor_scalar(wsi[:, :], wsi[:, :], 7, None, ALU.logical_shift_right)
                v.drain()
                v.tensor_copy(wst[:, :], wsi[:, :])
                v.drain()
                v.tensor_scalar(wst[:, 0:1], wst[:, 0:1], float(J - 1), None, ALU.min)
                v.tensor_scalar(wst[0:NWIN - 1 - P, 1:2], wst[0:NWIN - 1 - P, 1:2], float(J - 1), None, ALU.min)
                v.drain()
                v.tensor_tensor(wst[:, :], wst[:, :], widx[:, :], ALU.add)
                v.drain()
                for i in range(2):
                    v.tensor_scalar(cmp[:, i, :], kio[:, :], wst[:, i:i + 1], None, ALU.is_ge)
                v.drain().then_inc(compared, 1)
                dve.wait_ge(counted, 1)
                for i in range(2):
                    v.tensor_copy(wa[:, i * HI:(i + 1) * HI], count[i][:, 0:HI])
                v.drain()
                v.tensor_tensor(ta[:, :], kio[:, :], wa[:, :], ALU.subtract)
                v.drain()
                v.memset(wa[:, J + NWIN - 1:], float(NWIN))
                v.memset(ta[:, J + NWIN - 1:], float(J - 1))
                v.drain()
                for g in range(4):
                    v.tensor_scalar(K.sel[:, g, :], ta[:, :], tile_no[:, g:g + 1], None, ALU.is_equal)
                v.drain().then_inc(selected, 1)
                v.tensor_scalar(first[:, :], ta[0:1, ::IB], float(J - IB), None, ALU.min)
                v.tensor_scalar(first_w[:, :], wa[0:1, ::IB], float(ACC_W - IB), None, ALU.min)
                v.drain()
                v.tensor_tensor(place[:, 0, :].rearrange("p (b i) -> p b i", i=IB), wa[0:1, :].rearrange("p (b i) -> p b i", i=IB),
                                first_w[:, :].unsqueeze(2).to_broadcast([1, BODIES, IB]), ALU.subtract)
                v.tensor_copy(K.body_w[:, :], first_w[:, :])
                v.drain()
                v.tensor_scalar(place[:, 1, :], place[:, 0, :], 7.0, float(512 - 7 * (D + 1)), ALU.is_ge, ALU.mult)
                v.tensor_scalar(place[:, 0, :], place[:, 0, :], float(D + 1), None, ALU.mult)
                v.drain()
                v.tensor_tensor(place[:, 0, :], place[:, 0, :], place[:, 1, :], ALU.add)
                v.drain()
                v.tensor_copy(K.item_out[:, :], place[:, 0, :])
                v.tensor_tensor(slot[:, :].rearrange("p (b i) -> p b i", i=IB), ta[0:1, :].rearrange("p (b i) -> p b i", i=IB),
                                first[:, :].unsqueeze(2).to_broadcast([1, BODIES, IB]), ALU.subtract)
                v.tensor_copy(K.item_first[:, :], first[:, :])
                v.drain()
                v.tensor_copy(K.item_slot[:, :], slot[:, :])
                for i in range(2):
                    dve.wait_ge(spread, i + 1)
                    hs = slice(i * HI, (i + 1) * HI)
                    v.scalar_tensor_tensor(K.item_rel[:, hs], wa[:, hs], -float(WIN), bank[i][:, 0:HI], ALU.mult, ALU.add)

            @block.tensor
            def _(pe):
                pe.wait_ge(compared, 1)
                for i in range(2):
                    for c in range(2):
                        lt = nc.tensor.matmul(count[i][:, 0:HI], ones[:, :], cmp[:, c, i * HI:(i + 1) * HI], start=(c == 0), stop=(c == 1))
                lt.then_inc(counted, 1)
                pe.wait_ge(selected, 1)
                for i in range(2):
                    for g in range(4):
                        lt = nc.tensor.matmul(bank[i][:, 0:HI], K.nodec[:, g * P:(g + 1) * P], K.sel[0:CP, g, i * HI:(i + 1) * HI],
                                              start=(g == 0), stop=(g == 3))
                    lt.then_inc(spread, 1)


def layer1_spread(K):
    nc = K.nc
    HI = ITEMS // 2
    with Phase(K, "l1x") as ph:
        bank = [ph.ps(f"bank{i}") for i in range(4)]
        spread, kept = ph.sems("spread", "kept")
        with Step(nc, True) as block:
            @block.vector
            def _(dve):
                for i in range(4):
                    nc.vector.memset(K.acc[:, i * ACC_W // 4:(i + 1) * ACC_W // 4, :], 0.0)

            @block.tensor
            def _(pe):
                for n in range(2 * H):
                    if n >= 4:
                        pe.wait_ge(kept, n - 3)
                    h, i = n // 2, n % 2
                    for g in range(4):
                        lt = nc.tensor.matmul(bank[n % 4][:, 0:HI], K.F[:, h, g * P:(g + 1) * P],
                                              K.sel[0:CP, g, i * HI:(i + 1) * HI], start=(g == 0), stop=(g == 3))
                    lt.then_inc(spread, 1)

            @block.scalar
            def _(act):
                for n in range(2 * H):
                    h, i = n // 2, n % 2
                    act.wait_ge(spread, n + 1)
                    nc.scalar.copy(K.item_ex[:, h, i * HI:(i + 1) * HI], bank[n % 4][:, 0:HI]).then_inc(kept, 1)


def layer1_sums(K):
    nc = K.nc
    with Phase(K, "l1a") as ph:
        g = ph.sb("g", [P, 2, IB, D + 1])
        place = ph.sb("place", [P, 2, IB, WIN])
        wt = ph.sb("wt", [P, 2, IB, H, WIN])
        zero = ph.sb("zero", [1, 512], BF16)
        pa = [ph.ps(f"pa{b}", (P, 1024)) for b in range(2)]
        fetched = [ph.sem(f"fetched{b}") for b in range(2)]
        weighed, multiplied, added, zeroed = ph.sems("weighed", "multiplied", "added", "zeroed")
        SPAN = 7 * (D + 1)
        with Step(nc, True) as block:
            @block.sync
            def _(sp):
                def body(it, first):
                    for b in range(2):
                        n = it * 2 + b
                        t, = values(nc, K.item_first[0:1, bass.ds(n, 1)], mybir.EngineType.SP, J - IB)
                        if not first:
                            sp.wait_ge(multiplied, n - 1)
                        sp.dma_start(g[:, b], K.g1[:, bass.ds(t, IB), :]).then_inc(fetched[b], 16)
                rounds(sp, body, BODIES // 2)

            @block.tensor
            def _(pe):
                pe.wait_ge(zeroed, 1)

                def body(it, first):
                    for b in range(2):
                        n = it * 2 + b
                        slots = values(nc, K.item_slot[0:1, bass.ds(n * IB, IB)], mybir.EngineType.PE, IB - 1)
                        places = values(nc, K.item_out[0:1, bass.ds(n * IB, IB)], mybir.EngineType.PE, 512 + 6 * (D + 1))
                        pe.wait_ge(weighed, n + 1)
                        pe.wait_ge(fetched[b], (it + 1) * 16)
                        if not first:
                            pe.wait_ge(added, n - 1)
                        for i in range(2):
                            nc.tensor.matmul(pa[b][:, i * 512:i * 512 + SPAN], zero[:, 0:P], zero[:, 0:SPAN], start=True, stop=False)
                        for u in range(IB):
                            nc.tensor.matmul(pa[b][:, bass.ds(places[u], D + 1)], wt[:, b, u].rearrange("p h s -> p (h s)"),
                                                  g[:, b, bass.ds(slots[u], 1), :].rearrange("p o d -> p (o d)"), start=False, stop=False)
                        for i in range(2):
                            lt = nc.tensor.matmul(pa[b][:, i * 512:i * 512 + 1], zero[:, 0:P], zero[:, 0:1], start=False, stop=True)
                        lt.then_inc(multiplied, 1)
                rounds(pe, body, BODIES // 2)

            @block.vector
            def _(dve):
                v = nc.vector

                def weigh(n, b):
                    v.tensor_tensor(place[:, b], K.iot[:, 0:WIN].unsqueeze(1).to_broadcast([P, IB, WIN]),
                                    K.item_rel[:, bass.ds(n * IB, IB)].unsqueeze(2).to_broadcast([P, IB, WIN]), ALU.is_equal)
                    v.drain()
                    v.tensor_tensor(wt[:, b], place[:, b].unsqueeze(2).to_broadcast([P, IB, H, WIN]),
                                    K.item_ex[:, :, bass.ds(n * IB, IB)].rearrange("p h i -> p i h").unsqueeze(3).to_broadcast([P, IB, H, WIN]),
                                    ALU.mult).then_inc(weighed, 1)

                def add(n, b):
                    w, = values(nc, K.body_w[0:1, bass.ds(n, 1)], mybir.EngineType.DVE, ACC_W - IB)
                    dve.wait_ge(multiplied, n + 1)
                    for i in range(2):
                        sums = K.acc[:, bass.ds(w + 7 * i, 7), :].rearrange("p w d -> p (w d)")
                        last = v.tensor_tensor(sums, sums, pa[b][:, i * 512:i * 512 + SPAN], ALU.add)
                    last.then_inc(added, 1)
                    v.drain()

                v.memset(zero[:, :], 0.0)
                v.drain().then_inc(zeroed, 1)
                weigh(0, 0)
                weigh(1, 1)
                with dve.Fori(1, BODIES // 2) as it:
                    for b in range(2):
                        add(it * 2 + b - 2, b)
                        weigh(it * 2 + b, b)
                for b in range(2):
                    add(BODIES - 2 + b, b)


def values(nc, ap, engine, most):
    return nc.values_load_multi_w_load_instructions(ap, engines=[engine], min_val=0, max_val=most,
                                                    skip_runtime_bounds_check_because="the table is clamped where it is made")[1]


def layer1_finish(K):
    nc = K.nc
    with Phase(K, "l1f") as ph:
        rec = ph.sb("rec", [P, ACC_W])
        bias = ph.sb("bias", [P, D])
        W = ph.sb("W", [D, H * D])
        nrm = ph.sb("nrm", [P, 2, H, D])
        at = ph.sb("at", [D, 2, H, 8, WIN])
        pt = [[ph.ps(f"pt{i}{j}") for j in range(2)] for i in range(2)]
        po = [ph.ps(f"po{i}") for i in range(2)]
        loaded, scaled, turned, moved, times, added = ph.sems("loaded", "scaled", "turned", "moved", "times", "added")
        with Step(nc, True) as block:
            @block.sync
            def _(sp):
                sp.dma_start(bias[:, :], K.a["L1_gnn_bias"].unsqueeze(0).to_broadcast([P, D])).then_inc(loaded, 16)
                sp.dma_start(W[:, :], K.a["L1_gnn_W"]).then_inc(loaded, 16)
                sp.wait_ge(loaded, 32)

            @block.vector
            def _(dve):
                v = nc.vector
                dve.wait_ge(loaded, 32)
                v.tensor_scalar(rec[:, :], K.acc[:, :, D], 1e-30, None, ALU.max)
                v.tensor_tensor(K.x[:, :, :], K.x[:, :, :], bias[:, :].unsqueeze(1).to_broadcast([P, NT, D]), ALU.add)
                v.drain()
                v.reciprocal(rec[:, :], rec[:, :])
                v.drain()
                for w in range(NT + 1):
                    if w < NT:
                        if w >= 2:
                            dve.wait_ge(turned, w - 1)
                        v.tensor_tensor(nrm[:, w % 2], K.acc[:, 8 * w:8 * w + 8, 0:D],
                                        rec[:, 8 * w:8 * w + 8].unsqueeze(2).to_broadcast([P, 8, D]), ALU.mult).then_inc(scaled, 1)
                    if w >= 1:
                        u = w - 1
                        dve.wait_ge(times, u + 1)
                        v.scalar_tensor_tensor(K.x[:, u, :], po[u % 2][:, 0:D], 1.0 / H, K.x[:, u, :], ALU.mult, ALU.add).then_inc(added, 1)

            @block.tensor
            def _(pe):
                pe.wait_ge(loaded, 32)
                for w in range(NT + 1):
                    if w < NT:
                        pe.wait_ge(scaled, w + 1)
                        if w >= 2:
                            pe.wait_ge(moved, 2 * (w - 1))
                        for m in range(8):
                            lt = nc.tensor.transpose(pt[w % 2][m // 4][0:D, m % 4 * P:(m % 4 + 1) * P], nrm[:, w % 2, m, :], K.ident[:, :])
                        lt.then_inc(turned, 1)
                    if w >= 1:
                        u = w - 1
                        pe.wait_ge(moved, 2 * (u + 1))
                        if u >= 2:
                            pe.wait_ge(added, u - 1)
                        for h in range(H):
                            lt = nc.tensor.matmul(po[u % 2][:, 0:D],
                                                  at[:, u % 2, h].rearrange("c m s -> c (m s)"),
                                                  W[:, h * D:(h + 1) * D], start=(h == 0), stop=(h == H - 1))
                        lt.then_inc(times, 1)

            @block.scalar
            def _(act):
                for w in range(NT):
                    act.wait_ge(turned, w + 1)
                    if w >= 2:
                        act.wait_ge(times, w - 1)
                    for i in range(2):
                        nc.scalar.copy(at[:, w % 2, :, 4 * i:4 * i + 4, :],
                                       pt[w % 2][i][0:D, :].rearrange("c (m h s) -> c h m s", m=4, h=H)).then_inc(moved, 1)


def layer2_tables(K):
    nc = K.nc
    normalise(K, "n2", True)
    with Phase(K, "t2") as ph:
        W = ph.sb("W", [D, R2])
        tab = ph.sb("tab", [P, NT, R2])
        b1 = ph.sb("b1", [P, R2])
        loaded = ph.sem("loaded")
        with Step(nc, True) as block:
            @block.sync
            def _(sp):
                sp.dma_start(W[:, :].rearrange("k (i d) -> k i d", i=2),
                             K.a["L2_gnn_W1_msg"][D:3 * D, :].rearrange("(i k) d -> k i d", i=2)).then_inc(loaded, 16)
                sp.dma_start(b1[:, 0:D], K.a["L2_gnn_b1_msg"].unsqueeze(0).to_broadcast([P, D])).then_inc(loaded, 16)
                sp.wait_ge(loaded, 32)

            @block.vector
            def _(dve):
                nc.vector.memset(b1[:, D:], 0.0)
        node_dense(K, "t2m", K.hn, D, None, R2, None, None, None,
                   lambda v, w, ps: v.tensor_tensor(tab[:, w, :], ps, b1[:, :].unsqueeze(1).to_broadcast([P, ps.shape[1], R2]), ALU.add), w1d=W, pool_ahead=True)
        store_table(K, K.tab2, tab)


def layer3_weights(K, scratch):
    nc = K.nc
    with Phase(K, "w3") as ph:
        dstf, y, z = (scratch[:, i, :] for i in range(3))
        co = K.co_parts
        loaded, d1, d2, a1, a2 = ph.sems("loaded", "d1", "d2", "a1", "a2")
        with Step(nc, meet=False) as block:
            @block.sync
            def _(sp):
                row = lambda n, k: K.a[n].unsqueeze(0).to_broadcast([P, k])
                sp.dma_start(co[:, 0:3], row("L3_gnn_coeff_param", 3)).then_inc(loaded, 16)
                sp.dma_start(co[:, 4:6], row("L3_gnn_deg_coeff", 2)).then_inc(loaded, 16)
                sp.dma_start(co[:, 6:7], row("L3_gnn_scale_param", 1)).then_inc(loaded, 16)
                sp.wait_ge(loaded, 48)

            @block.vector
            def _(dve):
                v = nc.vector
                dve.wait_ge(loaded, 48)
                meta = K.meta[:, :, :].bitcast(F32)
                v.tensor_copy(dstf, K.by_src.other[:, :])
                v.tensor_scalar(y, meta[:, :, 1], co[:, 4:5], co[:, 5:6], ALU.mult, ALU.add)
                v.tensor_copy(co[:, 7:8], co[:, 6:7])
                v.tensor_reduce(co[:, 3:4], co[:, 0:3], AX.X, ALU.max)
                v.drain()
                v.tensor_scalar(z, y, -1.0, None, ALU.mult)
                v.tensor_scalar(K.co[:, 4:5], co[:, 7:8], -1.0, None, ALU.mult)
                v.tensor_scalar(co[:, 0:3], co[:, 0:3], co[:, 3:4], None, ALU.subtract)
                v.drain()
                v.tensor_tensor(z, z, y, ALU.min)
                v.tensor_tensor(K.co[:, 4:5], K.co[:, 4:5], co[:, 7:8], ALU.min)
                v.drain().then_inc(d1, 1)
                dve.wait_ge(a1, 3)
                v.tensor_scalar(z, z, 1.0, None, ALU.add)
                v.tensor_scalar(K.co[:, 4:5], K.co[:, 4:5], 1.0, None, ALU.add)
                v.tensor_reduce(co[:, 3:4], co[:, 0:3], AX.X, ALU.add)
                v.drain().then_inc(d2, 1)
                v.reciprocal(co[:, 3:4], co[:, 3:4])
                v.tensor_scalar(y, y, 0.0, None, ALU.max)
                v.tensor_scalar(co[:, 7:8], co[:, 7:8], 0.0, None, ALU.max)
                v.tensor_tensor(dstf, dstf, K.nodes[:, :], ALU.not_equal)
                v.drain()
                v.tensor_scalar(K.co[:, 0:3], co[:, 0:3], co[:, 3:4], None, ALU.mult)
                v.tensor_tensor(dstf, dstf, meta[:, :, 0], ALU.mult)
                dve.wait_ge(a2, 2)
                v.tensor_tensor(y, y, z, ALU.add)
                v.tensor_tensor(K.co[:, 3:4], co[:, 7:8], K.co[:, 4:5], ALU.add)
                v.drain()
                v.tensor_tensor(K.base[:, :], dstf, y, ALU.mult)

            @block.scalar
            def _(act):
                act.wait_ge(d1, 1)
                nc.scalar.activation(z, z, ACT.Exp).then_inc(a1, 1)
                nc.scalar.activation(K.co[:, 4:5], K.co[:, 4:5], ACT.Exp).then_inc(a1, 1)
                nc.scalar.activation(co[:, 0:3], co[:, 0:3], ACT.Exp).then_inc(a1, 1)
                act.wait_ge(d2, 1)
                nc.scalar.activation(z, z, ACT.Ln).then_inc(a2, 1)
                nc.scalar.activation(K.co[:, 4:5], K.co[:, 4:5], ACT.Ln).then_inc(a2, 1)


def layer2_gather(K):
    nc = K.nc
    GRP = 4
    G = TB // GRP
    with Phase(K, "l2g") as ph:
        scratch = ph.sb("scratch", [P, 3, J])
        layer3_weights(K, scratch)
        ring = Ring(ph, R2)
        u = ph.sb("u", [P, RING, TB, RE], I32)
        wm = ph.sb("wm", [D, D])
        at = ph.sb("at", [D, 2, GRP * P])
        proj = ph.sb("proj", [P, RING, TB, D])
        pt = [ph.ps(f"pt{i}") for i in range(2)]
        pu = [ph.ps(f"pu{i}") for i in range(2)]
        loaded, turned, moved, times, projected = ph.sems("loaded", "turned", "moved", "times", "projected")
        sums = ph.sb("sums", [P, RING, TB, D])
        first = ph.sb("first", [P, R2])
        q = ph.sb("q", [P, D])
        kb = ph.sb("kb", [P, TB])
        mk = ph.sb("mk", [P, TB])
        got = ph.sem("got")
        fetched, mixed, acted, scanned, freed, stored = (
            [ph.sem(f"{n}{s}") for s in range(RING)] for n in ("fetched", "mixed", "acted", "scanned", "freed", "stored"))
        turned_all = [ph.sem(f"turned_all{s}") for s in range(RING)]
        out = K.sums2.rearrange("(p j) d -> p j d", p=P)
        with Step(nc) as block:
            @block.gpsimd
            def _(pool):
                nc.gpsimd.indirect_dma_start(out=first[:, :], out_offset=None, in_=K.tab2,
                                             in_offset=bass.IndirectOffsetOnAxis(ap=K.by_dst.node0[:, 0:1], axis=0)).then_inc(got, 16)
                gather_rounds(nc, pool, ring, K.tab2, None, [(freed, 1)], taken=(fetched, u))

            @block.sync
            def _(sp):
                sp.dma_start(wm[:, :], K.a["L2_gnn_W1_msg"][0:D, :]).then_inc(loaded, 16)

                def body(it, isfirst):
                    for s in range(RING):
                        if not isfirst:
                            sp.wait_ge(turned_all[s], it)
                            sp.wait_ge(ring.gathered[s], it * TB * 16)
                        sp.dma_start(u[:, s], K.rowsd[:, block_cols(it, s), :]).then_inc(fetched[s], 16)
                        if not isfirst:
                            sp.wait_ge(scanned[s], it)
                            sp.dma_start(out[:, block_cols(it - 1, s), :], sums[:, s]).then_inc(stored[s], 16)
                rounds(sp, body)
                for s in range(RING):
                    sp.wait_ge(scanned[s], NBLK // RING)
                    sp.dma_start(out[:, block_cols(NBLK // RING - 1, s), :], sums[:, s]).then_inc(stored[s], 16)
                for s in range(RING):
                    sp.wait_ge(stored[s], NBLK // RING * 16)

            @block.tensor
            def _(pe):
                pe.wait_ge(loaded, 16)

                def body(it, first):
                    for s in range(RING):
                        pe.wait_ge(fetched[s], (it + 1) * 16)
                        r = u[:, s].bitcast(F32)
                        base = (it * RING + s) * G
                        for g in range(G + 1):
                            if g < G:
                                if not first or s or g >= 2:
                                    pe.wait_ge(moved, base + max(g - 1, 0))
                                for k in range(GRP):
                                    last = nc.tensor.transpose(pt[g % 2][0:RE, k * P:(k + 1) * P], r[:, GRP * g + k, :], K.ident[:, :])
                                last.then_inc(turned_all[s] if g == G - 1 else turned, 1)
                            if g >= 1:
                                n = g - 1
                                pe.wait_ge(moved, base + n + 1)
                                if not first or s or n >= 2:
                                    pe.wait_ge(projected, base + max(n - 1, 0))
                                for k in range(GRP):
                                    last = nc.tensor.matmul(pu[n % 2][:, k * D:(k + 1) * D],
                                                            at[:, n % 2, k * P:(k + 1) * P], wm[:, :], start=True, stop=True)
                                last.then_inc(times, 1)
                rounds(pe, body)

            @block.scalar
            def _(act):
                def body(it, isfirst):
                    for s in range(RING):
                        base = (it * RING + s) * G
                        for g in range(G + 1):
                            if g < G:
                                if g < G - 1:
                                    act.wait_ge(turned, (it * RING + s) * (G - 1) + g + 1)
                                else:
                                    act.wait_ge(turned_all[s], it + 1)
                                if not isfirst or s or g >= 2:
                                    act.wait_ge(times, base + max(g - 1, 0))
                                nc.scalar.copy(at[:, g % 2, :], pt[g % 2][0:D, :]).then_inc(moved, 1)
                            if g == 1 and not isfirst:
                                act.wait_ge(mixed[s], it)
                            if g >= 1:
                                n = g - 1
                                act.wait_ge(times, base + g)
                                nc.scalar.copy(proj[:, s, GRP * n:GRP * g, :],
                                               pu[n % 2][:, 0:GRP * D].rearrange("p (t d) -> p t d", d=D)).then_inc(projected, 1)
                        act.wait_ge(mixed[s], it + 1)
                        nc.scalar.activation(sums[:, s], sums[:, s], ACT.Silu).then_inc(acted[s], 1)
                rounds(act, body)

            @block.vector
            def _(dve):
                v = nc.vector
                v.memset(K.st[:, :], 0.0)
                dve.wait_ge(got, 16)
                v.tensor_copy(q[:, :], first[:, D:])

                def body(it, isfirst):
                    for s in range(RING):
                        r = ring.rows
                        seg_masks(v, K.by_dst.keep, block_cols(it, s), kb, mk=mk)
                        dve.wait_ge(ring.gathered[s], (it + 1) * TB * 16)
                        v.tensor_tensor(r[:, s, :, D:], r[:, s, :, D:], mk[:, :].unsqueeze(2).to_broadcast([P, TB, D]), ALU.mult)
                        dve.wait_ge(projected, (it * RING + s + 1) * G)
                        v.tensor_tensor(r[:, s, :, 0:D], r[:, s, :, 0:D], proj[:, s], ALU.add)
                        v.drain()
                        for f in range(D):
                            v.tensor_tensor_scan(r[:, s, :, D + f], kb[:, :], r[:, s, :, D + f], q[:, f:f + 1], ALU.mult, ALU.add)
                        v.drain()
                        if not isfirst:
                            dve.wait_ge(stored[s], it * 16)
                        v.tensor_tensor(sums[:, s], r[:, s, :, 0:D], r[:, s, :, D:], ALU.add)
                        v.tensor_copy(q[:, :], r[:, s, TB - 1, D:])
                        v.drain().then_inc(mixed[s], 1)
                        dve.wait_ge(acted[s], it + 1)
                        v.tensor_tensor(sums[:, s], sums[:, s], kb[:, :].unsqueeze(2).to_broadcast([P, TB, D]), ALU.mult).then_inc(freed[s], 1)
                        v.drain()
                        for f in range(D):
                            v.tensor_tensor_scan(sums[:, s, :, f], kb[:, :], sums[:, s, :, f], K.st[:, f:f + 1], ALU.mult, ALU.add)
                        v.drain().then_inc(scanned[s], 1)
                        v.tensor_copy(K.st[:, :], sums[:, s, TB - 1, :])
                rounds(dve, body)


def layer2_finish(K):
    nc = K.nc
    with Phase(K, "l2f") as ph:
        res = ph.sb("res", [P, NT, D])
        feat = ph.sb("feat", [P, NT, 2 * D])
        b2m = ph.sb("b2m", [P, D])
        b2u = ph.sb("b2u", [P, D])
        W2m = ph.sb("W2m", [D, D])
        r = ph.sb("r", [P, 2, NT])
        loaded = ph.sem("loaded")
        collect(K, K.by_dst, K.sums2, D, res)
        with Step(nc) as block:
            @block.sync
            def _(sp):
                for t, n in ((b2m, "L2_gnn_b2_msg"), (b2u, "L2_gnn_b2_upd")):
                    sp.dma_start(t[:, :], K.a[n].unsqueeze(0).to_broadcast([P, D])).then_inc(loaded, 16)
                sp.dma_start(W2m[:, :], K.a["L2_gnn_W2_msg"]).then_inc(loaded, 16)
                sp.wait_ge(loaded, 48)

            @block.vector
            def _(dve):
                v = nc.vector
                wide = lambda t, n: t.unsqueeze(2).to_broadcast([P, NT, n])
                row = lambda t: t[:, :].unsqueeze(1).to_broadcast([P, NT, D])
                dve.wait_ge(loaded, 48)
                v.tensor_scalar(r[:, 0], K.by_dst.cnt[:, :], 1e-6, None, ALU.add)
                v.tensor_scalar(r[:, 1], K.by_dst.cnt[:, :], 0.0, None, ALU.is_gt)
                v.tensor_tensor(K.x[:, :, :], K.x[:, :, :], row(b2u), ALU.add)
                v.tensor_copy(feat[:, :, 0:D], K.hn[:, :, :])
                v.drain()
                v.reciprocal(r[:, 0], r[:, 0])
                v.drain()
                v.tensor_tensor(r[:, 1], r[:, 1], r[:, 0], ALU.mult)
                v.tensor_tensor(r[:, 0], K.by_dst.cnt[:, :], r[:, 0], ALU.mult)
                v.drain()
                v.tensor_tensor(res[:, :, :], res[:, :, :], wide(r[:, 1], D), ALU.mult)
                v.tensor_tensor(feat[:, :, D:], row(b2m), wide(r[:, 0], D), ALU.mult)
        node_dense(K, "l2a", res, D, None, D, None, None, None,
                   lambda v, w, ps: v.tensor_tensor(feat[:, w, D:], feat[:, w, D:], ps, ALU.add), w1d=W2m)
        node_dense(K, "l2m", feat, 2 * D, K.a["L2_gnn_W1_upd"], D, ACT.Silu, K.a["L2_gnn_b1_upd"], K.a["L2_gnn_W2_upd"],
                   lambda v, w, ps: v.tensor_tensor(K.x[:, w, :], K.x[:, w, :], ps, ALU.add))


def layer3_gather(K):
    nc = K.nc
    normalise(K, "n3")
    C1 = D + 1
    with Phase(K, "t3") as ph:
        b = ph.sb("b", [P, D])
        W = ph.sb("W", [D, D])
        sq = ph.sb("sq", [P, NT, D])
        loaded, d1, a3 = ph.sems("loaded", "d1", "a3")
        with Step(nc) as block:
            @block.sync
            def _(sp):
                sp.dma_start(b[:, :], K.a["L3_gnn_b"].unsqueeze(0).to_broadcast([P, D])).then_inc(loaded, 16)
                sp.dma_start(W[:, :], K.a["L3_gnn_W"]).then_inc(loaded, 16)
                sp.wait_ge(loaded, 32)

        wh = K.wh
        node_dense(K, "t3m", K.hn, D, None, D, None, None, None,
                   lambda v, w, ps: v.tensor_tensor(wh[:, w, 0:D], ps, b[:, :].unsqueeze(1).to_broadcast([P, ps.shape[1], D]), ALU.add), w1d=W)
        with Step(nc) as block:
            @block.vector
            def _(dve):
                v = nc.vector
                v.tensor_tensor(sq[:, :, :], wh[:, :, 0:D], wh[:, :, 0:D], ALU.mult)
                v.memset(wh[:, :, C1:], 0.0)
                v.drain()
                v.tensor_reduce(wh[:, :, D], sq[:, :, :], AX.X, ALU.add)
                v.drain().then_inc(d1, 1)

            @block.scalar
            def _(act):
                act.wait_ge(d1, 1)
                nc.scalar.sqrt(wh[:, :, D], wh[:, :, D]).then_inc(a3, 1)
                act.wait_ge(a3, 1)
        store_table(K, K.tab3, wh)
    with Phase(K, "l3g") as ph:
        ring = Ring(ph, R3)
        own = ph.sb("own", [P, TB, C1])
        prod = ph.sb("prod", [P, TB, D])
        sums = ph.sb("sums", [P, RING, TB, D])
        first = ph.sb("first", [P, R3])
        q = ph.sb("q", [P, C1])
        kb = ph.sb("kb", [P, TB])
        mk = ph.sb("mk", [P, TB])
        dot = ph.sb("dot", [P, TB])
        nn = ph.sb("nn", [P, TB])
        neg = ph.sb("neg", [P, TB])
        bb = ph.sb("bb", [P, TB])
        got = ph.sem("got")
        scanned, freed, stored = ([ph.sem(f"{n}{s}") for s in range(RING)] for n in ("scanned", "freed", "stored"))
        out = K.sums3.rearrange("(p j) d -> p j d", p=P)
        with Step(nc) as block:
            @block.gpsimd
            def _(pool):
                nc.gpsimd.indirect_dma_start(out=first[:, :], out_offset=None, in_=K.tab3,
                                             in_offset=bass.IndirectOffsetOnAxis(ap=K.by_src.node0[:, 0:1], axis=0)).then_inc(got, 16)
                gather_rounds(nc, pool, ring, K.tab3, K.by_src.other, [(freed, 1)])

            @block.sync
            def _(sp):
                def body(it, isfirst):
                    for s in range(RING):
                        if not isfirst:
                            sp.wait_ge(scanned[s], it)
                            sp.dma_start(out[:, block_cols(it - 1, s), :], sums[:, s]).then_inc(stored[s], 16)
                rounds(sp, body)
                for s in range(RING):
                    sp.wait_ge(scanned[s], NBLK // RING)
                    sp.dma_start(out[:, block_cols(NBLK // RING - 1, s), :], sums[:, s]).then_inc(stored[s], 16)
                for s in range(RING):
                    sp.wait_ge(stored[s], NBLK // RING * 16)

            @block.vector
            def _(dve):
                v = nc.vector
                v.memset(K.st[:, :], 0.0)
                dve.wait_ge(got, 16)
                v.tensor_copy(q[:, :], first[:, 0:C1])

                def body(it, isfirst):
                    for s in range(RING):
                        r = ring.rows
                        seg_masks(v, K.by_src.keep, block_cols(it, s), kb, mk=mk)
                        dve.wait_ge(ring.gathered[s], (it + 1) * TB * 16)
                        v.tensor_tensor(own[:, :, :], r[:, s, :, 0:C1], mk[:, :].unsqueeze(2).to_broadcast([P, TB, C1]), ALU.mult)
                        v.drain()
                        for f in range(C1):
                            v.tensor_tensor_scan(own[:, :, f], kb[:, :], own[:, :, f], q[:, f:f + 1], ALU.mult, ALU.add)
                        v.drain()
                        v.tensor_copy(q[:, :], own[:, TB - 1, :])
                        v.tensor_tensor(prod[:, :, :], own[:, :, 0:D], r[:, s, :, 0:D], ALU.mult)
                        v.tensor_tensor(nn[:, :], own[:, :, D], r[:, s, :, D], ALU.mult)
                        v.drain()
                        v.tensor_reduce(dot[:, :], prod[:, :, :], AX.X, ALU.add)
                        v.tensor_scalar(nn[:, :], nn[:, :], 1e-8, None, ALU.max)
                        v.drain()
                        v.reciprocal(nn[:, :], nn[:, :])
                        v.drain()
                        v.tensor_tensor(dot[:, :], dot[:, :], nn[:, :], ALU.mult)
                        v.drain()
                        v.tensor_scalar(neg[:, :], dot[:, :], 0.0, K.co[:, 1:2], ALU.min, ALU.mult)
                        v.tensor_scalar(nn[:, :], dot[:, :], 0.0, K.co[:, 0:1], ALU.max, ALU.mult)
                        v.drain()
                        v.tensor_tensor(dot[:, :], nn[:, :], neg[:, :], ALU.add)
                        v.tensor_copy(bb[:, :], K.base[:, block_cols(it, s)])
                        v.drain()
                        v.tensor_tensor(dot[:, :], dot[:, :], bb[:, :], ALU.mult)
                        v.drain()
                        if not isfirst:
                            dve.wait_ge(stored[s], it * 16)
                        v.tensor_tensor(sums[:, s], r[:, s, :, 0:D], dot[:, :].unsqueeze(2).to_broadcast([P, TB, D]), ALU.mult).then_inc(freed[s], 1)
                        v.drain()
                        for f in range(D):
                            v.tensor_tensor_scan(sums[:, s, :, f], kb[:, :], sums[:, s, :, f], K.st[:, f:f + 1], ALU.mult, ALU.add)
                        v.drain().then_inc(scanned[s], 1)
                        v.tensor_copy(K.st[:, :], sums[:, s, TB - 1, :])
                rounds(dve, body)


def layer3_finish(K):
    nc = K.nc
    with Phase(K, "l3f") as ph:
        res = ph.sb("res", [P, NT, D])
        has = ph.sb("has", [P, NT])
        done, stored = ph.sems("done", "stored")
        collect(K, K.by_src, K.sums3, D, res)
        with Step(nc) as block:
            @block.vector
            def _(dve):
                v = nc.vector
                v.tensor_scalar(has[:, :], K.by_src.cnt[:, :], 0.0, None, ALU.is_gt)
                v.tensor_scalar(K.wh[:, :, 0:D], K.wh[:, :, 0:D], K.co[:, 2:3], None, ALU.mult)
                v.drain()
                v.tensor_tensor(res[:, :, :], res[:, :, :], has[:, :].unsqueeze(2).to_broadcast([P, NT, D]), ALU.mult)
                v.drain()
                v.tensor_tensor(res[:, :, :], res[:, :, :], K.wh[:, :, 0:D], ALU.add)
                v.drain()
                v.scalar_tensor_tensor(K.x[:, :, :], res[:, :, :], K.co[:, 3:4], K.x[:, :, :], ALU.mult, ALU.add).then_inc(done, 1)

            @block.sync
            def _(sp):
                sp.wait_ge(done, 1)
                sp.dma_start(K.out[0:(NT - 1) * P, :].rearrange("(w p) d -> p w d", p=P), K.x[:, 0:NT - 1, :]).then_inc(stored, 16)
                sp.dma_start(K.out[(NT - 1) * P:N, :], K.x[0:N - (NT - 1) * P, NT - 1, :]).then_inc(stored, 16)
                sp.wait_ge(stored, 32)


def kernel(**inputs):
    import numpy as np
    import concourse.bacc as _bacc
    from concourse.bass_utils import run_bass_kernel_spmd as _run
    nc = _bacc.Bacc("TRN2", target_bir_lowering=False, num_devices=1)
    i = {k: np.ascontiguousarray(v) for k, v in inputs.items()}
    i32 = np.int32
    ids = np.arange(N, dtype=i32)
    pad = np.full(L - M, N, i32)
    rest = np.full(SORT_L - L, 4095, i32)
    arrays = {k: v for k, v in i.items() if k[0] == "L" or k == "x"}
    arrays["nodess"] = np.concatenate([ids, i["src"], pad, rest])
    arrays["srcs"] = np.concatenate([ids, i["src"], pad, rest])
    arrays["edge_bits"] = np.full(SORT_L, KEY_ONE, i32)
    arrays["edge_bits"][N:M] += 1 << 12
    arrays["nodesd"] = np.concatenate([ids, i["dst"], pad, rest])

    def rows(columns, other, width):
        body = np.concatenate([c.view(i32).reshape(E, -1) for c in columns] + [other.reshape(E, 1)], axis=1)
        r = np.zeros((L, width), i32)
        r[N:M, :body.shape[1]] = body
        r[:N, body.shape[1] - 1] = ids
        r[M:, body.shape[1] - 1] = N
        return r
    arrays["rec_s"] = rows([i["edge_attr_32"], i["edge_weight"], i["edge_weight_n2"]], i["dst"], R0)
    arrays["rec_d"] = rows([i["edge_attr_64"]], i["src"], RE)
    a = {k: nc.dram_tensor("in_" + k, v.shape, mybir.dt.from_np(v.dtype), kind="ExternalInput").ap()
         for k, v in arrays.items()}
    out = nc.dram_tensor("out_0", (N, D), F32, kind="ExternalOutput").ap()
    build(nc, a, out)
    r = _run(nc, [{"in_" + k: v for k, v in arrays.items()}], core_ids=[0])
    return r.results[0]["out_0"]
```
